# Optimizing a Trainium2 kernel written in Bass

```python
import numpy as np
import jax
import jax.numpy as jnp

def _softmax(x, axis=-1):
    return jax.nn.softmax(x, axis=axis)

def _gelu(x):
    return jax.nn.gelu(x, approximate=True)

def _silu(x):
    return jax.nn.silu(x)

def _sigmoid(x):
    return jax.nn.sigmoid(x)

def _layernorm(x, axis=-1, eps=1e-05):
    m = jnp.mean(x, axis=axis, keepdims=True)
    v = jnp.var(x, axis=axis, keepdims=True)
    return (x - m) / jnp.sqrt(v + eps)

def _scatter_add(tgt, idx, src, axis=0):
    return tgt.at[idx].add(src)

def _segment_sum(src, seg, n):
    return jax.ops.segment_sum(src, seg, n)
kernel_name = 'mk_recurrent_d2_jaxref_r8_0f5d6e'

def setup_inputs(seed: int=0):
    np.random.seed(seed)
    _w = jnp.asarray

    def _L0_attn_setup():
        import jax, jax.numpy as jnp
        import numpy as np
        B, N, D, H = (4, 512, 128, 16)
        HD = D // H

        def _kernel(x):
            return jax.nn.elu(x) + 1.0
        key = jax.random.key(seed)
        k1, k2, k3, k4 = jax.random.split(key, 4)
        x = jax.random.normal(k1, (B, N, D), dtype=jnp.float32)
        w_qkv = jax.random.normal(k2, (3 * D, D), dtype=jnp.float32) * (1.0 / np.sqrt(D))
        w_out = jax.random.normal(k3, (D, D), dtype=jnp.float32) * (1.0 / np.sqrt(D))
        b_out = jax.random.normal(k4, (D,), dtype=jnp.float32) * 0.01
        return {'x': x, 'w_qkv': w_qkv, 'w_out': w_out, 'b_out': b_out}
    _L0_attn_in = _L0_attn_setup()

    def _L0_ffn_setup():
        import jax, jax.numpy as jnp
        import numpy as np
        D = 128
        H = 16
        HD = D // H
        L = 64
        E = 8
        B, T = (4, 256)
        EPS = 1e-06

        def _glorot(k, shape):
            fan_in, fan_out = (shape[-2], shape[-1])
            lim = np.sqrt(6.0 / (fan_in + fan_out)).astype(np.float32)
            return jax.random.uniform(k, shape, jnp.float32, -lim, lim)

        def _rmsnorm(x, gamma):
            return gamma * x * jax.lax.rsqrt(jnp.mean(x * x, axis=-1, keepdims=True) + EPS)
        key = jax.random.key(seed)
        ks = jax.random.split(key, 8)
        return {'x': jax.random.normal(ks[0], (B, T, D), jnp.float32), 'gamma1': jnp.ones((D,), jnp.float32), 'Wq': _glorot(ks[1], (D, D)), 'bq': jnp.zeros((D,), jnp.float32), 'Wdown': _glorot(ks[2], (D, L)), 'bdown': jnp.zeros((L,), jnp.float32), 'Wup': _glorot(ks[3], (L, 2 * D)), 'bup': jnp.zeros((2 * D,), jnp.float32), 'Wo': _glorot(ks[4], (D, D)), 'bo': jnp.zeros((D,), jnp.float32), 'gamma2': jnp.ones((D,), jnp.float32), 'Wg': _glorot(ks[5], (D, E)), 'bg': jnp.zeros((E,), jnp.float32), 'We': _glorot(ks[6], (E, D, D))}
    _L0_ffn_in = _L0_ffn_setup()

    def _L1_attn_setup():
        import jax, jax.numpy as jnp
        import numpy as np
        import math
        H = 16
        LORA_SCALING = 16 / 8
        NEG_INF = -1e+30

        def _alibi_slopes(n_heads):
            start = 2.0 ** (-2.0 ** (-(math.log2(n_heads) - 3)))
            return jnp.asarray([start * start ** i for i in range(n_heads)], dtype=jnp.float32)

        def _lora(x, W, A, Bm):
            return x @ W.T + x @ Bm.T @ A.T * LORA_SCALING
        key = jax.random.key(seed)
        ks = jax.random.split(key, 11)
        B, T, E, r = (4, 256, 128, 8)
        d = {'x': jax.random.normal(ks[0], (B, T, E), jnp.float32), 'Wq': jax.random.normal(ks[1], (E, E), jnp.float32) * E ** (-0.5), 'Aq': jax.random.normal(ks[2], (E, r), jnp.float32) * 0.01, 'Bq': jax.random.normal(ks[3], (r, E), jnp.float32) * 0.01, 'Wk': jax.random.normal(ks[4], (E, E), jnp.float32) * E ** (-0.5), 'Ak': jax.random.normal(ks[5], (E, r), jnp.float32) * 0.01, 'Bk': jax.random.normal(ks[6], (r, E), jnp.float32) * 0.01, 'Wv': jax.random.normal(ks[7], (E, E), jnp.float32) * E ** (-0.5), 'Av': jax.random.normal(ks[8], (E, r), jnp.float32) * 0.01, 'Bv': jax.random.normal(ks[9], (r, E), jnp.float32) * 0.01, 'Wp': jax.random.normal(ks[10], (E, E), jnp.float32) * E ** (-0.5)}
        return d
    _L1_attn_in = _L1_attn_setup()

    def _L1_ffn_setup():
        import jax, jax.numpy as jnp
        import numpy as np
        LN_EPS = 1e-05

        def layer_norm(x, g, b):
            mu = jnp.mean(x, axis=-1, keepdims=True)
            var = jnp.mean(jnp.square(x - mu), axis=-1, keepdims=True)
            return (x - mu) * jax.lax.rsqrt(var + LN_EPS) * g + b

        def ternary_quant(w):
            scale = 1.0 / jnp.clip(jnp.mean(jnp.abs(w)), 1e-05)
            wq = jnp.clip(jnp.round(w * scale), -1.0, 1.0) / scale
            return w + jax.lax.stop_gradient(wq - w)
        key = jax.random.key(seed)
        ks = jax.random.split(key, 3)
        dim, hidden = (128, 512)
        B, S = (8, 128)
        x = jax.random.normal(ks[0], (B, S, dim), dtype=jnp.float32)
        w1 = jax.random.normal(ks[1], (hidden, dim), dtype=jnp.float32) * 0.02
        w2 = jax.random.normal(ks[2], (dim, hidden), dtype=jnp.float32) * 0.02
        return {'x': x, 'ln1_g': jnp.ones((dim,), jnp.float32), 'ln1_b': jnp.zeros((dim,), jnp.float32), 'w1': w1, 'b1': jnp.zeros((hidden,), jnp.float32), 'ln2_g': jnp.ones((hidden,), jnp.float32), 'ln2_b': jnp.zeros((hidden,), jnp.float32), 'w2': w2, 'b2': jnp.zeros((dim,), jnp.float32)}
    _L1_ffn_in = _L1_ffn_setup()
    _d = {'L0_attn_x': _L0_attn_in['x'], 'L0_attn_w_qkv': _L0_attn_in['w_qkv'], 'L0_attn_w_out': _L0_attn_in['w_out'], 'L0_attn_b_out': _L0_attn_in['b_out'], 'L0_ffn_gamma1': _L0_ffn_in['gamma1'], 'L0_ffn_Wq': _L0_ffn_in['Wq'], 'L0_ffn_bq': _L0_ffn_in['bq'], 'L0_ffn_Wdown': _L0_ffn_in['Wdown'], 'L0_ffn_bdown': _L0_ffn_in['bdown'], 'L0_ffn_Wup': _L0_ffn_in['Wup'], 'L0_ffn_bup': _L0_ffn_in['bup'], 'L0_ffn_Wo': _L0_ffn_in['Wo'], 'L0_ffn_bo': _L0_ffn_in['bo'], 'L0_ffn_gamma2': _L0_ffn_in['gamma2'], 'L0_ffn_Wg': _L0_ffn_in['Wg'], 'L0_ffn_bg': _L0_ffn_in['bg'], 'L0_ffn_We': _L0_ffn_in['We'], 'L1_attn_Wq': _L1_attn_in['Wq'], 'L1_attn_Aq': _L1_attn_in['Aq'], 'L1_attn_Bq': _L1_attn_in['Bq'], 'L1_attn_Wk': _L1_attn_in['Wk'], 'L1_attn_Ak': _L1_attn_in['Ak'], 'L1_attn_Bk': _L1_attn_in['Bk'], 'L1_attn_Wv': _L1_attn_in['Wv'], 'L1_attn_Av': _L1_attn_in['Av'], 'L1_attn_Bv': _L1_attn_in['Bv'], 'L1_attn_Wp': _L1_attn_in['Wp'], 'L1_ffn_ln1_g': _L1_ffn_in['ln1_g'], 'L1_ffn_ln1_b': _L1_ffn_in['ln1_b'], 'L1_ffn_w1': _L1_ffn_in['w1'], 'L1_ffn_b1': _L1_ffn_in['b1'], 'L1_ffn_ln2_g': _L1_ffn_in['ln2_g'], 'L1_ffn_ln2_b': _L1_ffn_in['ln2_b'], 'L1_ffn_w2': _L1_ffn_in['w2'], 'L1_ffn_b2': _L1_ffn_in['b2']}
    _x0 = _d['L0_attn_x']
    _d['L0_attn_x'] = jax.random.normal(jax.random.fold_in(jax.random.key(seed), 1), (2, 1024, 128), dtype=_x0.dtype)
    del _x0
    return _d

def reference(L0_attn_x, L0_attn_w_qkv, L0_attn_w_out, L0_attn_b_out, L0_ffn_gamma1, L0_ffn_Wq, L0_ffn_bq, L0_ffn_Wdown, L0_ffn_bdown, L0_ffn_Wup, L0_ffn_bup, L0_ffn_Wo, L0_ffn_bo, L0_ffn_gamma2, L0_ffn_Wg, L0_ffn_bg, L0_ffn_We, L1_attn_Wq, L1_attn_Aq, L1_attn_Bq, L1_attn_Wk, L1_attn_Ak, L1_attn_Bk, L1_attn_Wv, L1_attn_Av, L1_attn_Bv, L1_attn_Wp, L1_ffn_ln1_g, L1_ffn_ln1_b, L1_ffn_w1, L1_ffn_b1, L1_ffn_ln2_g, L1_ffn_ln2_b, L1_ffn_w2, L1_ffn_b2):

    def _L0_attn_ref(x, w_qkv, w_out, b_out):
        import jax, jax.numpy as jnp
        import numpy as np
        B, N, D, H = (4, 512, 128, 16)
        HD = D // H

        def _kernel(x):
            return jax.nn.elu(x) + 1.0
        b, n, d = x.shape
        qkv = x @ w_qkv.T
        qkv = qkv.reshape(b, n, 3, H, HD)
        q, k, v = (qkv[:, :, 0], qkv[:, :, 1], qkv[:, :, 2])
        q = _kernel(q)
        k = _kernel(k)
        kv = jnp.einsum('bnhd,bnhm->bhdm', k, v)
        z = 1.0 / (jnp.einsum('bnhd,bhd->bnh', q, k.sum(axis=1)) + 1e-06)
        out = jnp.einsum('bnhd,bhdm,bnh->bnhm', q, kv, z)
        out = out.reshape(b, n, d)
        return out @ w_out.T + b_out

    def _L0_ffn_ref(x, gamma1, Wq, bq, Wdown, bdown, Wup, bup, Wo, bo, gamma2, Wg, bg, We):
        import jax, jax.numpy as jnp
        import numpy as np
        D = 128
        H = 16
        HD = D // H
        L = 64
        E = 8
        B, T = (4, 256)
        EPS = 1e-06

        def _glorot(k, shape):
            fan_in, fan_out = (shape[-2], shape[-1])
            lim = np.sqrt(6.0 / (fan_in + fan_out)).astype(np.float32)
            return jax.random.uniform(k, shape, jnp.float32, -lim, lim)

        def _rmsnorm(x, gamma):
            return gamma * x * jax.lax.rsqrt(jnp.mean(x * x, axis=-1, keepdims=True) + EPS)
        b, t = (x.shape[0], x.shape[1])
        h = _rmsnorm(x, gamma1)
        q = (h @ Wq + bq).reshape(b, t, H, HD)
        kv = ((h @ Wdown + bdown) @ Wup + bup).reshape(b, t, H, 2 * HD)
        k, v = jnp.split(kv, 2, axis=-1)
        att = jnp.einsum('bthd,btgd->bthg', q, k) / np.sqrt(HD).astype(np.float32)
        att = jax.nn.softmax(att, axis=-1)
        out = jnp.einsum('bthg,btgd->bthd', att, v).reshape(b, t, D)
        x = x + (out @ Wo + bo)
        h2 = _rmsnorm(x, gamma2)
        gate = jax.nn.softmax(h2 @ Wg + bg, axis=-1)
        combined = jnp.einsum('btd,edf,bte->btf', h2, We, gate)
        return x + combined

    def _L1_attn_ref(x, Wq, Aq, Bq, Wk, Ak, Bk, Wv, Av, Bv, Wp):
        import jax, jax.numpy as jnp
        import numpy as np
        import math
        H = 16
        LORA_SCALING = 16 / 8
        NEG_INF = -1e+30

        def _alibi_slopes(n_heads):
            start = 2.0 ** (-2.0 ** (-(math.log2(n_heads) - 3)))
            return jnp.asarray([start * start ** i for i in range(n_heads)], dtype=jnp.float32)

        def _lora(x, W, A, Bm):
            return x @ W.T + x @ Bm.T @ A.T * LORA_SCALING
        B, T, E = x.shape
        dh = E // H
        q = _lora(x, Wq, Aq, Bq).reshape(B, T, H, dh).transpose(0, 2, 1, 3)
        k = _lora(x, Wk, Ak, Bk).reshape(B, T, H, dh).transpose(0, 2, 1, 3)
        v = _lora(x, Wv, Av, Bv).reshape(B, T, H, dh).transpose(0, 2, 1, 3)
        s = jnp.einsum('bhqd,bhkd->bhqk', q, k) / jnp.sqrt(jnp.float32(dh))
        i = jnp.arange(T)[:, None]
        j = jnp.arange(T)[None, :]
        slopes = _alibi_slopes(H)
        bias = slopes[:, None, None] * (i - j).astype(jnp.float32)
        s = s + bias[None]
        s = jnp.where(j[None, None] <= i[None, None], s, NEG_INF)
        out = jnp.einsum('bhqk,bhkd->bhqd', jax.nn.softmax(s, axis=-1), v)
        out = out.transpose(0, 2, 1, 3).reshape(B, T, E)
        return out @ Wp.T

    def _L1_ffn_ref(x, ln1_g, ln1_b, w1, b1, ln2_g, ln2_b, w2, b2):
        import jax, jax.numpy as jnp
        import numpy as np
        LN_EPS = 1e-05

        def layer_norm(x, g, b):
            mu = jnp.mean(x, axis=-1, keepdims=True)
            var = jnp.mean(jnp.square(x - mu), axis=-1, keepdims=True)
            return (x - mu) * jax.lax.rsqrt(var + LN_EPS) * g + b

        def ternary_quant(w):
            scale = 1.0 / jnp.clip(jnp.mean(jnp.abs(w)), 1e-05)
            wq = jnp.clip(jnp.round(w * scale), -1.0, 1.0) / scale
            return w + jax.lax.stop_gradient(wq - w)
        h = layer_norm(x, ln1_g, ln1_b)
        h = jnp.einsum('bsd,hd->bsh', h, ternary_quant(w1)) + b1
        h = jax.nn.gelu(h, approximate=False)
        h = layer_norm(h, ln2_g, ln2_b)
        out = jnp.einsum('bsh,dh->bsd', h, ternary_quant(w2)) + b2
        return out
    x = L0_attn_x
    xn = _layernorm(x, axis=-1)
    s = _L0_attn_ref(xn, L0_attn_w_qkv, L0_attn_w_out, L0_attn_b_out)
    g = _silu(_L0_ffn_ref(xn, L0_ffn_gamma1, L0_ffn_Wq, L0_ffn_bq, L0_ffn_Wdown, L0_ffn_bdown, L0_ffn_Wup, L0_ffn_bup, L0_ffn_Wo, L0_ffn_bo, L0_ffn_gamma2, L0_ffn_Wg, L0_ffn_bg, L0_ffn_We))
    x = x + s * g
    xn = _layernorm(x, axis=-1)
    s = _L1_attn_ref(xn, L1_attn_Wq, L1_attn_Aq, L1_attn_Bq, L1_attn_Wk, L1_attn_Ak, L1_attn_Bk, L1_attn_Wv, L1_attn_Av, L1_attn_Bv, L1_attn_Wp)
    g = _silu(_L1_ffn_ref(xn, L1_ffn_ln1_g, L1_ffn_ln1_b, L1_ffn_w1, L1_ffn_b1, L1_ffn_ln2_g, L1_ffn_ln2_b, L1_ffn_w2, L1_ffn_b2))
    x = x + s * g
    return x

_drawn_inputs = setup_inputs


def setup_inputs(seed=0):
    import zlib

    import numpy as np

    out = dict(_drawn_inputs(seed))
    spreads = {'L0_ffn_gamma1': (1.0, 0.6),
     'L0_ffn_bq': (0.0, 0.8),
     'L0_ffn_bdown': (0.0, 0.8),
     'L0_ffn_bup': (0.0, 0.8),
     'L0_ffn_bo': (0.0, 2.0),
     'L0_ffn_gamma2': (1.0, 0.6),
     'L0_ffn_bg': (0.0, 2.0),
     'L1_ffn_ln1_g': (1.0, 0.6),
     'L1_ffn_ln1_b': (0.0, 2.0),
     'L1_ffn_b1': (0.0, 0.8),
     'L1_ffn_ln2_g': (1.0, 0.6),
     'L1_ffn_ln2_b': (0.0, 2.0),
     'L1_ffn_b2': (0.0, 2.0)}
    factors = {'L0_attn_b_out': 7.564,
     'L0_ffn_Wq': 8.0,
     'L0_ffn_Wdown': 6.363,
     'L0_ffn_Wup': 6.369,
     'L0_ffn_Wo': 6.376,
     'L0_ffn_Wg': 16.272,
     'L0_ffn_We': 11.443,
     'L1_attn_Aq': 64.0,
     'L1_attn_Bq': 64.0,
     'L1_attn_Ak': 64.0,
     'L1_attn_Bk': 64.0,
     'L1_attn_Av': 64.0,
     'L1_attn_Bv': 64.0,
     'L1_attn_Wq': 8.0,
     'L1_attn_Wk': 8.0,
     'L1_attn_Wv': 3.235,
     'L1_attn_Wp': 3.628,
     'L1_ffn_w1': 6.573,
     'L1_ffn_w2': 5.144}
    for name, (base, spread) in spreads.items():
        noise = np.random.default_rng([zlib.crc32(name.encode()), seed]).standard_normal(out[name].shape)
        drawn = base * np.exp(spread * noise) if base else spread * noise
        out[name] = jnp.asarray(drawn.astype(out[name].dtype))
    for name, factor in factors.items():
        out[name] = (out[name] * factor).astype(out[name].dtype)
    return out
```

```python
import concourse.bass as bass
from concourse import mybir
from contextlib import ExitStack

F32 = mybir.dt.float32
BF16 = mybir.dt.bfloat16
ALU = mybir.AluOpType
ACT = mybir.ActivationFunctionType
AX = mybir.AxisListType

B, N, D, H = 2, 1024, 128, 16
HD = D // H
P = 128
NT = B * N // P
TB = N // P
L = 64
E = 8
HID = 512
HC = HID // P
R = 8
QUAD = 4
NG = B * H // QUAD
BANK = 512

PARTS = 3
ROW_ALIBI = PARTS * PARTS * HD
ROW_MAX = 96
ROWS = ROW_MAX + PARTS

LN_EPS = 1e-5
RMS_EPS = 1e-6


def need(eng, sem, n):
    if isinstance(n, int) and n <= 0:
        return
    eng.wait_ge(sem, n)


def upto(n, most=NT):
    return min(n, most) if isinstance(n, int) else n


def one(i):
    return bass.ds(i, 1)


def tile_loop(eng, tiles, stages):
    deepest = max(lag for lag, _ in stages)

    def step(n, parity):
        for lag, stage in stages:
            if isinstance(n, int) and not 0 <= n - lag < tiles:
                continue
            stage(n - lag, (parity + lag) % 2)

    first = deepest + 4
    first += first % 2
    last = first + (tiles - first) // 2 * 2
    for n in range(first):
        step(n, n % 2)
    with eng.Fori(0, (last - first) // 2) as i:
        for u in range(2):
            step(2 * i + (first + u), u)
    for n in range(last, tiles + deepest):
        step(n, n % 2)


def mixer_kernel(nc, a, out):
    with ExitStack() as whole:
        def sb(name, shape, dt=F32, ctx=whole):
            return ctx.enter_context(nc.sbuf_tensor(name, shape, dt))

        x_sb = sb("x_sb", [P, NT, D])
        ident = sb("ident", [P, P])
        split_dram = nc.dram_tensor("split_scratch", [B, PARTS, 2, D, N], BF16, kind="Internal").ap()

        layer0(nc, a, x_sb, ident)
        with ExitStack() as c:
            v_sb = sb("v_sb", [P, NT, D], F32, c)
            y_sb = sb("y_sb", [P, NT, D], F32, c)
            layer1_dense(nc, a, x_sb, ident, v_sb, y_sb, split_dram)
            o_sb = sb("o_sb", [P, NT, D], F32, c)
            layer1_attention(nc, a, ident, v_sb, o_sb, split_dram)
            layer1_out(nc, a, x_sb, ident, y_sb, o_sb, out)


def layer0(nc, a, x_sb, ident):
    with ExitStack() as c:
        def sb(name, shape, dt=F32):
            return c.enter_context(nc.sbuf_tensor("l0_" + name, shape, dt))

        def sem(name):
            return c.enter_context(nc.semaphore("l0_" + name))

        banks = [c.enter_context(nc.psum_tensor(f"l0_bank{i}", [P, BANK], F32)) for i in range(8)]

        w_all = sb("w_all", [P, 6 * D])
        w_out = sb("w_out", [P, D])
        w_o = sb("w_o", [P, D])
        w_e = sb("w_e", [P, E, D])
        w_g = sb("w_g", [P, E])
        w_q = sb("w_q", [P, D])
        w_dT = sb("w_dT", [L, D])
        w_up = sb("w_up", [L, 2 * D])
        gam1 = sb("gam1", [P, 1])
        gam2 = sb("gam2", [P, 1])
        b_down = sb("b_down", [L, 1])
        b_down_rep = sb("b_down_rep", [L, P])
        b_qkv = sb("b_qkv", [P, 3 * D])
        b_out = sb("b_out", [P, D])
        b_o = sb("b_o", [P, D])
        b_g = sb("b_g", [P, E])
        head_mask = sb("head_mask", [P, H])
        half = sb("half", [P, NT])

        st6 = sb("st6", [P, NT, 6])
        mv = sb("mv", [P, NT, 2])
        ve = sb("ve", [P, NT])
        rstd = sb("rstd", [P, NT])
        vr = sb("vr", [P, NT])
        rms1 = sb("rms1", [P, NT])

        xn = sb("xn", [P, NT, D])
        xnb = sb("xnb", [P, NT, D])
        qkv = sb("qkv", [P, NT, 3 * D])
        att = sb("att", [P, 2, H * H])
        rsum = sb("rsum", [P, 2, H])
        ql_T = sb("ql_T", [P, NT, P])
        kv_part = sb("kv_part", [P, NT, D + 1])
        gate = sb("gate", [P, NT, D])
        xs = sb("xs", [P, 2, D])
        xT = sb("xT", [P, 2, P])
        mn = sb("mn", [P, 2, 2 * D])
        ex = sb("ex", [P, 2, 2 * D])
        ql = sb("ql", [P, 2, 2 * D])
        vl = sb("vl", [P, 2, D + 1])
        prod = sb("prod", [P, 2, H * H * HD])
        mx = sb("mx", [P, 2, H])
        o_raw = sb("o_raw", [P, 2, D])
        o_n = sb("o_n", [P, 2, D])
        o_T = sb("o_T", [P, 2, P])
        x2s = sb("x2s", [P, 2, D])
        x2_T = sb("x2_T", [P, 2, P])
        sq = sb("sq", [P, 2, D])
        ss = sb("ss", [P, NT])
        ms = sb("ms", [P, NT])
        rms2 = sb("rms2", [P, NT])
        lg = sb("lg", [P, 2, E])
        nmx = sb("nmx", [P, 2, 1])
        ge = sb("ge", [P, 2, E])
        gs = sb("gs", [P, 2, 1])
        gr = sb("gr", [P, 2, 1])
        gw = sb("gw", [P, 2, E])
        acc = sb("acc", [P, 2, 2, D])
        th = sb("th", [P, 2, D])
        kv_sum = sb("kv_sum", [P, B, D + 1])
        bdks = sb("bdks", [P, B, D + H])
        q_s = sb("q_s", [P, 2, P])
        den = sb("den", [P, 2, H])
        rden = sb("rden", [P, 2, H])
        lin = sb("lin", [P, 2, D])
        lin_T = sb("lin_T", [P, 2, P])
        s_b = sb("s_b", [P, 2, D])
        s_g = sb("s_g", [P, 2, D])

        x_in, w_in = sem("x_in"), sem("w_in")
        prep_ps, prep = sem("prep_ps"), sem("prep")
        stat, pool_pow = sem("stat"), sem("pool_pow")
        xs_ok, xs_T, xT_ok, xs_kept = sem("xs_ok"), sem("xs_T"), sem("xT_ok"), sem("xs_kept")
        projA, projB = sem("projA"), sem("projB")
        mn_ok, ex_ok, ql_ok, vl_ok, qkv_ok = sem("mn_ok"), sem("ex_ok"), sem("ql_ok"), sem("vl_ok"), sem("qkv_ok")
        qlT_kv, qlT_ok = sem("qlT_kv"), sem("qlT_ok")
        xnb_ok = sem("xnb_ok")
        p1_ok, s1_ok, mx_ok, sub_ok, exp_ok, sum_ok, rs_ok = (sem(n) for n in (
            "p1_ok", "s1_ok", "mx_ok", "sub_ok", "exp_ok", "sum_ok", "rs_ok"))
        p2_ok, or_ok, on_ok, on_T, oT_ok, wo_ok, x2_ok = (sem(n) for n in (
            "p2_ok", "or_ok", "on_ok", "on_T", "oT_ok", "wo_ok", "x2_ok"))
        sq_ok, ms_ok, r2_ok, x2_T_ps, x2T_ok, gl_ok, moe_ok = (sem(n) for n in (
            "sq_ok", "ms_ok", "r2_ok", "x2_T_ps", "x2T_ok", "gl_ok", "moe_ok"))
        gv, ge_ok, acc_ok, th_ok, gate_ok = (sem(n) for n in ("gv", "ge_ok", "acc_ok", "th_ok", "gate_ok"))
        kvs = sem("kvs")
        qs_ok, nd_ok, den_ok, rden_ok, lin_ok, lin_T_ps, linT_ok, so_ok, sb_ok, sg_ok, x1_ok = (sem(n) for n in (
            "qs_ok", "nd_ok", "den_ok", "rden_ok", "lin_ok", "lin_T_ps", "linT_ok", "so_ok", "sb_ok", "sg_ok", "x1_ok"))

        W_LOADS = 18
        scale = float(HD) ** -0.5
        v_T, v_A, v_B, v_Q, v_O, v_G, v_M0, v_M1 = banks

        block = c.enter_context(nc.Block())

        @block.sync
        def _(sp):
            x_d = a["L0_attn_x"].rearrange("b (k p) d -> p (b k) d", p=P)
            for k in range(4):
                sp.dma_start(x_sb[:, 4 * k:4 * k + 4, :], x_d[:, 4 * k:4 * k + 4, :]).then_inc(x_in, 16)
            for dst, src in (
                (ident[:], a["ident"]), (w_all[:, 0:3 * D], a["w_qkvT"]), (w_q[:], a["L0_ffn_Wq"]),
                (w_dT[:], a["WdownT"]), (w_up[:], a["L0_ffn_Wup"]), (gam1[:], a["gamma1"]),
                (gam2[:], a["gamma2"]), (b_down[:], a["bdown"]),
                (b_qkv[:, 0:D], a["L0_ffn_bq"].partition_broadcast(P)),
                (b_qkv[:, D:3 * D], a["L0_ffn_bup"].partition_broadcast(P)),
                (w_out[:], a["w_outT"]), (w_o[:], a["L0_ffn_Wo"]),
                (w_e[:], a["L0_ffn_We"].rearrange("e d f -> d e f")), (w_g[:], a["L0_ffn_Wg"]),
                (b_out[:], a["L0_attn_b_out"].partition_broadcast(P)),
                (b_o[:], a["L0_ffn_bo"].partition_broadcast(P)),
                (b_g[:], a["L0_ffn_bg"].partition_broadcast(P)), (head_mask[:], a["head_mask"]),
            ):
                sp.dma_start(dst, src).then_inc(w_in, 16)

        @block.vector
        def _(v):
            v.wait_ge(w_in, 16 * W_LOADS)
            nc.vector.memset(half[:], -0.5).then_inc(prep, 1)
            nc.vector.memset(vl[:, :, D:D + 1], 1.0).then_inc(prep, 1)
            nc.vector.tensor_copy(b_down_rep[:], b_down[:].broadcast_to([L, P])).then_inc(prep, 1)
            nc.vector.tensor_scalar(w_all[:, 3 * D:4 * D], w_q[:], gam1[:], scale, ALU.mult, ALU.mult).then_inc(prep, 1)
            nc.vector.tensor_scalar(w_g[:], w_g[:], gam2[:], None, ALU.mult).then_inc(prep, 1)
            nc.vector.tensor_scalar(w_e[:], w_e[:], gam2[:], None, ALU.mult).then_inc(prep, 1)
            nc.vector.tensor_scalar(b_qkv[:, 0:D], b_qkv[:, 0:D], scale, None, ALU.mult).then_inc(prep, 1)
            v.wait_ge(prep_ps, 1)
            nc.vector.tensor_scalar(w_all[:, 4 * D:6 * D], v_A[:, 0:2 * D], gam1[:], None, ALU.mult).then_inc(prep, 1)
            v.wait_ge(prep_ps, 2)
            nc.vector.tensor_tensor(b_qkv[:, D:3 * D], v_B[:, 0:2 * D], b_qkv[:, D:3 * D], ALU.add).then_inc(prep, 1)

            v.wait_ge(x_in, 16 * 4)
            with v.Fori(0, NT) as t:
                nc.vector.bn_stats(st6[:, one(t), :], x_sb[:, one(t), :]).then_inc(stat, 1)
            v.wait_ge(stat, NT)
            for t in range(NT):
                nc.vector.bn_aggr(mv[:, t, :], st6[:, t, :]).then_inc(stat, 1)
            v.wait_ge(stat, 2 * NT)
            nc.vector.tensor_scalar(ve[:], mv[:, :, 1], LN_EPS, None, ALU.add).then_inc(stat, 1)
            v.wait_ge(pool_pow, 1)
            nc.vector.tensor_tensor(vr[:], rstd[:], rstd[:], ALU.mult).then_inc(stat, 1)
            v.wait_ge(stat, 2 * NT + 2)
            nc.vector.tensor_tensor(vr[:], vr[:], mv[:, :, 1], ALU.mult).then_inc(stat, 1)
            v.wait_ge(stat, 2 * NT + 3)
            nc.vector.tensor_scalar(vr[:], vr[:], RMS_EPS, None, ALU.add).then_inc(stat, 1)
            v.wait_ge(pool_pow, 2)

            def normalise(t, p):
                need(v, xs_kept, t - 1)
                need(v, xs_T, t - 1)
                nc.vector.tensor_scalar(xs[:, p, :], x_sb[:, one(t), :], mv[:, one(t), 0], rstd[:, one(t)],
                                        ALU.subtract, ALU.mult).then_inc(xs_ok, 1)

            def elu_min(t, p):
                v.wait_ge(projA, t + 1)
                need(v, ex_ok, t - 1)
                nc.vector.tensor_scalar(mn[:, p, :], v_A[:, 0:2 * D], 0.0, None, ALU.min).then_inc(mn_ok, 1)

            def elu_sum(t, p):
                v.wait_ge(ex_ok, t + 1)
                need(v, qlT_kv, t - 1)
                nc.vector.scalar_tensor_tensor(ql[:, p, :], v_A[:, 0:2 * D], 0.0, ex[:, p, :],
                                               ALU.max, ALU.add).then_inc(ql_ok, 1)

            def token_qkv(t, p):
                v.wait_ge(projB, t + 1)
                nc.vector.scalar_tensor_tensor(qkv[:, one(t), :], v_B[:, 0:3 * D], rms1[:, one(t)], b_qkv[:],
                                               ALU.mult, ALU.add).then_inc(qkv_ok, 1)

            def scores(t, p):
                v.wait_ge(p1_ok, t + 1)
                need(v, p2_ok, t - 1)
                nc.vector.tensor_reduce(att[:, p, :], prod[:, 0, :].rearrange("p (s d) -> p s d", d=HD),
                                        AX.X, ALU.add).then_inc(s1_ok, 1)
                v.wait_ge(s1_ok, t + 1)
                need(v, sub_ok, t - 1)
                at = att[:, p, :].rearrange("p (h g) -> p h g", g=H)
                nc.vector.tensor_reduce(mx[:, p, :], at, AX.X, ALU.max).then_inc(mx_ok, 1)
                v.wait_ge(mx_ok, t + 1)
                nc.vector.tensor_tensor(at, at, mx[:, p, :].unsqueeze(2).broadcast_to([P, H, H]),
                                        ALU.subtract).then_inc(sub_ok, 1)

            def sums(t, p):
                v.wait_ge(exp_ok, t + 1)
                nc.vector.tensor_reduce(rsum[:, p, :], att[:, p, :].rearrange("p (h g) -> p h g", g=H),
                                        AX.X, ALU.add).then_inc(sum_ok, 1)
                v.wait_ge(sum_ok, t + 1)
                nc.vector.reciprocal(rsum[:, p, :], rsum[:, p, :]).then_inc(rs_ok, 1)

            def weighted(t, p):
                v.wait_ge(p2_ok, t + 1)
                nc.vector.tensor_reduce(o_raw[:, p, :], prod[:, 1, :].rearrange("p (s g) -> p s g", g=H),
                                        AX.X, ALU.add).then_inc(or_ok, 1)
                v.wait_ge(or_ok, t + 1)
                v.wait_ge(rs_ok, t + 1)
                need(v, on_T, t - 1)
                nc.vector.tensor_tensor(o_n[:, p, :].rearrange("p (h d) -> p h d", d=HD),
                                        o_raw[:, p, :].rearrange("p (h d) -> p h d", d=HD),
                                        rsum[:, p, :].unsqueeze(2).broadcast_to([P, H, HD]),
                                        ALU.mult).then_inc(on_ok, 1)

            def residual(t, p):
                v.wait_ge(wo_ok, t + 1)
                v.wait_ge(xnb_ok, t + 1)
                need(v, x2_T_ps, t - 1)
                need(v, sq_ok, t - 1)
                nc.vector.tensor_tensor(x2s[:, p, :], v_O[:, P:2 * P], xnb[:, one(t), :].rearrange("p o d -> p (o d)"),
                                        ALU.add).then_inc(x2_ok, 1)

            def mean_square(t, p):
                v.wait_ge(sq_ok, t + 1)
                nc.vector.tensor_scalar(ms[:, one(t)], ss[:, one(t)], 1.0 / D, RMS_EPS, ALU.mult, ALU.add).then_inc(ms_ok, 1)

            def gate_logits(t, p):
                v.wait_ge(gl_ok, t + 1)
                v.wait_ge(r2_ok, t + 1)
                nc.vector.scalar_tensor_tensor(lg[:, p, :], v_G[:, 0:E], rms2[:, one(t)], b_g[:],
                                               ALU.mult, ALU.add).then_inc(gv, 1)
                v.wait_ge(gv, 4 * t + 1)
                nc.vector.tensor_reduce(nmx[:, p, :], lg[:, p, :], AX.X, ALU.max, negate=True).then_inc(gv, 1)

            def experts(t, p):
                v.wait_ge(ge_ok, t + 1)
                nc.vector.reciprocal(gr[:, p, :], gs[:, p, :]).then_inc(gv, 1)
                v.wait_ge(gv, 4 * t + 3)
                nc.vector.tensor_scalar(gw[:, p, :], ge[:, p, :], gr[:, p, :], rms2[:, one(t)],
                                        ALU.mult, ALU.mult).then_inc(gv, 1)
                v.wait_ge(gv, 4 * t + 4)
                v.wait_ge(moe_ok, t + 1)
                need(v, th_ok, t - 1)
                for e in range(E):
                    bank = (v_M0, v_M1)[e // 4]
                    before = x2s[:, p, :] if e == 0 else acc[:, p, (e - 1) % 2, :]
                    nc.vector.scalar_tensor_tensor(acc[:, p, e % 2, :], bank[:, e % 4 * D:(e % 4 + 1) * D],
                                                   gw[:, p, e:e + 1], before, ALU.mult, ALU.add).then_inc(acc_ok, 1)
                    v.wait_ge(acc_ok, E * t + e + 1)

            def silu(t, p):
                v.wait_ge(th_ok, t + 1)
                nc.vector.scalar_tensor_tensor(gate[:, one(t), :], th[:, p:p + 1, :], 1.0, acc[:, p:p + 1, (E - 1) % 2, :],
                                               ALU.add, ALU.mult).then_inc(gate_ok, 1)

            tile_loop(v, NT, [(2, scores), (0, normalise), (3, weighted), (1, elu_min), (4, residual),
                              (1, elu_sum), (1, token_qkv), (2, sums), (4, mean_square), (5, gate_logits),
                              (5, experts), (5, silu)])

            v.wait_ge(qlT_ok, 2 * NT)
            for b in range(B):
                nc.vector.tensor_reduce(kv_sum[:, b, :], kv_part[:, b * TB:(b + 1) * TB, :].rearrange("p k n -> p n k"),
                                        AX.X, ALU.add).then_inc(kvs, 1)
            v.wait_ge(kvs, B)
            for b in range(B):
                nc.vector.tensor_tensor(bdks[:, b, 0:D].rearrange("p (h m) -> p h m", m=HD),
                                        kv_sum[:, b, 0:D].rearrange("p (h m) -> p h m", m=HD),
                                        head_mask[:].unsqueeze(2).broadcast_to([P, H, HD]), ALU.mult).then_inc(kvs, 1)
                nc.vector.tensor_scalar(bdks[:, b, D:D + H], head_mask[:], kv_sum[:, b, D:D + 1], None,
                                        ALU.mult).then_inc(kvs, 1)

            def denominators(t, p):
                v.wait_ge(nd_ok, t + 1)
                nc.vector.tensor_scalar(den[:, p, :], v_A[:, D:D + H], 1e-6, None, ALU.add).then_inc(den_ok, 1)
                v.wait_ge(den_ok, t + 1)
                nc.vector.reciprocal(rden[:, p, :], den[:, p, :]).then_inc(rden_ok, 1)
                v.wait_ge(rden_ok, t + 1)
                need(v, lin_T_ps, t - 1)
                nc.vector.tensor_tensor(lin[:, p, :].rearrange("p (h m) -> p h m", m=HD),
                                        v_A[:, 0:D].rearrange("p (h m) -> p h m", m=HD),
                                        rden[:, p, :].unsqueeze(2).broadcast_to([P, H, HD]), ALU.mult).then_inc(lin_ok, 1)

            def gated(t, p):
                v.wait_ge(so_ok, t + 1)
                v.wait_ge(gate_ok, NT)
                nc.vector.tensor_tensor(s_b[:, p, :], v_O[:, 0:D], b_out[:], ALU.add).then_inc(sb_ok, 1)
                v.wait_ge(sb_ok, t + 1)
                nc.vector.scalar_tensor_tensor(s_g[:, p:p + 1, :], s_b[:, p:p + 1, :], 0.5, gate[:, one(t), :],
                                               ALU.mult, ALU.mult).then_inc(sg_ok, 1)
                v.wait_ge(sg_ok, t + 1)
                nc.vector.tensor_tensor(x_sb[:, one(t), :], x_sb[:, one(t), :], s_g[:, p:p + 1, :], ALU.add).then_inc(x1_ok, 1)

            tile_loop(v, NT, [(0, denominators), (1, gated)])

        @block.tensor
        def _(pe):
            pe.wait_ge(w_in, 16 * W_LOADS)
            nc.tensor.matmul(v_A[:, 0:2 * D], w_dT[:], w_up[:], start=True, stop=True).then_inc(prep_ps, 1)
            pe.wait_ge(prep, 3)
            nc.tensor.matmul(v_B[:, 0:2 * D], b_down_rep[:], w_up[:], start=True, stop=True).then_inc(prep_ps, 1)
            pe.wait_ge(prep, 9)

            def transpose_x(t, p):
                pe.wait_ge(xs_ok, t + 1)
                need(pe, xT_ok, t)
                need(pe, oT_ok, t - 3)
                nc.tensor.transpose(v_T[:, 0:P], xs[:, p, :], ident[:]).then_inc(xs_T, 1)

            def project(t, p):
                pe.wait_ge(xT_ok, t + 1)
                need(pe, ql_ok, t)
                need(pe, vl_ok, t)
                nc.tensor.matmul(v_A[:, 0:3 * D], xT[:, p, :], w_all[:, 0:3 * D], start=True, stop=True).then_inc(projA, 1)
                need(pe, qkv_ok, t)
                nc.tensor.matmul(v_B[:, 0:3 * D], xT[:, p, :], w_all[:, 3 * D:6 * D], start=True, stop=True).then_inc(projB, 1)

            def linear_kv(t, p):
                pe.wait_ge(ql_ok, t + 1)
                pe.wait_ge(vl_ok, t + 1)
                need(pe, qlT_ok, 2 * t)
                need(pe, x2T_ok, t - 3)
                nc.tensor.transpose(v_Q[:, 0:P], ql[:, p, 0:D], ident[:])
                nc.tensor.matmul(v_Q[:, P:P + D + 1], ql[:, p, D:2 * D], vl[:, p, :], start=True, stop=True).then_inc(qlT_kv, 1)

            def transpose_o(t, p):
                pe.wait_ge(on_ok, t + 1)
                need(pe, xT_ok, upto(t + 4))
                need(pe, oT_ok, t)
                nc.tensor.transpose(v_T[:, P:2 * P], o_n[:, p, :], ident[:]).then_inc(on_T, 1)

            def project_o(t, p):
                pe.wait_ge(oT_ok, t + 1)
                need(pe, x2_ok, t)
                nc.tensor.matmul(v_O[:, P:2 * P], o_T[:, p, :], w_o[:], start=True, stop=True).then_inc(wo_ok, 1)

            def transpose_x2(t, p):
                pe.wait_ge(x2_ok, t + 1)
                need(pe, x2T_ok, t)
                need(pe, qlT_ok, 2 * upto(t + 4))
                nc.tensor.transpose(v_Q[:, 3 * P:4 * P], x2s[:, p, :], ident[:]).then_inc(x2_T_ps, 1)

            def expert_products(t, p):
                pe.wait_ge(x2T_ok, t + 1)
                need(pe, gv, 4 * t)
                need(pe, acc_ok, E * t)
                nc.tensor.matmul(v_G[:, 0:E], x2_T[:, p, :], w_g[:], start=True, stop=True).then_inc(gl_ok, 1)
                for m, bank in enumerate((v_M0, v_M1)):
                    last = nc.tensor.matmul(bank[:, :], x2_T[:, p, :],
                                            w_e[:, 4 * m:4 * m + 4, :].rearrange("p e f -> p (e f)"), start=True, stop=True)
                last.then_inc(moe_ok, 1)

            tile_loop(pe, NT, [(0, transpose_x), (3, transpose_o), (1, project), (3, project_o), (1, linear_kv),
                               (4, transpose_x2), (4, expert_products)])

            pe.wait_ge(kvs, 3 * B)
            pe.wait_ge(x2T_ok, NT)

            def transpose_lin(t, p):
                pe.wait_ge(lin_ok, t + 1)
                need(pe, linT_ok, t)
                nc.tensor.transpose(v_Q[:, 0:P], lin[:, p, :], ident[:]).then_inc(lin_T_ps, 1)

            def project_lin(t, p):
                pe.wait_ge(linT_ok, t + 1)
                need(pe, sb_ok, t)
                nc.tensor.matmul(v_O[:, 0:D], lin_T[:, p, :], w_out[:], start=True, stop=True).then_inc(so_ok, 1)

            def nd(t, p):
                pe.wait_ge(qs_ok, t + 1)
                need(pe, lin_ok, t)
                nc.tensor.matmul(v_A[:, 0:D + H], q_s[:, p, :], bdks[:, one(t // TB), :], start=True, stop=True).then_inc(nd_ok, 1)

            tile_loop(pe, NT, [(0, nd), (0, transpose_lin), (0, project_lin)])

        @block.scalar
        def _(s):
            def copies_x(t, p):
                s.wait_ge(xs_T, t + 1)
                need(s, projB, t - 1)
                nc.scalar.copy(xT[:, p, :], v_T[:, 0:P]).then_inc(xT_ok, 1)
                nc.scalar.copy(xn[:, one(t), :], xs[:, p:p + 1, :]).then_inc(xs_kept, 1)

            def exps(t, p):
                s.wait_ge(mn_ok, t + 1)
                need(s, ql_ok, t - 1)
                nc.scalar.activation(ex[:, p, :], mn[:, p, :], ACT.Exp).then_inc(ex_ok, 1)
                need(s, qlT_kv, t - 1)
                s.wait_ge(ql_ok, t + 1)
                nc.scalar.copy(vl[:, p, 0:D], v_A[:, 2 * D:3 * D]).then_inc(vl_ok, 1)

            def keep_linear(t, p):
                s.wait_ge(qlT_kv, t + 1)
                nc.scalar.copy(ql_T[:, one(t), :], v_Q[:, 0:P]).then_inc(qlT_ok, 1)
                nc.scalar.copy(kv_part[:, one(t), :], v_Q[:, P:P + D + 1]).then_inc(qlT_ok, 1)

            def softmax_exp(t, p):
                s.wait_ge(sub_ok, t + 1)
                nc.scalar.activation(att[:, p, :], att[:, p, :], ACT.Exp).then_inc(exp_ok, 1)

            def copy_oT(t, p):
                s.wait_ge(on_T, t + 1)
                need(s, wo_ok, t - 1)
                nc.scalar.copy(o_T[:, p, :], v_T[:, P:2 * P]).then_inc(oT_ok, 1)

            def square_x2(t, p):
                s.wait_ge(x2_ok, t + 1)
                need(s, sq_ok, t - 1)
                nc.scalar.activation(sq[:, p, :], x2s[:, p, :], ACT.Square, accum_out=ss[:, one(t)]).then_inc(sq_ok, 1)
                s.wait_ge(x2_T_ps, t + 1)
                need(s, moe_ok, t - 1)
                nc.scalar.copy(x2_T[:, p, :], v_Q[:, 3 * P:4 * P]).then_inc(x2T_ok, 1)

            def gate_exp(t, p):
                s.wait_ge(gv, 4 * t + 2)
                nc.scalar.activation(ge[:, p, :], lg[:, p, :], ACT.Exp, bias=nmx[:, p, :],
                                     accum_out=gs[:, p, :]).then_inc(ge_ok, 1)

            def gate_tanh(t, p):
                s.wait_ge(acc_ok, E * t + E)
                need(s, gate_ok, t - 1)
                nc.scalar.activation(th[:, p, :], acc[:, p, (E - 1) % 2, :], ACT.Tanh, scale=0.5).then_inc(th_ok, 1)

            tile_loop(s, NT, [(0, copies_x), (3, copy_oT), (1, exps), (1, keep_linear), (2, softmax_exp),
                              (4, square_x2), (5, gate_exp), (5, gate_tanh)])

            def copy_q(t, p):
                need(s, nd_ok, t - 1)
                nc.scalar.copy(q_s[:, p:p + 1, :], ql_T[:, one(t), :]).then_inc(qs_ok, 1)

            def copy_linT(t, p):
                s.wait_ge(lin_T_ps, t + 1)
                need(s, so_ok, t - 1)
                nc.scalar.copy(lin_T[:, p, :], v_Q[:, 0:P]).then_inc(linT_ok, 1)

            s.wait_ge(qlT_ok, 2 * NT)
            tile_loop(s, NT, [(0, copy_q), (1, copy_linT)])

        @block.gpsimd
        def _(g):
            g.wait_ge(prep, 1)
            g.wait_ge(stat, 2 * NT + 1)
            nc.gpsimd.tensor_tensor(rstd[:], ve[:], half[:], ALU.pow).then_inc(pool_pow, 1)
            g.wait_ge(stat, 2 * NT + 4)
            nc.gpsimd.tensor_tensor(rms1[:], vr[:], half[:], ALU.pow).then_inc(pool_pow, 1)

            def products_qk(t, p):
                g.wait_ge(qkv_ok, t + 1)
                need(g, s1_ok, t)
                q = qkv[:, one(t), 0:D].rearrange("p o (h d) -> p (o h) d", d=HD)
                k = qkv[:, one(t), D:3 * D].rearrange("p o (h d) -> p (o h) d", d=2 * HD)[:, :, 0:HD]
                nc.gpsimd.tensor_tensor(prod[:, 0, :].rearrange("p (h g d) -> p h g d", g=H, d=HD),
                                        q.unsqueeze(2).broadcast_to([P, H, H, HD]),
                                        k.unsqueeze(1).broadcast_to([P, H, H, HD]), ALU.mult).then_inc(p1_ok, 1)

            def products_av(t, p):
                g.wait_ge(exp_ok, t + 1)
                need(g, or_ok, t)
                w = att[:, p, :].rearrange("p (h g) -> p h g", g=H)
                val = qkv[:, one(t), D:3 * D].rearrange("p o (h d) -> p (o h) d", d=2 * HD)[:, :, HD:2 * HD]
                nc.gpsimd.tensor_tensor(prod[:, 1, :].rearrange("p (h d g) -> p h d g", g=H, d=HD),
                                        w.unsqueeze(2).broadcast_to([P, H, HD, H]),
                                        val.rearrange("p g d -> p d g").unsqueeze(1).broadcast_to([P, H, HD, H]),
                                        ALU.mult).then_inc(p2_ok, 1)

            def add_bias(t, p):
                g.wait_ge(xs_kept, t + 1)
                nc.gpsimd.tensor_tensor(xnb[:, one(t), :], xn[:, one(t), :], b_o[:].unsqueeze(1), ALU.add).then_inc(xnb_ok, 1)

            def rms_x2(t, p):
                g.wait_ge(ms_ok, t + 1)
                nc.gpsimd.tensor_tensor(rms2[:, one(t)], ms[:, one(t)], half[:, 0:1], ALU.pow).then_inc(r2_ok, 1)

            tile_loop(g, NT, [(1, products_qk), (0, add_bias), (2, products_av), (4, rms_x2)])


def layer1_dense(nc, a, x_sb, ident, v_sb, y_sb, split_dram):
    with ExitStack() as c:
        def sb(name, shape, dt=F32):
            return c.enter_context(nc.sbuf_tensor("l1_" + name, shape, dt))

        def sem(name):
            return c.enter_context(nc.semaphore("l1_" + name))

        banks = [c.enter_context(nc.psum_tensor(f"l1_bank{i}", [P, BANK], F32)) for i in range(8)]
        k_T, k_QK, k_V, k_H, k_T4, k_Y = banks[:6]

        w_qkv = sb("w_qkv", [P, 3, D])
        lora_b = sb("lora_b", [R, 3, D])
        lora_aT = sb("lora_aT", [R, 3, D])
        w1 = sb("w1", [P, HID])
        w2 = sb("w2", [P, HC, D])
        tern = sb("tern", [P, 2, HID])
        w1g = sb("w1g", [P, HID])
        w2g = sb("w2g", [P, HC, D])
        g1 = sb("g1", [P, 1])
        be1 = sb("be1", [P, 1])
        g2 = sb("g2", [P, HC])
        be2 = sb("be2", [P, HC])
        be1_rep = sb("be1_rep", [P, P])
        be2_rep = sb("be2_rep", [P, HC, P])
        b1 = sb("b1", [P, HID])
        b2 = sb("b2", [P, D])
        asum = sb("asum", [P, 2])
        mean = sb("mean", [P, 2])
        inv = sb("inv", [P, 2])
        ones = sb("ones", [P, P])
        half = sb("half", [P, NT])
        st6 = sb("st6", [P, NT, 6])
        mv = sb("mv", [P, NT, 2])
        ve = sb("ve", [P, NT])
        rstd = sb("rstd", [P, NT])
        vr = sb("vr", [P, NT])
        rln1 = sb("rln1", [P, NT])
        h = sb("h", [P, NT, HID])
        hst6 = sb("hst6", [P, NT, 6])
        hmv = sb("hmv", [P, NT, 2])
        hve = sb("hve", [P, NT])
        hrstd = sb("hrstd", [P, NT])
        parts = sb("parts", [P, PARTS, 2, NT, P], BF16)
        xs = sb("xs", [P, 2, D])
        xT = sb("xT", [P, 2, P])
        rest = sb("rest", [P, 2, 2, 2 * P])
        hn = sb("hn", [P, 2, HID])
        hT = sb("hT", [P, 2, HID])

        w_in, prep, prep_ps, stat, pool_pow = (sem(n) for n in ("w_in", "prep", "prep_ps", "stat", "pool_pow"))
        xs_ok, xs_T, xT_ok, qk_ok, pv_ok, ph_ok = (sem(n) for n in ("xs_ok", "xs_T", "xT_ok", "qk_ok", "pv_ok", "ph_ok"))
        part1, rest1, part2, part3, v_ok = (sem(n) for n in ("part1", "rest1", "part2", "part3", "v_ok"))
        h_ok, gelu_ok, hst, hn_ok, hn_T, hT_ok, y_ps, y_ok = (sem(n) for n in (
            "h_ok", "gelu_ok", "hst", "hn_ok", "hn_T", "hT_ok", "y_ps", "y_ok"))
        stored = sem("stored")

        block = c.enter_context(nc.Block())
        loads = []
        for n, k in enumerate("qkv"):
            loads += [(w_qkv[:, n, :], a[f"W{k}T"]), (lora_b[:, n, :], a[f"L1_attn_B{k}"]), (lora_aT[:, n, :], a[f"A{k}T"])]
        loads += [(w1[:], a["w1T"]), (w2[:], a["w2T"].rearrange("(c p) n -> p c n", p=P)),
                  (g1[:], a["ln1_g"]), (be1[:], a["ln1_b"]),
                  (g2[:], a["ln2_g"].rearrange("(c p) o -> p (c o)", p=P)),
                  (be2[:], a["ln2_b"].rearrange("(c p) o -> p (c o)", p=P)),
                  (b1[:], a["L1_ffn_b1"].partition_broadcast(P)), (b2[:], a["L1_ffn_b2"].partition_broadcast(P))]
        W_LOADS = len(loads)

        @block.sync
        def _(sp):
            for dst, src in loads:
                sp.dma_start(dst, src, allow_slow_non_contiguous=True).then_inc(w_in, 16)
            for b in range(B):
                for part in range(PARTS):
                    sp.wait_ge((part1, part2, part3)[part], (b + 1) * TB)
                    for w in range(2):
                        sp.dma_start(split_dram[b, part, w, :, :],
                                     parts[:, part, w, b * TB:(b + 1) * TB, :].rearrange("p k t -> p (k t)")).then_inc(stored, 16)
            sp.wait_ge(stored, 16 * B * PARTS * 2)

        @block.vector
        def _(v):
            v.wait_ge(w_in, 16 * W_LOADS)
            count = [0]

            def then(ins):
                count[0] += 1
                ins.then_inc(prep, 1)
                v.wait_ge(prep, count[0])

            then(nc.vector.memset(half[:], -0.5))
            then(nc.vector.memset(ones[:], 1.0))
            w2f = w2[:].rearrange("p c n -> p (c n)")
            then(nc.vector.tensor_reduce(asum[:, 0:1], w1[:], AX.X, ALU.add, apply_absolute_value=True))
            then(nc.vector.tensor_reduce(asum[:, 1:2], w2f, AX.X, ALU.add, apply_absolute_value=True))
            v.wait_ge(prep_ps, 1)
            then(nc.vector.tensor_scalar(mean[:], k_T[:, 0:2], 1.0 / (D * HID), 1e-5, ALU.mult, ALU.max))
            then(nc.vector.reciprocal(inv[:], mean[:]))
            for n, w in enumerate((w1[:], w2f)):
                then(nc.vector.tensor_scalar(tern[:, 0, :], w, inv[:, n:n + 1], 0.5, ALU.mult, ALU.is_gt))
                then(nc.vector.tensor_scalar(tern[:, 1, :], w, inv[:, n:n + 1], -0.5, ALU.mult, ALU.is_lt))
                then(nc.vector.tensor_tensor(tern[:, 0, :], tern[:, 0, :], tern[:, 1, :], ALU.subtract))
                then(nc.vector.tensor_scalar(w, tern[:, 0, :], mean[:, n:n + 1], None, ALU.mult))
            then(nc.vector.tensor_scalar(w1g[:], w1[:], g1[:], None, ALU.mult))
            then(nc.vector.tensor_tensor(w2g[:], w2[:], g2[:].unsqueeze(2).broadcast_to([P, HC, D]), ALU.mult))
            then(nc.vector.tensor_copy(be1_rep[:], be1[:].broadcast_to([P, P])))
            then(nc.vector.tensor_copy(be2_rep[:], be2[:].unsqueeze(2).broadcast_to([P, HC, P])))
            v.wait_ge(prep_ps, 2)
            then(nc.vector.scalar_tensor_tensor(w_qkv[:].rearrange("p n d -> p (n d)"), k_QK[:, 0:3 * D], 2.0,
                                                w_qkv[:].rearrange("p n d -> p (n d)"), ALU.mult, ALU.add))
            then(nc.vector.tensor_scalar(w_qkv[:, 0, :], w_qkv[:, 0, :], float(HD) ** -0.5, None, ALU.mult))
            v.wait_ge(prep_ps, 4)
            then(nc.vector.tensor_tensor(b1[:], k_H[:, :], b1[:], ALU.add))
            then(nc.vector.tensor_tensor(b2[:], k_Y[:, 0:D], b2[:], ALU.add))

            with v.Fori(0, NT) as t:
                nc.vector.bn_stats(st6[:, one(t), :], x_sb[:, one(t), :]).then_inc(stat, 1)
            v.wait_ge(stat, NT)
            for t in range(NT):
                nc.vector.bn_aggr(mv[:, t, :], st6[:, t, :]).then_inc(stat, 1)
            v.wait_ge(stat, 2 * NT)
            nc.vector.tensor_scalar(ve[:], mv[:, :, 1], LN_EPS, None, ALU.add).then_inc(stat, 1)
            v.wait_ge(pool_pow, 1)
            nc.vector.tensor_tensor(vr[:], rstd[:], rstd[:], ALU.mult).then_inc(stat, 1)
            v.wait_ge(stat, 2 * NT + 2)
            nc.vector.tensor_tensor(vr[:], vr[:], mv[:, :, 1], ALU.mult).then_inc(stat, 1)
            v.wait_ge(stat, 2 * NT + 3)
            nc.vector.tensor_scalar(vr[:], vr[:], LN_EPS, None, ALU.add).then_inc(stat, 1)
            v.wait_ge(pool_pow, 2)

            def normalise(t, p):
                need(v, xs_T, t - 1)
                nc.vector.tensor_scalar(xs[:, p:p + 1, :], x_sb[:, one(t), :], mv[:, one(t), 0], rstd[:, one(t)],
                                        ALU.subtract, ALU.mult).then_inc(xs_ok, 1)

            def hidden(t, p):
                v.wait_ge(ph_ok, t + 1)
                nc.vector.scalar_tensor_tensor(h[:, one(t), :], k_H[:, :], rln1[:, one(t)], b1[:],
                                               ALU.mult, ALU.add).then_inc(h_ok, 1)

            def first_rest(t, p):
                v.wait_ge(part1, t + 1)
                need(v, part3, t - 1)
                nc.vector.tensor_tensor(rest[:, p, 0, :], k_QK[:, 0:2 * P],
                                        parts[:, 0, :, one(t), :].rearrange("p w o t -> p w (o t)"), ALU.subtract).then_inc(rest1, 1)

            def last_part(t, p):
                v.wait_ge(part2, t + 1)
                nc.vector.tensor_tensor(parts[:, 2, :, one(t), :].rearrange("p w o t -> p w (o t)"), rest[:, p, 0, :].rearrange("p (w t) -> p w t", w=2),
                                        parts[:, 1, :, one(t), :].rearrange("p w o t -> p w (o t)"), ALU.subtract).then_inc(part3, 1)

            def hidden_stats(t, p):
                v.wait_ge(gelu_ok, t + 1)
                nc.vector.bn_stats(hst6[:, one(t), :], h[:, one(t), :]).then_inc(hst, 1)

            tile_loop(v, NT, [(0, normalise), (1, hidden), (1, first_rest), (2, hidden_stats), (1, last_part)])
            v.wait_ge(hst, NT)
            for t in range(NT):
                nc.vector.bn_aggr(hmv[:, t, :], hst6[:, t, :]).then_inc(hst, 1)
            v.wait_ge(hst, 2 * NT)
            nc.vector.tensor_scalar(hve[:], hmv[:, :, 1], LN_EPS, None, ALU.add).then_inc(hst, 1)
            v.wait_ge(pool_pow, 3)

            def normalise_hidden(t, p):
                need(v, hn_T, t - 1)
                nc.vector.tensor_scalar(hn[:, p:p + 1, :], h[:, one(t), :], hmv[:, one(t), 0], hrstd[:, one(t)],
                                        ALU.subtract, ALU.mult).then_inc(hn_ok, 1)

            def keep_y(t, p):
                v.wait_ge(y_ps, t + 1)
                nc.vector.tensor_tensor(y_sb[:, one(t), :], k_Y[:, 0:D].unsqueeze(1), b2[:].unsqueeze(1), ALU.add).then_inc(y_ok, 1)

            tile_loop(v, NT, [(0, normalise_hidden), (2, keep_y)])
            v.wait_ge(y_ok, NT)

        @block.tensor
        def _(pe):
            pe.wait_ge(prep, 4)
            nc.tensor.matmul(k_T[:, 0:2], ones[:], asum[:], start=True, stop=True).then_inc(prep_ps, 1)
            for n in range(3):
                last = nc.tensor.matmul(k_QK[:, n * D:(n + 1) * D], lora_b[:, n, :], lora_aT[:, n, :], start=True, stop=True)
            last.then_inc(prep_ps, 1)
            pe.wait_ge(prep, 18)
            nc.tensor.matmul(k_H[:, :], be1_rep[:], w1[:], start=True, stop=True).then_inc(prep_ps, 1)
            for n in range(HC):
                last = nc.tensor.matmul(k_Y[:, 0:D], be2_rep[:, n, :], w2[:, n, :], start=(n == 0), stop=(n == HC - 1))
            last.then_inc(prep_ps, 1)
            pe.wait_ge(prep, 22)

            def transpose_x(t, p):
                pe.wait_ge(xs_ok, t + 1)
                need(pe, xT_ok, t)
                nc.tensor.transpose(k_T[:, 0:P], xs[:, p, :], ident[:]).then_inc(xs_T, 1)

            def project(t, p):
                pe.wait_ge(xT_ok, t + 1)
                need(pe, rest1, t)
                for n in range(2):
                    last = nc.tensor.matmul(k_QK[:, n * P:(n + 1) * P], w_qkv[:, n, :], xT[:, p, :], start=True, stop=True)
                last.then_inc(qk_ok, 1)
                need(pe, h_ok, t)
                nc.tensor.matmul(k_H[:, :], xT[:, p, :], w1g[:], start=True, stop=True).then_inc(ph_ok, 1)
                need(pe, v_ok, t)
                nc.tensor.matmul(k_V[:, 0:D], xT[:, p, :], w_qkv[:, 2, :], start=True, stop=True).then_inc(pv_ok, 1)

            tile_loop(pe, NT, [(0, transpose_x), (1, project)])

            def transpose_hidden(t, p):
                pe.wait_ge(hn_ok, t + 1)
                need(pe, hT_ok, t)
                for n in range(HC):
                    last = nc.tensor.transpose(k_T4[:, n * P:(n + 1) * P], hn[:, p, n * P:(n + 1) * P], ident[:])
                last.then_inc(hn_T, 1)

            def second(t, p):
                pe.wait_ge(hT_ok, t + 1)
                need(pe, y_ok, t)
                for n in range(HC):
                    last = nc.tensor.matmul(k_Y[:, 0:D], hT[:, p, n * P:(n + 1) * P], w2g[:, n, :],
                                            start=(n == 0), stop=(n == HC - 1))
                last.then_inc(y_ps, 1)

            tile_loop(pe, NT, [(0, transpose_hidden), (1, second)])

        @block.scalar
        def _(s):
            def copy_xT(t, p):
                s.wait_ge(xs_T, t + 1)
                need(s, pv_ok, t - 1)
                nc.scalar.copy(xT[:, p, :], k_T[:, 0:P]).then_inc(xT_ok, 1)

            def split(t, p):
                s.wait_ge(qk_ok, t + 1)
                nc.scalar.copy(parts[:, 0, :, one(t), :].rearrange("p w o t -> p w (o t)"), k_QK[:, 0:2 * P].rearrange("p (w t) -> p w t", w=2)).then_inc(part1, 1)
                s.wait_ge(pv_ok, t + 1)
                nc.scalar.copy(v_sb[:, one(t), :], k_V[:, 0:D]).then_inc(v_ok, 1)

            def second_part(t, p):
                s.wait_ge(rest1, t + 1)
                nc.scalar.copy(parts[:, 1, :, one(t), :].rearrange("p w o t -> p w (o t)"), rest[:, p, 0, :].rearrange("p (w t) -> p w t", w=2)).then_inc(part2, 1)

            def gelu(t, p):
                s.wait_ge(h_ok, t + 1)
                nc.scalar.activation(h[:, one(t), :], h[:, one(t), :], ACT.Gelu).then_inc(gelu_ok, 1)

            tile_loop(s, NT, [(0, copy_xT), (1, split), (1, gelu), (1, second_part)])

            def copy_hT(t, p):
                s.wait_ge(hn_T, t + 1)
                need(s, y_ps, t - 1)
                nc.scalar.copy(hT[:, p, :], k_T4[:, :]).then_inc(hT_ok, 1)

            tile_loop(s, NT, [(0, copy_hT)])

        @block.gpsimd
        def _(g):
            g.wait_ge(prep, 1)
            g.wait_ge(stat, 2 * NT + 1)
            nc.gpsimd.tensor_tensor(rstd[:], ve[:], half[:], ALU.pow).then_inc(pool_pow, 1)
            g.wait_ge(stat, 2 * NT + 4)
            nc.gpsimd.tensor_tensor(rln1[:], vr[:], half[:], ALU.pow).then_inc(pool_pow, 1)
            g.wait_ge(hst, 2 * NT + 1)
            nc.gpsimd.tensor_tensor(hrstd[:], hve[:], half[:], ALU.pow).then_inc(pool_pow, 1)


def layer1_attention(nc, a, ident, v_sb, o_sb, split_dram):
    with ExitStack() as c:
        def sb(name, shape, dt=F32):
            return c.enter_context(nc.sbuf_tensor("at_" + name, shape, dt))

        def sem(name):
            return c.enter_context(nc.semaphore("at_" + name))

        s_bank = [c.enter_context(nc.psum_tensor(f"at_s{i}", [P, BANK], F32)) for i in range(2)]
        e_bank = [c.enter_context(nc.psum_tensor(f"at_e{i}", [P, 2 * BANK], F32)) for i in range(2)]
        o_bank = [c.enter_context(nc.psum_tensor(f"at_o{i}", [P, BANK], F32)) for i in range(2)]

        NB = 3
        qa = sb("qa", [P, NB, QUAD, N], BF16)
        ka = sb("ka", [P, NB, QUAD, N], BF16)
        ident_bf = sb("ident_bf", [P, P], BF16)
        above = sb("above", [P, P], BF16)
        below = sb("below", [P, P], BF16)
        m = sb("m", [P, NB, QUAD, TB])
        m2 = sb("m2", [P, QUAD, TB // 2, 2])
        mpart = sb("mpart", [QUAD * TB, NB, PARTS, P], BF16)
        mrest = sb("mrest", [QUAD * TB, NB, P])
        vg = sb("vg", [P, NB, TB, QUAD, 32])
        pr = sb("pr", [P, 2, QUAD, N])
        oT = sb("oT", [P, 2, BANK])
        rd = sb("rd", [P, 2, QUAD, QUAD])

        c_in, zero_ok, vg0 = sem("c_in"), sem("zero_ok"), sem("vg0")
        sp_in = [sem(f"sp_in{i}") for i in range(NB)]
        s_ps, s_max = sem("s_ps"), sem("s_max")
        m_ok, mp_ok = sem("m_ok"), sem("mp_ok")
        m_in = [sem(f"m_in{i}") for i in range(NB)]
        e_ps, e_ok, pv_ps = sem("e_ps"), sem("e_ok"), sem("pv_ps")
        o_evac, oT_ps, rd_ok, o_norm, vg_ok = sem("o_evac"), sem("oT_ps"), sem("rd_ok"), sem("o_norm"), sem("vg_ok")

        UNITS = []
        for qb in reversed(range(TB)):
            for j in range(QUAD):
                for lo in range(0, (qb + 1) * P, BANK):
                    UNITS.append((qb, j, lo, min((qb + 1) * P - lo, BANK)))
        MU = len(UNITS) + 1
        ROW1 = 2 * QUAD * 2
        EU = TB * QUAD
        LOADS = 2 * PARTS * PARTS

        block = c.enter_context(nc.Block())

        def load_parts(q, g, p):
            b, hg = g // QUAD, g % QUAD
            need(q, e_ok, EU * (g - 2) + 1)
            for i in range(PARTS):
                for k in range(PARTS):
                    rows = slice((i * PARTS + k) * HD, (i * PARTS + k + 1) * HD)
                    for w, dst, part in ((0, qa, i), (1, ka, k)):
                        src = split_dram[one(b), part, w, bass.ds(hg * QUAD * HD, QUAD * HD), :]
                        q.dma_start(dst[rows, p, :, :], src.rearrange("o (j d) t -> (o d) j t", d=HD)).then_inc(sp_in[p], 16)
            src = a["alibi"].bitcast(BF16)[:, bass.ds(hg * QUAD, QUAD), :]
            q.dma_start(ka[ROW_ALIBI:ROW_ALIBI + PARTS, p, :, :], src).then_inc(sp_in[p], 16)

        PER = LOADS + 1

        @block.sync
        def _(sp):
            sp.dma_start(ident_bf[:], a["ident_bf"].bitcast(BF16)).then_inc(c_in, 16)
            sp.dma_start(above[:], a["above"].bitcast(BF16)).then_inc(c_in, 16)
            sp.dma_start(below[:], a["below"].bitcast(BF16)).then_inc(c_in, 16)
            sp.wait_ge(zero_ok, 2 * NB)
            for p in range(NB):
                sp.dma_start(qa[ROW_ALIBI:ROW_ALIBI + PARTS, p, :, :], a["ones_bf"].bitcast(BF16)).then_inc(c_in, 16)
                sp.dma_start(ka[ROW_MAX:ROWS, p, :, :], a["ones_bf"].bitcast(BF16)).then_inc(c_in, 16)
            sp.wait_ge(c_in, 16 * (3 + 2 * NB))

            def maxima_rows(g, p):
                sp.wait_ge(mp_ok, 4 * (g + 1))
                for part in range(PARTS):
                    sp.dma_start(qa[ROW_MAX + part:ROW_MAX + part + 1, p, :, :].rearrange("o j t -> o (j t)"),
                                 mpart[:, p, part, :]).then_inc(m_in[p], 16)

            for g in range(2):
                load_parts(sp, g, g)
            with sp.Fori(0, (NG - 2) // NB) as i:
                for u in range(NB):
                    maxima_rows(NB * i + u, u)
                    load_parts(sp, NB * i + (u + 2), (u + 2) % NB)
            for g in range(NG - 2, NG):
                maxima_rows(g, g % NB)
            for p in range(NB):
                sp.wait_ge(m_in[p], 16 * PARTS * len(range(p, NG, NB)))

        def turns(eng, body):
            for n in range(2):
                body(n, n % NB)
            with eng.Fori(0, (NG - 2) // NB) as i:
                for u in range(NB):
                    body(NB * i + (2 + u), (2 + u) % NB)
            for n in range(NG, NG + 2):
                body(n, n % NB)

        def has(n, lag):
            return not isinstance(n, int) or 0 <= n - lag < NG

        @block.tensor
        def _(pe):
            pe.wait_ge(c_in, 16 * (3 + 2 * NB))

            def score_unit(g, p, u):
                qb, j, lo, w = UNITS[u]
                k = MU * g + u
                need(pe, s_max, k if u == 0 else k - 1)
                bank = s_bank[u % 2]
                diag = lo + w == (qb + 1) * P
                last = nc.tensor.matmul(bank[:, 0:w], qa[0:ROW_MAX, p, j, qb * P:(qb + 1) * P],
                                        ka[0:ROW_MAX, p, j, lo:lo + w], start=True, stop=not diag)
                if diag:
                    last = nc.tensor.matmul(bank[:, w - P:w], ident_bf[:], above[:], start=False, stop=True)
                last.then_inc(s_ps, 1)

            def exp_unit(g, p, kb, j):
                k = EU * g + kb * QUAD + j
                need(pe, e_ok, k - 1)
                bank = e_bank[j % 2]
                w = N - kb * P
                for lo in range(0, w, BANK):
                    ww = min(BANK, w - lo)
                    last = nc.tensor.matmul(bank[:, lo:lo + ww], ka[0:ROWS, p, j, kb * P:(kb + 1) * P],
                                            qa[0:ROWS, p, j, kb * P + lo:kb * P + lo + ww], start=True, stop=lo > 0)
                    if lo == 0:
                        last = nc.tensor.matmul(bank[:, 0:P], ident_bf[:], below[:], start=False, stop=True)
                last.then_inc(e_ps, 1)

            def values(g, p, kb):
                pe.wait_ge(e_ok, EU * g + (kb + 1) * QUAD)
                for half in range(2):
                    lo = max(kb * P, half * BANK)
                    if lo >= (half + 1) * BANK:
                        continue
                    if kb == 0:
                        need(pe, o_evac, 2 * g - 1 + half)
                    for j in range(QUAD):
                        last = nc.tensor.matmul(
                            o_bank[half][32 * j:32 * (j + 1), lo - half * BANK:BANK],
                            vg[:, p, kb, j, :], pr[:, kb % 2, j, lo - kb * P:(half + 1) * BANK - kb * P],
                            start=(kb == 0), stop=(kb == QUAD * (half + 1) - 1))
                last.then_inc(pv_ps, 1)

            def transpose_out(g, half):
                pe.wait_ge(o_evac, 2 * g + half + 1)
                for n in range(QUAD):
                    last = nc.tensor.transpose(s_bank[half][:, n * P:(n + 1) * P], oT[:, half, n * P:(n + 1) * P], ident[:])
                last.then_inc(oT_ps, 1)

            def body(n, p):
                q = (p - 1) % NB
                for row in range(TB):
                    if has(n, 0):
                        if row == 0:
                            pe.wait_ge(sp_in[p], 16 * PER * (n // NB + 1))
                        for u in (u for u in range(len(UNITS)) if UNITS[u][0] == TB - 1 - row):
                            score_unit(n, p, u)
                    if row == 0 and has(n, 2):
                        values(n - 2, (p - 2) % NB, TB - 1)
                    if has(n, 1):
                        if row == 0:
                            pe.wait_ge(m_in[q], 16 * PARTS * ((n - 1) // NB + 1))
                            pe.wait_ge(vg_ok, n)
                        for j in range(QUAD):
                            exp_unit(n - 1, q, row, j)
                        if row > 0:
                            values(n - 1, q, row - 1)
                    if row == 1 and has(n, 2):
                        pe.wait_ge(s_max, MU * n + ROW1 if has(n, 0) else MU * NG)
                        for half in range(2):
                            transpose_out(n - 2, half)
                        pe.wait_ge(o_norm, 2 * (n - 1))
                if has(n, 0):
                    pe.wait_ge(m_ok, n + 1)
                    pe.wait_ge(s_max, MU * n + len(UNITS))
                    nc.tensor.transpose(s_bank[0][0:QUAD * TB, 0:P], m[:, p, :, :].rearrange("p j k -> p (j k)"),
                                        ident[:]).then_inc(s_ps, 1)

            turns(pe, body)

        @block.vector
        def _(v):
            for g in range(NB):
                nc.vector.memset(qa[:, g, :, :], 0.0).then_inc(zero_ok, 1)
                nc.vector.memset(ka[:, g, :, :], 0.0).then_inc(zero_ok, 1)

            def row_units(n, p, row):
                for k, (qb, j, lo, w) in enumerate(UNITS):
                    if qb != TB - 1 - row:
                        continue
                    v.wait_ge(s_ps, MU * n + k + 1)
                    bank = s_bank[k % 2]
                    dst = m[:, p, j, qb:qb + 1] if qb < QUAD else m2[:, j, qb - QUAD, lo // BANK:lo // BANK + 1]
                    nc.vector.tensor_reduce(dst, bank[:, 0:w], AX.X, ALU.max).then_inc(s_max, 1)

            def minus_maxima(n, p):
                v.wait_ge(s_ps, MU * n + MU)
                mt = s_bank[0][0:QUAD * TB, 0:P]
                nc.vector.tensor_scalar(mpart[:, p, 0, :], mt, -1.0, None, ALU.mult).then_inc(mp_ok, 1)
                v.wait_ge(mp_ok, 4 * n + 1)
                nc.vector.scalar_tensor_tensor(mrest[:, p, :], mt, -1.0, mpart[:, p, 0, :],
                                               ALU.mult, ALU.subtract).then_inc(s_max, 1)
                v.wait_ge(s_max, MU * (n + 1))
                nc.vector.tensor_copy(mpart[:, p, 1, :], mrest[:, p, :]).then_inc(mp_ok, 1)
                v.wait_ge(mp_ok, 4 * n + 2)
                nc.vector.tensor_tensor(mpart[:, p, 2, :], mrest[:, p, :], mpart[:, p, 1, :],
                                        ALU.subtract).then_inc(mp_ok, 2)

            def outputs(g):
                b, hg = g // QUAD, g % QUAD
                for half in range(2):
                    v.wait_ge(oT_ps, 2 * g + half + 1)
                    ot = s_bank[half][:, :].rearrange("p (n j r) -> p n j r", n=QUAD, j=QUAD)
                    nc.vector.reciprocal(rd[:, half, :, :], ot[:, :, :, HD]).then_inc(rd_ok, 1)
                    v.wait_ge(rd_ok, 2 * g + half + 1)
                    dst = o_sb[:, bass.ds(b * TB + half * QUAD, QUAD), bass.ds(hg * QUAD * HD, QUAD * HD)]
                    nc.vector.tensor_tensor(dst.rearrange("p n (j d) -> p n j d", d=HD), ot[:, :, :, 0:HD],
                                            rd[:, half, :, :].unsqueeze(3).broadcast_to([P, QUAD, QUAD, HD]),
                                            ALU.mult).then_inc(o_norm, 1)

            def body(n, p):
                for row in range(TB):
                    if has(n, 0):
                        row_units(n, p, row)
                        if row == QUAD - 1:
                            v.wait_ge(s_max, MU * n + 2 * QUAD * QUAD)
                            nc.vector.tensor_reduce(m[:, p, :, QUAD:TB], m2[:], AX.X, ALU.max).then_inc(m_ok, 1)
                    if row == 1 and has(n, 2):
                        outputs(n - 2)
                if has(n, 0):
                    minus_maxima(n, p)

            turns(v, body)

        @block.scalar
        def _(s):
            def exp_unit(g, p, kb, j):
                s.wait_ge(e_ps, EU * g + kb * QUAD + j + 1)
                need(s, pv_ps, TB * g + kb - 1)
                w = N - kb * P
                nc.scalar.activation(pr[:, kb % 2, j, 0:w], e_bank[j % 2][:, 0:w], ACT.Exp).then_inc(e_ok, 1)

            def evacuate(g, half):
                s.wait_ge(pv_ps, TB * g + (QUAD if half == 0 else TB))
                nc.scalar.copy(oT[:, half, :], o_bank[half][:, :]).then_inc(o_evac, 1)

            def body(n, p):
                if has(n, 2):
                    evacuate(n - 2, 1)
                for row in range(TB):
                    if has(n, 1):
                        for j in range(QUAD):
                            exp_unit(n - 1, p, row, j)
                        if row == QUAD + 1:
                            evacuate(n - 1, 0)

            turns(s, body)

        @block.gpsimd
        def _(g_):
            nc.gpsimd.memset(vg[:], 0.0).then_inc(vg0, 1)
            g_.wait_ge(vg0, 1)
            nc.gpsimd.memset(vg[:, :, :, :, HD:HD + 1], 1.0).then_inc(vg0, 1)
            g_.wait_ge(vg0, 2)

            def body(n, p):
                if has(n, 0):
                    b, hg = n // QUAD, n % QUAD
                    need(g_, pv_ps, TB * (n - 2) + 1)
                    src = v_sb[:, bass.ds(b * TB, TB), bass.ds(hg * QUAD * HD, QUAD * HD)]
                    nc.gpsimd.tensor_copy(vg[:, p, :, :, 0:HD], src.rearrange("p k (j d) -> p k j d", d=HD)).then_inc(vg_ok, 1)

            turns(g_, body)


def layer1_out(nc, a, x_sb, ident, y_sb, o_sb, out):
    with ExitStack() as c:
        def sb(name, shape, dt=F32):
            return c.enter_context(nc.sbuf_tensor("out_" + name, shape, dt))

        def sem(name):
            return c.enter_context(nc.semaphore("out_" + name))

        b_T, b_S = (c.enter_context(nc.psum_tensor(f"out_bank{i}", [P, BANK], F32)) for i in range(2))
        w_p = sb("w_p", [P, D])
        o_s = sb("o_s", [P, 2, D])
        o_T = sb("o_T", [P, 2, P])
        th = sb("th", [P, NT, D])
        sg = sb("sg", [P, 2, D])
        w_in, os_ok, o_Tp, oT_ok, th_ok, g_ok, s_ps, sg_ok, x_ok, stored = (sem(n) for n in (
            "w_in", "os_ok", "o_Tp", "oT_ok", "th_ok", "g_ok", "s_ps", "sg_ok", "x_ok", "stored"))
        out_t = out.rearrange("b (k p) d -> p (b k) d", p=P)
        block = c.enter_context(nc.Block())

        @block.sync
        def _(sp):
            sp.dma_start(w_p[:], a["WpT"]).then_inc(w_in, 16)
            with sp.Fori(0, NT // 4) as i:
                sp.wait_ge(x_ok, 4 * i + 4)
                sp.dma_start(out_t[:, bass.ds(4 * i, 4), :], x_sb[:, bass.ds(4 * i, 4), :]).then_inc(stored, 16)
            sp.wait_ge(stored, 16 * (NT // 4))

        @block.scalar
        def _(s):
            def copy_o(t, p):
                need(s, o_Tp, t - 1)
                nc.scalar.copy(o_s[:, p:p + 1, :], o_sb[:, one(t), :]).then_inc(os_ok, 1)
                nc.scalar.activation(th[:, one(t), :], y_sb[:, one(t), :], ACT.Tanh, scale=0.5).then_inc(th_ok, 1)

            def copy_T(t, p):
                s.wait_ge(o_Tp, t + 1)
                need(s, s_ps, t - 1)
                nc.scalar.copy(o_T[:, p, :], b_T[:, 0:P]).then_inc(oT_ok, 1)

            tile_loop(s, NT, [(0, copy_o), (1, copy_T)])

        @block.tensor
        def _(pe):
            pe.wait_ge(w_in, 16)

            def transpose_o(t, p):
                pe.wait_ge(os_ok, t + 1)
                need(pe, oT_ok, t)
                nc.tensor.transpose(b_T[:, 0:P], o_s[:, p, :], ident[:]).then_inc(o_Tp, 1)

            def project(t, p):
                pe.wait_ge(oT_ok, t + 1)
                need(pe, sg_ok, t)
                nc.tensor.matmul(b_S[:, 0:D], o_T[:, p, :], w_p[:], start=True, stop=True).then_inc(s_ps, 1)

            tile_loop(pe, NT, [(0, transpose_o), (1, project)])

        @block.vector
        def _(v):
            def gate(t, p):
                v.wait_ge(th_ok, t + 1)
                nc.vector.scalar_tensor_tensor(y_sb[:, one(t), :], th[:, one(t), :], 1.0, y_sb[:, one(t), :],
                                               ALU.add, ALU.mult).then_inc(g_ok, 1)

            def finish(t, p):
                v.wait_ge(g_ok, t + 1)
                v.wait_ge(s_ps, t + 1)
                need(v, x_ok, t - 1)
                nc.vector.scalar_tensor_tensor(sg[:, p:p + 1, :], b_S[:, 0:D].unsqueeze(1), 0.5, y_sb[:, one(t), :],
                                               ALU.mult, ALU.mult).then_inc(sg_ok, 1)
                v.wait_ge(sg_ok, t + 1)
                nc.vector.tensor_tensor(x_sb[:, one(t), :], x_sb[:, one(t), :], sg[:, p:p + 1, :], ALU.add).then_inc(x_ok, 1)

            tile_loop(v, NT, [(0, gate), (1, finish)])


def constants():
    import numpy as np

    def bf16(v):
        u = np.ascontiguousarray(v, np.float32).view(np.uint32)
        return ((u + 0x7FFF + ((u >> 16) & 1)) >> 16).astype(np.uint16)

    def value(bits):
        return (bits.astype(np.uint32) << 16).view(np.float32).astype(np.float64)

    head = np.arange(P) // HD
    i, j = np.arange(P)[:, None], np.arange(P)[None, :]
    start = 2.0 ** (-(2.0 ** -1))
    slopes = np.asarray([start * start ** h for h in range(H)], np.float32).astype(np.float64)
    bias = -slopes[:, None] * np.arange(N, dtype=np.float64)[None, :]
    alibi = []
    for _ in range(PARTS):
        alibi.append(bf16(bias))
        bias = bias - value(alibi[-1])
    return {
        "ident": np.eye(P, dtype=np.float32),
        "ident_bf": bf16(np.eye(P)),
        "head_mask": (head[:, None] == np.arange(H)[None, :]).astype(np.float32),
        "above": bf16(np.where(j > i, -1e30, 0.0)),
        "below": bf16(np.where(j < i, -1e30, 0.0)),
        "alibi": np.stack(alibi),
        "ones_bf": bf16(np.ones((PARTS, QUAD, N))),
    }


def layouts(x):
    import numpy as np

    col = lambda v: np.asarray(v).reshape(-1, 1)
    t = lambda v: np.ascontiguousarray(np.asarray(v).T)
    out = {k: np.ascontiguousarray(np.asarray(x[k])) for k in (
        "L0_attn_x", "L0_attn_b_out", "L0_ffn_Wq", "L0_ffn_Wup", "L0_ffn_bq", "L0_ffn_bup", "L0_ffn_Wo",
        "L0_ffn_bo", "L0_ffn_Wg", "L0_ffn_bg", "L0_ffn_We", "L1_attn_Bq", "L1_attn_Bk", "L1_attn_Bv",
        "L1_ffn_b1", "L1_ffn_b2")}
    out.update(w_qkvT=t(x["L0_attn_w_qkv"]), w_outT=t(x["L0_attn_w_out"]), WdownT=t(x["L0_ffn_Wdown"]),
               gamma1=col(x["L0_ffn_gamma1"]), gamma2=col(x["L0_ffn_gamma2"]), bdown=col(x["L0_ffn_bdown"]),
               WqT=t(x["L1_attn_Wq"]), WkT=t(x["L1_attn_Wk"]), WvT=t(x["L1_attn_Wv"]), WpT=t(x["L1_attn_Wp"]),
               AqT=t(x["L1_attn_Aq"]), AkT=t(x["L1_attn_Ak"]), AvT=t(x["L1_attn_Av"]),
               ln1_g=col(x["L1_ffn_ln1_g"]), ln1_b=col(x["L1_ffn_ln1_b"]),
               ln2_g=col(x["L1_ffn_ln2_g"]), ln2_b=col(x["L1_ffn_ln2_b"]),
               w1T=t(x["L1_ffn_w1"]), w2T=t(x["L1_ffn_w2"]))
    return out


def kernel(**inputs):
    import numpy as _np
    import concourse.bacc as _bacc
    from concourse import mybir as _mybir
    from concourse.bass_utils import run_bass_kernel_spmd as _run

    nc = _bacc.Bacc("TRN2", target_bir_lowering=False, num_devices=1)
    arrays, args = {}, {}
    for name, arr in {**layouts(inputs), **constants()}.items():
        arrays[f"in_{name}_dram"] = arr
        args[name] = nc.dram_tensor(f"in_{name}_dram", arr.shape, _mybir.dt.from_np(arr.dtype), kind="ExternalInput").ap()
    out = nc.dram_tensor("out_0_dram", (B, N, D), F32, kind="ExternalOutput").ap()
    mixer_kernel(nc, args, out)
    r = _run(nc, [arrays], core_ids=[0])
    return r.results[0]["out_0_dram"]
```

```python
import concourse.bass as bass
from concourse import mybir
from contextlib import ExitStack

F32 = mybir.dt.float32
BF16 = mybir.dt.bfloat16
ALU = mybir.AluOpType
ACT = mybir.ActivationFunctionType
AX = mybir.AxisListType

B, N, D, H = 2, 1024, 128, 16
HD = D // H
P = 128
NT = B * N // P
TB = N // P
L = 64
E = 8
HID = 512
HC = HID // P
R = 8
QUAD = 4
NG = B * H // QUAD
BANK = 512

PARTS = 3
ROW_ALIBI = PARTS * PARTS * HD
ROW_MAX = 96
ROWS = ROW_MAX + PARTS

LN_EPS = 1e-5
RMS_EPS = 1e-6


def need(eng, sem, n):
    if isinstance(n, int) and n <= 0:
        return
    eng.wait_ge(sem, n)


def upto(n, most=NT):
    return min(n, most) if isinstance(n, int) else n


def one(i):
    return bass.ds(i, 1)


def tile_loop(eng, tiles, stages):
    deepest = max(lag for lag, _ in stages)

    def step(n, parity):
        for lag, stage in stages:
            if isinstance(n, int) and not 0 <= n - lag < tiles:
                continue
            stage(n - lag, (parity + lag) % 2)

    first = deepest + 4
    first += first % 2
    last = first + (tiles - first) // 2 * 2
    for n in range(first):
        step(n, n % 2)
    with eng.Fori(0, (last - first) // 2) as i:
        for u in range(2):
            step(2 * i + (first + u), u)
    for n in range(last, tiles + deepest):
        step(n, n % 2)


def mixer_kernel(nc, a, out):
    with ExitStack() as whole:
        def sb(name, shape, dt=F32, ctx=whole):
            return ctx.enter_context(nc.sbuf_tensor(name, shape, dt))

        x_sb = sb("x_sb", [P, NT, D])
        ident = sb("ident", [P, P])
        split_dram = nc.dram_tensor("split_scratch", [B, PARTS, 2, D, N], BF16, kind="Internal").ap()

        layer0(nc, a, x_sb, ident)
        with ExitStack() as c:
            v_sb = sb("v_sb", [P, NT, D], F32, c)
            y_sb = sb("y_sb", [P, NT, D], F32, c)
            layer1_dense(nc, a, x_sb, ident, v_sb, y_sb, split_dram)
            o_sb = sb("o_sb", [P, NT, D], F32, c)
            layer1_attention(nc, a, ident, v_sb, o_sb, split_dram)
            layer1_out(nc, a, x_sb, ident, y_sb, o_sb, out)


def layer0(nc, a, x_sb, ident):
    with ExitStack() as c:
        def sb(name, shape, dt=F32):
            return c.enter_context(nc.sbuf_tensor("l0_" + name, shape, dt))

        def sem(name):
            return c.enter_context(nc.semaphore("l0_" + name))

        banks = [c.enter_context(nc.psum_tensor(f"l0_bank{i}", [P, BANK], F32)) for i in range(8)]

        w_all = sb("w_all", [P, 6 * D])
        w_out = sb("w_out", [P, D])
        w_o = sb("w_o", [P, D])
        w_e = sb("w_e", [P, E, D])
        w_g = sb("w_g", [P, E])
        w_q = sb("w_q", [P, D])
        w_dT = sb("w_dT", [L, D])
        w_up = sb("w_up", [L, 2 * D])
        gam1 = sb("gam1", [P, 1])
        gam2 = sb("gam2", [P, 1])
        b_down = sb("b_down", [L, 1])
        b_down_rep = sb("b_down_rep", [L, P])
        b_qkv = sb("b_qkv", [P, 3 * D])
        b_out = sb("b_out", [P, D])
        b_o = sb("b_o", [P, D])
        b_g = sb("b_g", [P, E])
        head_mask = sb("head_mask", [P, H])
        half = sb("half", [P, NT])

        st6 = sb("st6", [P, NT, 6])
        mv = sb("mv", [P, NT, 2])
        ve = sb("ve", [P, NT])
        rstd = sb("rstd", [P, NT])
        vr = sb("vr", [P, NT])
        rms1 = sb("rms1", [P, NT])

        xn = sb("xn", [P, NT, D])
        xnb = sb("xnb", [P, NT, D])
        qkv = sb("qkv", [P, NT, 3 * D])
        att = sb("att", [P, 2, H * H])
        rsum = sb("rsum", [P, 2, H])
        ql_T = sb("ql_T", [P, NT, P])
        kv_part = sb("kv_part", [P, NT, D + 1])
        gate = sb("gate", [P, NT, D])
        xs = sb("xs", [P, 2, D])
        xT = sb("xT", [P, 2, P])
        mn = sb("mn", [P, 2, 2 * D])
        ex = sb("ex", [P, 2, 2 * D])
        ql = sb("ql", [P, 2, 2 * D])
        vl = sb("vl", [P, 2, D + 1])
        prod = sb("prod", [P, 2, 2, H * H * HD])
        mx = sb("mx", [P, 2, H])
        o_raw = sb("o_raw", [P, 2, D])
        o_n = sb("o_n", [P, 2, D])
        o_T = sb("o_T", [P, 2, P])
        x2s = sb("x2s", [P, 2, D])
        x2_T = sb("x2_T", [P, 2, P])
        sq = sb("sq", [P, 2, D])
        ss = sb("ss", [P, NT])
        ms = sb("ms", [P, NT])
        rms2 = sb("rms2", [P, NT])
        lg = sb("lg", [P, 2, E])
        nmx = sb("nmx", [P, 2, 1])
        ge = sb("ge", [P, 2, E])
        gs = sb("gs", [P, 2, 1])
        gr = sb("gr", [P, 2, 1])
        gw = sb("gw", [P, 2, E])
        acc = sb("acc", [P, 2, 2, D])
        th = sb("th", [P, 2, D])
        kv_sum = sb("kv_sum", [P, B, D + 1])
        bdks = sb("bdks", [P, B, D + H])
        q_s = sb("q_s", [P, 2, P])
        den = sb("den", [P, 2, H])
        rden = sb("rden", [P, 2, H])
        lin = sb("lin", [P, 2, D])
        lin_T = sb("lin_T", [P, 2, P])
        s_b = sb("s_b", [P, 2, D])
        s_g = sb("s_g", [P, 2, D])

        x_in, w_in = sem("x_in"), sem("w_in")
        prep_ps, prep = sem("prep_ps"), sem("prep")
        stat, pool_pow = sem("stat"), sem("pool_pow")
        xs_ok, xs_T, xT_ok, xs_kept = sem("xs_ok"), sem("xs_T"), sem("xT_ok"), sem("xs_kept")
        projA, projB = sem("projA"), sem("projB")
        mn_ok, ex_ok, ql_ok, vl_ok, qkv_ok = sem("mn_ok"), sem("ex_ok"), sem("ql_ok"), sem("vl_ok"), sem("qkv_ok")
        qlT_kv, qlT_ok = sem("qlT_kv"), sem("qlT_ok")
        xnb_ok = sem("xnb_ok")
        p1_ok, s1_ok, mx_ok, sub_ok, exp_ok, sum_ok, rs_ok = (sem(n) for n in (
            "p1_ok", "s1_ok", "mx_ok", "sub_ok", "exp_ok", "sum_ok", "rs_ok"))
        p2_ok, or_ok, on_ok, on_T, oT_ok, wo_ok, x2_ok = (sem(n) for n in (
            "p2_ok", "or_ok", "on_ok", "on_T", "oT_ok", "wo_ok", "x2_ok"))
        sq_ok, ms_ok, r2_ok, x2_T_ps, x2T_ok, gl_ok, moe_ok = (sem(n) for n in (
            "sq_ok", "ms_ok", "r2_ok", "x2_T_ps", "x2T_ok", "gl_ok", "moe_ok"))
        gv, ge_ok, acc_ok, th_ok, gate_ok = (sem(n) for n in ("gv", "ge_ok", "acc_ok", "th_ok", "gate_ok"))
        kvs = sem("kvs")
        qs_ok, nd_ok, den_ok, rden_ok, lin_ok, lin_T_ps, linT_ok, so_ok, sb_ok, sg_ok, x1_ok = (sem(n) for n in (
            "qs_ok", "nd_ok", "den_ok", "rden_ok", "lin_ok", "lin_T_ps", "linT_ok", "so_ok", "sb_ok", "sg_ok", "x1_ok"))

        W_LOADS = 18
        scale = float(HD) ** -0.5
        v_T, v_A, v_B, v_Q, v_O, v_G, v_M0, v_M1 = banks
        nd_bank, linT_bank, so_bank = (v_A, v_B), (v_T, v_Q), (v_O, v_G)

        block = c.enter_context(nc.Block())

        @block.sync
        def _(sp):
            x_d = a["L0_attn_x"].rearrange("b (k p) d -> p (b k) d", p=P)
            for k in range(4):
                sp.dma_start(x_sb[:, 4 * k:4 * k + 4, :], x_d[:, 4 * k:4 * k + 4, :]).then_inc(x_in, 16)
            for dst, src in (
                (ident[:], a["ident"]), (w_all[:, 0:3 * D], a["w_qkvT"]), (w_q[:], a["L0_ffn_Wq"]),
                (w_dT[:], a["WdownT"]), (w_up[:], a["L0_ffn_Wup"]), (gam1[:], a["gamma1"]),
                (gam2[:], a["gamma2"]), (b_down[:], a["bdown"]),
                (b_qkv[:, 0:D], a["L0_ffn_bq"].partition_broadcast(P)),
                (b_qkv[:, D:3 * D], a["L0_ffn_bup"].partition_broadcast(P)),
                (w_out[:], a["w_outT"]), (w_o[:], a["L0_ffn_Wo"]),
                (w_e[:], a["L0_ffn_We"].rearrange("e d f -> d e f")), (w_g[:], a["L0_ffn_Wg"]),
                (b_out[:], a["L0_attn_b_out"].partition_broadcast(P)),
                (b_o[:], a["L0_ffn_bo"].partition_broadcast(P)),
                (b_g[:], a["L0_ffn_bg"].partition_broadcast(P)), (head_mask[:], a["head_mask"]),
            ):
                sp.dma_start(dst, src).then_inc(w_in, 16)

        @block.vector
        def _(v):
            nc.vector.memset(half[:], -0.5).then_inc(prep, 1)
            nc.vector.memset(vl[:, :, D:D + 1], 1.0).then_inc(prep, 1)

            v.wait_ge(x_in, 16 * 4)
            with v.Fori(0, NT) as t:
                nc.vector.bn_stats(st6[:, one(t), :], x_sb[:, one(t), :]).then_inc(stat, 1)
            v.wait_ge(stat, NT)
            for t in range(NT):
                nc.vector.bn_aggr(mv[:, t, :], st6[:, t, :]).then_inc(stat, 1)
            v.wait_ge(stat, 2 * NT)
            nc.vector.tensor_scalar(ve[:], mv[:, :, 1], LN_EPS, None, ALU.add).then_inc(stat, 1)

            v.wait_ge(w_in, 16 * W_LOADS)
            nc.vector.tensor_copy(b_down_rep[:], b_down[:].broadcast_to([L, P])).then_inc(prep, 1)
            nc.vector.tensor_scalar(w_all[:, 3 * D:4 * D], w_q[:], gam1[:], scale, ALU.mult, ALU.mult).then_inc(prep, 1)
            nc.vector.tensor_scalar(w_g[:], w_g[:], gam2[:], None, ALU.mult).then_inc(prep, 1)
            nc.vector.tensor_scalar(w_e[:], w_e[:], gam2[:], None, ALU.mult).then_inc(prep, 1)
            nc.vector.tensor_scalar(b_qkv[:, 0:D], b_qkv[:, 0:D], scale, None, ALU.mult).then_inc(prep, 1)
            v.wait_ge(prep_ps, 1)
            nc.vector.tensor_scalar(w_all[:, 4 * D:6 * D], v_A[:, 0:2 * D], gam1[:], None, ALU.mult).then_inc(prep, 1)
            v.wait_ge(prep_ps, 2)
            nc.vector.tensor_tensor(b_qkv[:, D:3 * D], v_B[:, 0:2 * D], b_qkv[:, D:3 * D], ALU.add).then_inc(prep, 1)

            v.wait_ge(pool_pow, 1)
            nc.vector.tensor_tensor(vr[:], rstd[:], rstd[:], ALU.mult).then_inc(stat, 1)
            v.wait_ge(stat, 2 * NT + 2)
            nc.vector.tensor_tensor(vr[:], vr[:], mv[:, :, 1], ALU.mult).then_inc(stat, 1)
            v.wait_ge(stat, 2 * NT + 3)
            nc.vector.tensor_scalar(vr[:], vr[:], RMS_EPS, None, ALU.add).then_inc(stat, 1)
            v.wait_ge(pool_pow, 2)

            def normalise(t, p):
                need(v, xs_kept, t - 1)
                need(v, xs_T, t - 1)
                nc.vector.tensor_scalar(xs[:, p, :], x_sb[:, one(t), :], mv[:, one(t), 0], rstd[:, one(t)],
                                        ALU.subtract, ALU.mult).then_inc(xs_ok, 1)

            def elu_min(t, p):
                v.wait_ge(projA, t + 1)
                need(v, ex_ok, t - 1)
                nc.vector.tensor_scalar(mn[:, p, :], v_A[:, 0:2 * D], 0.0, None, ALU.min).then_inc(mn_ok, 1)

            def elu_sum(t, p):
                v.wait_ge(ex_ok, t + 1)
                need(v, qlT_kv, t - 1)
                nc.vector.scalar_tensor_tensor(ql[:, p, :], v_A[:, 0:2 * D], 0.0, ex[:, p, :],
                                               ALU.max, ALU.add).then_inc(ql_ok, 1)

            def token_qkv(t, p):
                v.wait_ge(projB, t + 1)
                nc.vector.scalar_tensor_tensor(qkv[:, one(t), :], v_B[:, 0:3 * D], rms1[:, one(t)], b_qkv[:],
                                               ALU.mult, ALU.add).then_inc(qkv_ok, 1)

            def scores(t, p):
                v.wait_ge(p1_ok, t + 1)
                need(v, p2_ok, t - 1)
                nc.vector.tensor_reduce(att[:, p, :], prod[:, p, 0, :].rearrange("p (s d) -> p s d", d=HD),
                                        AX.X, ALU.add).then_inc(s1_ok, 1)
                v.wait_ge(s1_ok, t + 1)
                need(v, sub_ok, t - 1)
                at = att[:, p, :].rearrange("p (h g) -> p h g", g=H)
                nc.vector.tensor_reduce(mx[:, p, :], at, AX.X, ALU.max).then_inc(mx_ok, 1)
                v.wait_ge(mx_ok, t + 1)
                nc.vector.tensor_tensor(at, at, mx[:, p, :].unsqueeze(2).broadcast_to([P, H, H]),
                                        ALU.subtract).then_inc(sub_ok, 1)

            def sums(t, p):
                v.wait_ge(exp_ok, t + 1)
                nc.vector.tensor_reduce(rsum[:, p, :], att[:, p, :].rearrange("p (h g) -> p h g", g=H),
                                        AX.X, ALU.add).then_inc(sum_ok, 1)
                v.wait_ge(sum_ok, t + 1)
                nc.vector.reciprocal(rsum[:, p, :], rsum[:, p, :]).then_inc(rs_ok, 1)

            def weighted(t, p):
                v.wait_ge(p2_ok, t + 1)
                nc.vector.tensor_reduce(o_raw[:, p, :], prod[:, p, 1, :].rearrange("p (s g) -> p s g", g=H),
                                        AX.X, ALU.add).then_inc(or_ok, 1)
                v.wait_ge(or_ok, t + 1)
                v.wait_ge(rs_ok, t + 1)
                need(v, on_T, t - 1)
                nc.vector.tensor_tensor(o_n[:, p, :].rearrange("p (h d) -> p h d", d=HD),
                                        o_raw[:, p, :].rearrange("p (h d) -> p h d", d=HD),
                                        rsum[:, p, :].unsqueeze(2).broadcast_to([P, H, HD]),
                                        ALU.mult).then_inc(on_ok, 1)

            def residual(t, p):
                v.wait_ge(wo_ok, t + 1)
                v.wait_ge(xnb_ok, t + 1)
                need(v, x2_T_ps, t - 1)
                need(v, sq_ok, t - 1)
                nc.vector.tensor_tensor(x2s[:, p, :], v_O[:, P:2 * P], xnb[:, one(t), :].rearrange("p o d -> p (o d)"),
                                        ALU.add).then_inc(x2_ok, 1)

            def mean_square(t, p):
                v.wait_ge(sq_ok, t + 1)
                nc.vector.tensor_scalar(ms[:, one(t)], ss[:, one(t)], 1.0 / D, RMS_EPS, ALU.mult, ALU.add).then_inc(ms_ok, 1)

            def gate_logits(t, p):
                v.wait_ge(gl_ok, t + 1)
                v.wait_ge(r2_ok, t + 1)
                nc.vector.scalar_tensor_tensor(lg[:, p, :], v_G[:, 0:E], rms2[:, one(t)], b_g[:],
                                               ALU.mult, ALU.add).then_inc(gv, 1)
                v.wait_ge(gv, 4 * t + 1)
                nc.vector.tensor_reduce(nmx[:, p, :], lg[:, p, :], AX.X, ALU.max, negate=True).then_inc(gv, 1)

            def experts(t, p):
                v.wait_ge(ge_ok, t + 1)
                nc.vector.reciprocal(gr[:, p, :], gs[:, p, :]).then_inc(gv, 1)
                v.wait_ge(gv, 4 * t + 3)
                nc.vector.tensor_scalar(gw[:, p, :], ge[:, p, :], gr[:, p, :], rms2[:, one(t)],
                                        ALU.mult, ALU.mult).then_inc(gv, 1)
                v.wait_ge(gv, 4 * t + 4)
                v.wait_ge(moe_ok, t + 1)
                need(v, th_ok, t - 1)
                for e in range(E):
                    bank = (v_M0, v_M1)[e // 4]
                    before = x2s[:, p, :] if e == 0 else acc[:, p, (e - 1) % 2, :]
                    nc.vector.scalar_tensor_tensor(acc[:, p, e % 2, :], bank[:, e % 4 * D:(e % 4 + 1) * D],
                                                   gw[:, p, e:e + 1], before, ALU.mult, ALU.add).then_inc(acc_ok, 1)
                    v.wait_ge(acc_ok, E * t + e + 1)

            def silu(t, p):
                v.wait_ge(th_ok, t + 1)
                nc.vector.scalar_tensor_tensor(gate[:, one(t), :], th[:, p:p + 1, :], 1.0, acc[:, p:p + 1, (E - 1) % 2, :],
                                               ALU.add, ALU.mult).then_inc(gate_ok, 1)

            tile_loop(v, NT, [(0, normalise), (3, scores), (1, elu_min), (7, gate_logits), (6, residual),
                              (1, elu_sum), (1, token_qkv), (5, weighted), (6, mean_square), (4, sums),
                              (7, experts), (7, silu)])

            v.wait_ge(qlT_ok, 2 * NT)
            for b in range(B):
                nc.vector.tensor_reduce(kv_sum[:, b, :], kv_part[:, b * TB:(b + 1) * TB, :].rearrange("p k n -> p n k"),
                                        AX.X, ALU.add).then_inc(kvs, 1)
            v.wait_ge(kvs, B)
            for b in range(B):
                nc.vector.tensor_tensor(bdks[:, b, 0:D].rearrange("p (h m) -> p h m", m=HD),
                                        kv_sum[:, b, 0:D].rearrange("p (h m) -> p h m", m=HD),
                                        head_mask[:].unsqueeze(2).broadcast_to([P, H, HD]), ALU.mult).then_inc(kvs, 1)
                nc.vector.tensor_scalar(bdks[:, b, D:D + H], head_mask[:], kv_sum[:, b, D:D + 1], None,
                                        ALU.mult).then_inc(kvs, 1)

            def denominators(t, p):
                v.wait_ge(nd_ok, t + 1)
                nc.vector.tensor_scalar(den[:, p, :], nd_bank[p][:, D:D + H], 1e-6, None, ALU.add).then_inc(den_ok, 1)
                v.wait_ge(den_ok, t + 1)
                nc.vector.reciprocal(rden[:, p, :], den[:, p, :]).then_inc(rden_ok, 1)
                v.wait_ge(rden_ok, t + 1)
                need(v, lin_T_ps, t - 1)
                nc.vector.tensor_tensor(lin[:, p, :].rearrange("p (h m) -> p h m", m=HD),
                                        nd_bank[p][:, 0:D].rearrange("p (h m) -> p h m", m=HD),
                                        rden[:, p, :].unsqueeze(2).broadcast_to([P, H, HD]), ALU.mult).then_inc(lin_ok, 1)

            def gated(t, p):
                v.wait_ge(so_ok, t + 1)
                v.wait_ge(gate_ok, NT)
                nc.vector.tensor_tensor(s_b[:, p, :], so_bank[p][:, 0:D], b_out[:], ALU.add).then_inc(sb_ok, 1)
                v.wait_ge(sb_ok, t + 1)
                nc.vector.scalar_tensor_tensor(s_g[:, p:p + 1, :], s_b[:, p:p + 1, :], 0.5, gate[:, one(t), :],
                                               ALU.mult, ALU.mult).then_inc(sg_ok, 1)
                v.wait_ge(sg_ok, t + 1)
                nc.vector.tensor_tensor(x_sb[:, one(t), :], x_sb[:, one(t), :], s_g[:, p:p + 1, :], ALU.add).then_inc(x1_ok, 1)

            tile_loop(v, NT, [(0, denominators), (3, gated)])

        @block.tensor
        def _(pe):
            pe.wait_ge(w_in, 16 * W_LOADS)
            nc.tensor.matmul(v_A[:, 0:2 * D], w_dT[:], w_up[:], start=True, stop=True).then_inc(prep_ps, 1)
            pe.wait_ge(prep, 3)
            nc.tensor.matmul(v_B[:, 0:2 * D], b_down_rep[:], w_up[:], start=True, stop=True).then_inc(prep_ps, 1)
            pe.wait_ge(prep, 9)

            def transpose_x(t, p):
                pe.wait_ge(xs_ok, t + 1)
                need(pe, xT_ok, t)
                need(pe, oT_ok, t - 5)
                nc.tensor.transpose(v_T[:, 0:P], xs[:, p, :], ident[:]).then_inc(xs_T, 1)

            def project(t, p):
                pe.wait_ge(xT_ok, t + 1)
                need(pe, ql_ok, t)
                need(pe, vl_ok, t)
                nc.tensor.matmul(v_A[:, 0:3 * D], xT[:, p, :], w_all[:, 0:3 * D], start=True, stop=True).then_inc(projA, 1)
                need(pe, qkv_ok, t)
                nc.tensor.matmul(v_B[:, 0:3 * D], xT[:, p, :], w_all[:, 3 * D:6 * D], start=True, stop=True).then_inc(projB, 1)

            def linear_kv(t, p):
                pe.wait_ge(ql_ok, t + 1)
                pe.wait_ge(vl_ok, t + 1)
                need(pe, qlT_ok, 2 * t)
                need(pe, x2T_ok, t - 4)
                nc.tensor.transpose(v_Q[:, 0:P], ql[:, p, 0:D], ident[:])
                nc.tensor.matmul(v_Q[:, P:P + D + 1], ql[:, p, D:2 * D], vl[:, p, :], start=True, stop=True).then_inc(qlT_kv, 1)

            def transpose_o(t, p):
                pe.wait_ge(on_ok, t + 1)
                need(pe, xT_ok, upto(t + 6))
                need(pe, oT_ok, t)
                nc.tensor.transpose(v_T[:, P:2 * P], o_n[:, p, :], ident[:]).then_inc(on_T, 1)

            def project_o(t, p):
                pe.wait_ge(oT_ok, t + 1)
                need(pe, x2_ok, t)
                nc.tensor.matmul(v_O[:, P:2 * P], o_T[:, p, :], w_o[:], start=True, stop=True).then_inc(wo_ok, 1)

            def transpose_x2(t, p):
                pe.wait_ge(x2_ok, t + 1)
                need(pe, x2T_ok, t)
                need(pe, qlT_ok, 2 * upto(t + 5))
                nc.tensor.transpose(v_Q[:, 3 * P:4 * P], x2s[:, p, :], ident[:]).then_inc(x2_T_ps, 1)

            def expert_products(t, p):
                pe.wait_ge(x2T_ok, t + 1)
                need(pe, gv, 4 * t)
                need(pe, acc_ok, E * t)
                nc.tensor.matmul(v_G[:, 0:E], x2_T[:, p, :], w_g[:], start=True, stop=True).then_inc(gl_ok, 1)
                for m, bank in enumerate((v_M0, v_M1)):
                    last = nc.tensor.matmul(bank[:, :], x2_T[:, p, :],
                                            w_e[:, 4 * m:4 * m + 4, :].rearrange("p e f -> p (e f)"), start=True, stop=True)
                last.then_inc(moe_ok, 1)

            tile_loop(pe, NT, [(7, expert_products), (0, transpose_x), (1, project), (6, transpose_x2),
                               (1, linear_kv), (5, transpose_o), (5, project_o)])

            pe.wait_ge(kvs, 3 * B)
            pe.wait_ge(x2T_ok, NT)

            def transpose_lin(t, p):
                pe.wait_ge(lin_ok, t + 1)
                need(pe, linT_ok, t - 1)
                nc.tensor.transpose(linT_bank[p][:, 0:P], lin[:, p, :], ident[:]).then_inc(lin_T_ps, 1)

            def project_lin(t, p):
                pe.wait_ge(linT_ok, t + 1)
                need(pe, sb_ok, t - 1)
                nc.tensor.matmul(so_bank[p][:, 0:D], lin_T[:, p, :], w_out[:], start=True, stop=True).then_inc(so_ok, 1)

            def nd(t, p):
                pe.wait_ge(qs_ok, t + 1)
                need(pe, lin_ok, t - 1)
                nc.tensor.matmul(nd_bank[p][:, 0:D + H], q_s[:, p, :], bdks[:, one(t // TB), :], start=True, stop=True).then_inc(nd_ok, 1)

            tile_loop(pe, NT, [(0, nd), (1, transpose_lin), (2, project_lin)])

        @block.scalar
        def _(s):
            def copies_x(t, p):
                s.wait_ge(xs_T, t + 1)
                need(s, projB, t - 1)
                nc.scalar.copy(xT[:, p, :], v_T[:, 0:P]).then_inc(xT_ok, 1)
                nc.scalar.copy(xn[:, one(t), :], xs[:, p:p + 1, :]).then_inc(xs_kept, 1)

            def exps(t, p):
                s.wait_ge(mn_ok, t + 1)
                need(s, ql_ok, t - 1)
                nc.scalar.activation(ex[:, p, :], mn[:, p, :], ACT.Exp).then_inc(ex_ok, 1)
                need(s, qlT_kv, t - 1)
                s.wait_ge(ql_ok, t + 1)
                nc.scalar.copy(vl[:, p, 0:D], v_A[:, 2 * D:3 * D]).then_inc(vl_ok, 1)

            def keep_linear(t, p):
                s.wait_ge(qlT_kv, t + 1)
                nc.scalar.copy(ql_T[:, one(t), :], v_Q[:, 0:P]).then_inc(qlT_ok, 1)
                nc.scalar.copy(kv_part[:, one(t), :], v_Q[:, P:P + D + 1]).then_inc(qlT_ok, 1)

            def softmax_exp(t, p):
                s.wait_ge(sub_ok, t + 1)
                nc.scalar.activation(att[:, p, :], att[:, p, :], ACT.Exp).then_inc(exp_ok, 1)

            def copy_oT(t, p):
                s.wait_ge(on_T, t + 1)
                need(s, wo_ok, t - 1)
                nc.scalar.copy(o_T[:, p, :], v_T[:, P:2 * P]).then_inc(oT_ok, 1)

            def square_x2(t, p):
                s.wait_ge(x2_ok, t + 1)
                need(s, sq_ok, t - 1)
                nc.scalar.activation(sq[:, p, :], x2s[:, p, :], ACT.Square, accum_out=ss[:, one(t)]).then_inc(sq_ok, 1)
                s.wait_ge(x2_T_ps, t + 1)
                need(s, moe_ok, t - 1)
                nc.scalar.copy(x2_T[:, p, :], v_Q[:, 3 * P:4 * P]).then_inc(x2T_ok, 1)

            def gate_exp(t, p):
                s.wait_ge(gv, 4 * t + 2)
                nc.scalar.activation(ge[:, p, :], lg[:, p, :], ACT.Exp, bias=nmx[:, p, :],
                                     accum_out=gs[:, p, :]).then_inc(ge_ok, 1)

            def gate_tanh(t, p):
                s.wait_ge(acc_ok, E * t + E)
                need(s, gate_ok, t - 1)
                nc.scalar.activation(th[:, p, :], acc[:, p, (E - 1) % 2, :], ACT.Tanh, scale=0.5).then_inc(th_ok, 1)

            tile_loop(s, NT, [(0, copies_x), (3, softmax_exp), (1, exps), (7, gate_exp), (6, square_x2),
                              (1, keep_linear), (5, copy_oT), (7, gate_tanh)])

            def copy_q(t, p):
                need(s, nd_ok, t - 1)
                nc.scalar.copy(q_s[:, p:p + 1, :], ql_T[:, one(t), :]).then_inc(qs_ok, 1)

            def copy_linT(t, p):
                s.wait_ge(lin_T_ps, t + 1)
                need(s, so_ok, t - 1)
                nc.scalar.copy(lin_T[:, p, :], linT_bank[p][:, 0:P]).then_inc(linT_ok, 1)

            s.wait_ge(qlT_ok, 2 * NT)
            tile_loop(s, NT, [(0, copy_q), (1, copy_linT)])

        @block.gpsimd
        def _(g):
            g.wait_ge(prep, 1)
            g.wait_ge(stat, 2 * NT + 1)
            nc.gpsimd.tensor_tensor(rstd[:], ve[:], half[:], ALU.pow).then_inc(pool_pow, 1)
            g.wait_ge(stat, 2 * NT + 4)
            nc.gpsimd.tensor_tensor(rms1[:], vr[:], half[:], ALU.pow).then_inc(pool_pow, 1)

            def products_qk(t, p):
                g.wait_ge(qkv_ok, t + 1)
                need(g, s1_ok, t - 1)
                q = qkv[:, one(t), 0:D].rearrange("p o (h d) -> p (o h) d", d=HD)
                k = qkv[:, one(t), D:3 * D].rearrange("p o (h d) -> p (o h) d", d=2 * HD)[:, :, 0:HD]
                nc.gpsimd.tensor_tensor(prod[:, p, 0, :].rearrange("p (h g d) -> p h g d", g=H, d=HD),
                                        q.unsqueeze(2).broadcast_to([P, H, H, HD]),
                                        k.unsqueeze(1).broadcast_to([P, H, H, HD]), ALU.mult).then_inc(p1_ok, 1)

            def products_av(t, p):
                g.wait_ge(exp_ok, t + 1)
                need(g, or_ok, t - 1)
                w = att[:, p, :].rearrange("p (h g) -> p h g", g=H)
                val = qkv[:, one(t), D:3 * D].rearrange("p o (h d) -> p (o h) d", d=2 * HD)[:, :, HD:2 * HD]
                nc.gpsimd.tensor_tensor(prod[:, p, 1, :].rearrange("p (h d g) -> p h d g", g=H, d=HD),
                                        w.unsqueeze(2).broadcast_to([P, H, HD, H]),
                                        val.rearrange("p g d -> p d g").unsqueeze(1).broadcast_to([P, H, HD, H]),
                                        ALU.mult).then_inc(p2_ok, 1)

            def add_bias(t, p):
                g.wait_ge(xs_kept, t + 1)
                nc.gpsimd.tensor_tensor(xnb[:, one(t), :], xn[:, one(t), :], b_o[:].unsqueeze(1), ALU.add).then_inc(xnb_ok, 1)

            def rms_x2(t, p):
                g.wait_ge(ms_ok, t + 1)
                nc.gpsimd.tensor_tensor(rms2[:, one(t)], ms[:, one(t)], half[:, 0:1], ALU.pow).then_inc(r2_ok, 1)

            tile_loop(g, NT, [(7, rms_x2), (2, products_qk), (0, add_bias), (4, products_av)])


def layer1_dense(nc, a, x_sb, ident, v_sb, y_sb, split_dram):
    with ExitStack() as c:
        def sb(name, shape, dt=F32):
            return c.enter_context(nc.sbuf_tensor("l1_" + name, shape, dt))

        def sem(name):
            return c.enter_context(nc.semaphore("l1_" + name))

        banks = [c.enter_context(nc.psum_tensor(f"l1_bank{i}", [P, BANK], F32)) for i in range(8)]
        k_T, k_Y = banks[0:2]
        k_QKV, k_H, k_T4 = banks[2:4], banks[4:6], banks[6:8]

        w_qkv = sb("w_qkv", [P, 3, D])
        lora_b = sb("lora_b", [R, 3, D])
        lora_aT = sb("lora_aT", [R, 3, D])
        w1 = sb("w1", [P, HID])
        w2 = sb("w2", [P, HC, D])
        tern = sb("tern", [P, 2, HID])
        w1g = sb("w1g", [P, HID])
        w2g = sb("w2g", [P, HC, D])
        g1 = sb("g1", [P, 1])
        be1 = sb("be1", [P, 1])
        g2 = sb("g2", [P, HC])
        be2 = sb("be2", [P, HC])
        be1_rep = sb("be1_rep", [P, P])
        be2_rep = sb("be2_rep", [P, HC, P])
        b1 = sb("b1", [P, HID])
        b2 = sb("b2", [P, D])
        asum = sb("asum", [P, 2])
        mean = sb("mean", [P, 2])
        inv = sb("inv", [P, 2])
        ones = sb("ones", [P, P])
        half = sb("half", [P, NT])
        st6 = sb("st6", [P, NT, 6])
        mv = sb("mv", [P, NT, 2])
        ve = sb("ve", [P, NT])
        rstd = sb("rstd", [P, NT])
        vr = sb("vr", [P, NT])
        rln1 = sb("rln1", [P, NT])
        h = sb("h", [P, NT, HID])
        hst6 = sb("hst6", [P, 2, 6])
        hmv = sb("hmv", [P, 2, 2])
        hve = sb("hve", [P, 2])
        hrstd = sb("hrstd", [P, 2])
        parts = sb("parts", [P, PARTS, 2, NT, P], BF16)
        xs = sb("xs", [P, 2, D])
        xT = sb("xT", [P, 2, P])
        rest = sb("rest", [P, 2, 2 * P])
        hn = sb("hn", [P, 2, HID])
        hT = sb("hT", [P, 2, HID])

        w_in, prep, prep_ps, stat, pool_pow = (sem(n) for n in ("w_in", "prep", "prep_ps", "stat", "pool_pow"))
        xs_ok, xs_T, xT_ok, qkv_ps, ph_ok, r_h = (sem(n) for n in ("xs_ok", "xs_T", "xT_ok", "qkv_ps", "ph_ok", "r_h"))
        part1, rest1, part2, part3, v_ok = (sem(n) for n in ("part1", "rest1", "part2", "part3", "v_ok"))
        h_ok, gelu_ok, hst, hn_ok, hn_T, hT_ok, y_ps, y_ok = (sem(n) for n in (
            "h_ok", "gelu_ok", "hst", "hn_ok", "hn_T", "hT_ok", "y_ps", "y_ok"))
        stored = sem("stored")

        block = c.enter_context(nc.Block())
        loads = []
        for n, k in enumerate("qkv"):
            loads += [(w_qkv[:, n, :], a[f"W{k}T"]), (lora_b[:, n, :], a[f"L1_attn_B{k}"]), (lora_aT[:, n, :], a[f"A{k}T"])]
        loads += [(w1[:], a["w1T"]), (w2[:], a["w2T"].rearrange("(c p) n -> p c n", p=P)),
                  (g1[:], a["ln1_g"]), (be1[:], a["ln1_b"]),
                  (g2[:], a["ln2_g"].rearrange("(c p) o -> p (c o)", p=P)),
                  (be2[:], a["ln2_b"].rearrange("(c p) o -> p (c o)", p=P)),
                  (b1[:], a["L1_ffn_b1"].partition_broadcast(P)), (b2[:], a["L1_ffn_b2"].partition_broadcast(P))]
        W_LOADS = len(loads)

        @block.sync
        def _(sp):
            for dst, src in loads:
                sp.dma_start(dst, src, allow_slow_non_contiguous=True).then_inc(w_in, 16)
            for b in range(B):
                for part in range(PARTS):
                    sp.wait_ge((part1, part2, part3)[part], (b + 1) * TB)
                    for w in range(2):
                        sp.dma_start(split_dram[b, part, w, :, :],
                                     parts[:, part, w, b * TB:(b + 1) * TB, :].rearrange("p k t -> p (k t)")).then_inc(stored, 16)
            sp.wait_ge(stored, 16 * B * PARTS * 2)

        @block.vector
        def _(v):
            count = [0]

            def then(ins):
                count[0] += 1
                ins.then_inc(prep, 1)
                v.wait_ge(prep, count[0])

            then(nc.vector.memset(half[:], -0.5))
            then(nc.vector.memset(ones[:], 1.0))
            with v.Fori(0, NT) as t:
                nc.vector.bn_stats(st6[:, one(t), :], x_sb[:, one(t), :]).then_inc(stat, 1)
            v.wait_ge(stat, NT)
            for t in range(NT):
                nc.vector.bn_aggr(mv[:, t, :], st6[:, t, :]).then_inc(stat, 1)
            v.wait_ge(stat, 2 * NT)
            nc.vector.tensor_scalar(ve[:], mv[:, :, 1], LN_EPS, None, ALU.add).then_inc(stat, 1)
            v.wait_ge(w_in, 16 * W_LOADS)
            w2f = w2[:].rearrange("p c n -> p (c n)")
            then(nc.vector.tensor_reduce(asum[:, 0:1], w1[:], AX.X, ALU.add, apply_absolute_value=True))
            then(nc.vector.tensor_reduce(asum[:, 1:2], w2f, AX.X, ALU.add, apply_absolute_value=True))
            v.wait_ge(prep_ps, 1)
            then(nc.vector.tensor_scalar(mean[:], k_T[:, 0:2], 1.0 / (D * HID), 1e-5, ALU.mult, ALU.max))
            then(nc.vector.reciprocal(inv[:], mean[:]))
            for n, w in enumerate((w1[:], w2f)):
                then(nc.vector.tensor_scalar(tern[:, 0, :], w, inv[:, n:n + 1], 0.5, ALU.mult, ALU.is_gt))
                then(nc.vector.tensor_scalar(tern[:, 1, :], w, inv[:, n:n + 1], -0.5, ALU.mult, ALU.is_lt))
                then(nc.vector.tensor_tensor(tern[:, 0, :], tern[:, 0, :], tern[:, 1, :], ALU.subtract))
                then(nc.vector.tensor_scalar(w, tern[:, 0, :], mean[:, n:n + 1], None, ALU.mult))
            then(nc.vector.tensor_scalar(w1g[:], w1[:], g1[:], None, ALU.mult))
            then(nc.vector.tensor_tensor(w2g[:], w2[:], g2[:].unsqueeze(2).broadcast_to([P, HC, D]), ALU.mult))
            then(nc.vector.tensor_copy(be1_rep[:], be1[:].broadcast_to([P, P])))
            then(nc.vector.tensor_copy(be2_rep[:], be2[:].unsqueeze(2).broadcast_to([P, HC, P])))
            v.wait_ge(prep_ps, 2)
            then(nc.vector.scalar_tensor_tensor(w_qkv[:].rearrange("p n d -> p (n d)"), k_QKV[0][:, 0:3 * D], 2.0,
                                                w_qkv[:].rearrange("p n d -> p (n d)"), ALU.mult, ALU.add))
            then(nc.vector.tensor_scalar(w_qkv[:, 0, :], w_qkv[:, 0, :], float(HD) ** -0.5, None, ALU.mult))
            v.wait_ge(prep_ps, 4)
            then(nc.vector.tensor_tensor(b1[:], k_H[0][:, :], b1[:], ALU.add))
            then(nc.vector.tensor_tensor(b2[:], k_Y[:, 0:D], b2[:], ALU.add))

            v.wait_ge(pool_pow, 1)
            nc.vector.tensor_tensor(vr[:], rstd[:], rstd[:], ALU.mult).then_inc(stat, 1)
            v.wait_ge(stat, 2 * NT + 2)
            nc.vector.tensor_tensor(vr[:], vr[:], mv[:, :, 1], ALU.mult).then_inc(stat, 1)
            v.wait_ge(stat, 2 * NT + 3)
            nc.vector.tensor_scalar(vr[:], vr[:], LN_EPS, None, ALU.add).then_inc(stat, 1)
            v.wait_ge(pool_pow, 2)

            def normalise(t, p):
                need(v, xs_T, t - 1)
                nc.vector.tensor_scalar(xs[:, p:p + 1, :], x_sb[:, one(t), :], mv[:, one(t), 0], rstd[:, one(t)],
                                        ALU.subtract, ALU.mult).then_inc(xs_ok, 1)

            def hidden(t, p):
                v.wait_ge(ph_ok, t + 1)
                nc.vector.scalar_tensor_tensor(h[:, one(t), :], k_H[p][:, :], rln1[:, one(t)], b1[:],
                                               ALU.mult, ALU.add).then_inc(h_ok, 1)

            def first_rest(t, p):
                v.wait_ge(part1, t + 1)
                need(v, part2, t - 1)
                nc.vector.tensor_tensor(rest[:, p, :], k_QKV[p][:, 0:2 * P],
                                        parts[:, 0, :, one(t), :].rearrange("p w o t -> p w (o t)"), ALU.subtract).then_inc(rest1, 1)

            def last_part(t, p):
                v.wait_ge(part2, t + 1)
                nc.vector.tensor_tensor(parts[:, 2, :, one(t), :].rearrange("p w o t -> p w (o t)"),
                                        rest[:, p, :].rearrange("p (w t) -> p w t", w=2),
                                        parts[:, 1, :, one(t), :].rearrange("p w o t -> p w (o t)"), ALU.subtract).then_inc(part3, 1)

            def hidden_stats(t, p):
                v.wait_ge(gelu_ok, t + 1)
                nc.vector.bn_stats(hst6[:, p, :], h[:, one(t), :]).then_inc(hst, 1)

            def stats_in(t, p):
                v.wait_ge(hst, 3 * t + 1)

            def hidden_moments(t, p):
                nc.vector.bn_aggr(hmv[:, p, :], hst6[:, p, :]).then_inc(hst, 1)

            def hidden_variance(t, p):
                v.wait_ge(hst, 3 * t + 2)
                nc.vector.tensor_scalar(hve[:, p:p + 1], hmv[:, p, 1:2], LN_EPS, None, ALU.add).then_inc(hst, 1)

            def normalise_hidden(t, p):
                v.wait_ge(r_h, t + 1)
                need(v, hn_T, t - 1)
                nc.vector.tensor_scalar(hn[:, p:p + 1, :], h[:, one(t), :], hmv[:, p, 0:1], hrstd[:, p:p + 1],
                                        ALU.subtract, ALU.mult).then_inc(hn_ok, 1)

            def keep_y(t, p):
                v.wait_ge(y_ps, t + 1)
                nc.vector.tensor_tensor(y_sb[:, one(t), :], k_Y[:, 0:D].unsqueeze(1), b2[:].unsqueeze(1), ALU.add).then_inc(y_ok, 1)

            tile_loop(v, NT, [(4, normalise_hidden), (0, normalise), (3, hidden_stats), (6, keep_y),
                              (3, stats_in), (2, last_part), (3, hidden_moments), (3, hidden_variance), (1, hidden), (1, first_rest)])

        @block.tensor
        def _(pe):
            pe.wait_ge(prep, 4)
            nc.tensor.matmul(k_T[:, 0:2], ones[:], asum[:], start=True, stop=True).then_inc(prep_ps, 1)
            for n in range(3):
                last = nc.tensor.matmul(k_QKV[0][:, n * D:(n + 1) * D], lora_b[:, n, :], lora_aT[:, n, :], start=True, stop=True)
            last.then_inc(prep_ps, 1)
            pe.wait_ge(prep, 18)
            nc.tensor.matmul(k_H[0][:, :], be1_rep[:], w1[:], start=True, stop=True).then_inc(prep_ps, 1)
            for n in range(HC):
                last = nc.tensor.matmul(k_Y[:, 0:D], be2_rep[:, n, :], w2[:, n, :], start=(n == 0), stop=(n == HC - 1))
            last.then_inc(prep_ps, 1)
            pe.wait_ge(prep, 22)

            def transpose_x(t, p):
                pe.wait_ge(xs_ok, t + 1)
                need(pe, xT_ok, t)
                nc.tensor.transpose(k_T[:, 0:P], xs[:, p, :], ident[:]).then_inc(xs_T, 1)

            def project(t, p):
                pe.wait_ge(xT_ok, t + 1)
                need(pe, rest1, t - 1)
                need(pe, v_ok, t - 1)
                nc.tensor.matmul(k_QKV[p][:, 2 * P:2 * P + D], xT[:, p, :], w_qkv[:, 2, :], start=True, stop=True)
                for n in range(2):
                    last = nc.tensor.matmul(k_QKV[p][:, n * P:(n + 1) * P], w_qkv[:, n, :], xT[:, p, :], start=True, stop=True)
                last.then_inc(qkv_ps, 1)
                need(pe, h_ok, t - 1)
                nc.tensor.matmul(k_H[p][:, :], xT[:, p, :], w1g[:], start=True, stop=True).then_inc(ph_ok, 1)

            def transpose_hidden(t, p):
                pe.wait_ge(hn_ok, t + 1)
                need(pe, hT_ok, t - 1)
                for n in range(HC):
                    last = nc.tensor.transpose(k_T4[p][:, n * P:(n + 1) * P], hn[:, p, n * P:(n + 1) * P], ident[:])
                last.then_inc(hn_T, 1)

            def second(t, p):
                pe.wait_ge(hT_ok, t + 1)
                need(pe, y_ok, t)
                for n in range(HC):
                    last = nc.tensor.matmul(k_Y[:, 0:D], hT[:, p, n * P:(n + 1) * P], w2g[:, n, :],
                                            start=(n == 0), stop=(n == HC - 1))
                last.then_inc(y_ps, 1)

            tile_loop(pe, NT, [(1, project), (0, transpose_x), (5, second), (4, transpose_hidden)])

        @block.scalar
        def _(s):
            def copy_xT(t, p):
                s.wait_ge(xs_T, t + 1)
                need(s, ph_ok, t - 1)
                nc.scalar.copy(xT[:, p, :], k_T[:, 0:P]).then_inc(xT_ok, 1)

            def first_part(t, p):
                s.wait_ge(qkv_ps, t + 1)
                nc.scalar.copy(v_sb[:, one(t), :], k_QKV[p][:, 2 * P:2 * P + D]).then_inc(v_ok, 1)
                nc.scalar.copy(parts[:, 0, :, one(t), :].rearrange("p w o t -> p w (o t)"),
                               k_QKV[p][:, 0:2 * P].rearrange("p (w t) -> p w t", w=2)).then_inc(part1, 1)

            def second_part(t, p):
                s.wait_ge(rest1, t + 1)
                nc.scalar.copy(parts[:, 1, :, one(t), :].rearrange("p w o t -> p w (o t)"),
                               rest[:, p, :].rearrange("p (w t) -> p w t", w=2)).then_inc(part2, 1)

            def gelu(t, p):
                s.wait_ge(h_ok, t + 1)
                nc.scalar.activation(h[:, one(t), :], h[:, one(t), :], ACT.Gelu).then_inc(gelu_ok, 1)

            def copy_hT(t, p):
                s.wait_ge(hn_T, t + 1)
                need(s, y_ps, t - 1)
                nc.scalar.copy(hT[:, p, :], k_T4[p][:, :]).then_inc(hT_ok, 1)

            tile_loop(s, NT, [(2, gelu), (0, copy_xT), (2, second_part), (1, first_part), (4, copy_hT)])

        @block.gpsimd
        def _(g):
            g.wait_ge(prep, 1)
            g.wait_ge(stat, 2 * NT + 1)
            nc.gpsimd.tensor_tensor(rstd[:], ve[:], half[:], ALU.pow).then_inc(pool_pow, 1)
            g.wait_ge(stat, 2 * NT + 4)
            nc.gpsimd.tensor_tensor(rln1[:], vr[:], half[:], ALU.pow).then_inc(pool_pow, 1)

            def hidden_rstd(t, p):
                g.wait_ge(hst, 3 * t + 3)
                nc.gpsimd.tensor_tensor(hrstd[:, p:p + 1], hve[:, p:p + 1], half[:, 0:1], ALU.pow).then_inc(r_h, 1)

            tile_loop(g, NT, [(3, hidden_rstd)])


def layer1_attention(nc, a, ident, v_sb, o_sb, split_dram):
    with ExitStack() as c:
        def sb(name, shape, dt=F32):
            return c.enter_context(nc.sbuf_tensor("at_" + name, shape, dt))

        def sem(name):
            return c.enter_context(nc.semaphore("at_" + name))

        s_bank = [c.enter_context(nc.psum_tensor(f"at_s{i}", [P, BANK], F32)) for i in range(3)]
        e_bank = [c.enter_context(nc.psum_tensor(f"at_e{i}", [P, BANK], F32)) for i in range(3)]
        o_bank = [c.enter_context(nc.psum_tensor(f"at_o{i}", [P, BANK], F32)) for i in range(2)]

        NB = 3
        qa = sb("qa", [P, NB, QUAD, N], BF16)
        ka = sb("ka", [P, NB, QUAD, N], BF16)
        ident_bf = sb("ident_bf", [P, P], BF16)
        below = sb("below", [P, P], BF16)
        later = sb("later", [P, P], BF16)
        m = sb("m", [P, NB, QUAD, TB])
        m2 = sb("m2", [P, QUAD, TB // 2, 2])
        mpart = sb("mpart", [QUAD * TB, NB, PARTS, P], BF16)
        mrest = sb("mrest", [QUAD * TB, NB, P])
        vg = sb("vg", [P, NB, TB, QUAD, 32])
        pr = sb("pr", [P, 2, QUAD, N])
        oT = sb("oT", [P, 2, BANK])
        rd = sb("rd", [P, 2, QUAD, QUAD])

        c_in, zero_ok, vg0 = sem("c_in"), sem("zero_ok"), sem("vg0")
        sp_in = [sem(f"sp_in{i}") for i in range(NB)]
        s_ps, s_max = sem("s_ps"), sem("s_max")
        m_ok, mp_ok = sem("m_ok"), sem("mp_ok")
        m_in = [sem(f"m_in{i}") for i in range(NB)]
        e_ps, e_ok, pv_ps = sem("e_ps"), sem("e_ok"), sem("pv_ps")
        o_evac, oT_ps, rd_ok, o_norm, vg_ok = sem("o_evac"), sem("oT_ps"), sem("rd_ok"), sem("o_norm"), sem("vg_ok")

        UNITS = []
        for qb in reversed(range(TB)):
            for j in range(QUAD):
                for lo in range(0, (qb + 1) * P, BANK):
                    UNITS.append((qb, j, lo, min((qb + 1) * P - lo, BANK)))
        MU = len(UNITS) + 1
        ROW2 = 3 * QUAD * 2
        EXPS = [(kb, j, lo, min(N - kb * P - lo, BANK)) for kb in range(TB) for j in range(QUAD)
                for lo in range(0, N - kb * P, BANK)]
        EU = len(EXPS)

        def exps_to(kb):
            return sum(u[0] <= kb for u in EXPS)
        LOADS = 2 * PARTS * PARTS

        block = c.enter_context(nc.Block())

        def load_parts(q, g, p):
            b, hg = g // QUAD, g % QUAD
            need(q, e_ok, EU * (g - 2) + 1)
            for i in range(PARTS):
                for k in range(PARTS):
                    rows = slice((i * PARTS + k) * HD, (i * PARTS + k + 1) * HD)
                    for w, dst, part in ((0, qa, i), (1, ka, k)):
                        src = split_dram[one(b), part, w, bass.ds(hg * QUAD * HD, QUAD * HD), :]
                        q.dma_start(dst[rows, p, :, :], src.rearrange("o (j d) t -> (o d) j t", d=HD)).then_inc(sp_in[p], 16)
            src = a["alibi"].bitcast(BF16)[:, bass.ds(hg * QUAD, QUAD), :]
            q.dma_start(ka[ROW_ALIBI:ROW_ALIBI + PARTS, p, :, :], src).then_inc(sp_in[p], 16)

        PER = LOADS + 1

        @block.sync
        def _(sp):
            sp.dma_start(ident_bf[:], a["ident_bf"].bitcast(BF16)).then_inc(c_in, 16)
            sp.dma_start(below[:], a["below"].bitcast(BF16)).then_inc(c_in, 16)
            sp.dma_start(later[:], a["later"].bitcast(BF16)).then_inc(c_in, 16)
            sp.wait_ge(zero_ok, 2 * NB)
            for p in range(NB):
                sp.dma_start(qa[ROW_ALIBI:ROW_ALIBI + PARTS, p, :, :], a["ones_bf"].bitcast(BF16)).then_inc(c_in, 16)
                sp.dma_start(ka[ROW_MAX:ROWS, p, :, :], a["ones_bf"].bitcast(BF16)).then_inc(c_in, 16)
            sp.wait_ge(c_in, 16 * (3 + 2 * NB))

            def maxima_rows(g, p):
                sp.wait_ge(mp_ok, 4 * (g + 1))
                for part in range(PARTS):
                    sp.dma_start(qa[ROW_MAX + part:ROW_MAX + part + 1, p, :, :].rearrange("o j t -> o (j t)"),
                                 mpart[:, p, part, :]).then_inc(m_in[p], 16)

            for g in range(2):
                load_parts(sp, g, g)
            with sp.Fori(0, (NG - 2) // NB) as i:
                for u in range(NB):
                    maxima_rows(NB * i + u, u)
                    load_parts(sp, NB * i + (u + 2), (u + 2) % NB)
            for g in range(NG - 2, NG):
                maxima_rows(g, g % NB)
            for p in range(NB):
                sp.wait_ge(m_in[p], 16 * PARTS * len(range(p, NG, NB)))

        def turns(eng, body):
            for n in range(2):
                body(n, n % NB)
            with eng.Fori(0, (NG - 2) // NB) as i:
                for u in range(NB):
                    body(NB * i + (2 + u), (2 + u) % NB)
            for n in range(NG, NG + 2):
                body(n, n % NB)

        def has(n, lag):
            return not isinstance(n, int) or 0 <= n - lag < NG

        @block.tensor
        def _(pe):
            pe.wait_ge(c_in, 16 * (3 + 2 * NB))

            def score_unit(g, p, u):
                qb, j, lo, w = UNITS[u]
                k = MU * g + u
                need(pe, s_max, k if u == 0 else k - 2)
                bank = s_bank[u % 3]
                diagonal = lo + w == (qb + 1) * P
                last = nc.tensor.matmul(bank[:, 0:w], qa[0:ROW_MAX, p, j, qb * P:(qb + 1) * P],
                                        ka[0:ROW_MAX, p, j, lo:lo + w], start=True, stop=not diagonal)
                if diagonal:
                    last = nc.tensor.matmul(bank[:, w - P:w], ident_bf[:], later[:], start=False, stop=True)
                last.then_inc(s_ps, 1)

            def exp_unit(g, p, u):
                kb, j, lo, w = EXPS[u]
                need(pe, e_ok, EU * g + u - 2)
                bank = e_bank[u % 3]
                last = nc.tensor.matmul(bank[:, 0:w], ka[0:ROWS, p, j, kb * P:(kb + 1) * P],
                                        qa[0:ROWS, p, j, kb * P + lo:kb * P + lo + w], start=True, stop=lo > 0)
                if lo == 0:
                    last = nc.tensor.matmul(bank[:, 0:P], ident_bf[:], below[:], start=False, stop=True)
                last.then_inc(e_ps, 1)

            def values(g, p, kb, half):
                lo = max(kb * P, half * BANK)
                if lo >= (half + 1) * BANK:
                    return
                pe.wait_ge(e_ok, EU * g + exps_to(kb))
                if kb == 0:
                    need(pe, o_evac, 2 * g - 1 + half)
                for j in range(QUAD):
                    last = nc.tensor.matmul(
                        o_bank[half][32 * j:32 * (j + 1), lo - half * BANK:BANK],
                        vg[:, p, kb, j, :], pr[:, kb % 2, j, lo - kb * P:(half + 1) * BANK - kb * P],
                        start=(kb == 0), stop=(kb == QUAD * (half + 1) - 1))
                if half == 1:
                    last.then_inc(pv_ps, 1)

            def transpose_out(g, half):
                pe.wait_ge(o_evac, 2 * g + half + 1)
                for n in range(QUAD):
                    last = nc.tensor.transpose(s_bank[half][:, n * P:(n + 1) * P], oT[:, half, n * P:(n + 1) * P], ident[:])
                last.then_inc(oT_ps, 1)

            def body(n, p):
                for row in range(TB):
                    e_lag, e_row = (2, TB - 1) if row == 0 else (1, row - 1)
                    v_lag, v_row = (2, TB - 2 + row) if row < 2 else (1, row - 2)
                    if row == 0 and has(n, 0):
                        pe.wait_ge(sp_in[p], 16 * PER * (n // NB + 1))
                    if row == 1 and has(n, 1):
                        pe.wait_ge(m_in[(p - 1) % NB], 16 * PARTS * ((n - 1) // NB + 1))
                        pe.wait_ge(vg_ok, n)
                    for j in range(QUAD):
                        for piece in range(2):
                            for u in range(MU - 1):
                                if has(n, 0) and UNITS[u][:3] == (TB - 1 - row, j, piece * BANK):
                                    if row == 3 and j == 0 and has(n, 2):
                                        pe.wait_ge(o_norm, 2 * (n - 2) + piece + 1)
                                    score_unit(n, p, u)
                            for u in range(EU):
                                if has(n, e_lag) and EXPS[u][:3] == (e_row, j, piece * BANK):
                                    exp_unit(n - e_lag, (p - e_lag) % NB, u)
                        if has(n, v_lag) and j in (1, 2):
                            values(n - v_lag, (p - v_lag) % NB, v_row, j - 1)
                    if row == 2 and has(n, 2):
                        for half in range(2):
                            pe.wait_ge(s_max, MU * n + ROW2 - 2 + half if has(n, 0) else MU * NG)
                            if not has(n, 0):
                                pe.wait_ge(o_norm, 2 * (n - 2))
                            transpose_out(n - 2, half)
                if has(n, 0):
                    pe.wait_ge(m_ok, n + 1)
                    pe.wait_ge(s_max, MU * n + len(UNITS))
                    if has(n, 2):
                        pe.wait_ge(o_norm, 2 * (n - 1))
                    nc.tensor.transpose(s_bank[0][0:QUAD * TB, 0:P], m[:, p, :, :].rearrange("p j k -> p (j k)"),
                                        ident[:]).then_inc(s_ps, 1)

            turns(pe, body)

        @block.vector
        def _(v):
            for g in range(NB):
                nc.vector.memset(qa[:, g, :, :], 0.0).then_inc(zero_ok, 1)
                nc.vector.memset(ka[:, g, :, :], 0.0).then_inc(zero_ok, 1)

            def row_units(n, p, row):
                for k, (qb, j, lo, w) in enumerate(UNITS):
                    if qb != TB - 1 - row:
                        continue
                    v.wait_ge(s_ps, MU * n + k + 1)
                    bank = s_bank[k % 3]
                    dst = m[:, p, j, qb:qb + 1] if qb < QUAD else m2[:, j, qb - QUAD, lo // BANK:lo // BANK + 1]
                    nc.vector.tensor_reduce(dst, bank[:, 0:w], AX.X, ALU.max).then_inc(s_max, 1)

            def minus_maxima(n, p):
                v.wait_ge(s_ps, MU * n + MU)
                mt = s_bank[0][0:QUAD * TB, 0:P]
                nc.vector.tensor_scalar(mpart[:, p, 0, :], mt, -1.0, None, ALU.mult).then_inc(mp_ok, 1)
                v.wait_ge(mp_ok, 4 * n + 1)
                nc.vector.scalar_tensor_tensor(mrest[:, p, :], mt, -1.0, mpart[:, p, 0, :],
                                               ALU.mult, ALU.subtract).then_inc(s_max, 1)
                v.wait_ge(s_max, MU * (n + 1))
                nc.vector.tensor_copy(mpart[:, p, 1, :], mrest[:, p, :]).then_inc(mp_ok, 1)
                v.wait_ge(mp_ok, 4 * n + 2)
                nc.vector.tensor_tensor(mpart[:, p, 2, :], mrest[:, p, :], mpart[:, p, 1, :],
                                        ALU.subtract).then_inc(mp_ok, 2)

            def outputs(g):
                b, hg = g // QUAD, g % QUAD
                for half in range(2):
                    v.wait_ge(oT_ps, 2 * g + half + 1)
                    ot = s_bank[half][:, :].rearrange("p (n j r) -> p n j r", n=QUAD, j=QUAD)
                    nc.vector.reciprocal(rd[:, half, :, :], ot[:, :, :, HD]).then_inc(rd_ok, 1)
                    v.wait_ge(rd_ok, 2 * g + half + 1)
                    dst = o_sb[:, bass.ds(b * TB + half * QUAD, QUAD), bass.ds(hg * QUAD * HD, QUAD * HD)]
                    nc.vector.tensor_tensor(dst.rearrange("p n (j d) -> p n j d", d=HD), ot[:, :, :, 0:HD],
                                            rd[:, half, :, :].unsqueeze(3).broadcast_to([P, QUAD, QUAD, HD]),
                                            ALU.mult).then_inc(o_norm, 1)

            def body(n, p):
                for row in range(TB):
                    if has(n, 0):
                        row_units(n, p, row)
                        if row == QUAD - 1:
                            v.wait_ge(s_max, MU * n + 2 * QUAD * QUAD)
                            nc.vector.tensor_reduce(m[:, p, :, QUAD:TB], m2[:], AX.X, ALU.max).then_inc(m_ok, 1)
                    if row == 2 and has(n, 2):
                        outputs(n - 2)
                if has(n, 0):
                    minus_maxima(n, p)

            turns(v, body)

        @block.scalar
        def _(s):
            def exp_unit(g, u):
                kb, j, lo, w = EXPS[u]
                if j == 0 and lo == 0:
                    need(s, pv_ps, TB * g + kb - 1)
                s.wait_ge(e_ps, EU * g + u + 1)
                nc.scalar.activation(pr[:, kb % 2, j, lo:lo + w], e_bank[u % 3][:, 0:w], ACT.Exp).then_inc(e_ok, 1)

            def evacuate(g, half):
                s.wait_ge(pv_ps, TB * g + (QUAD if half == 0 else TB))
                nc.scalar.copy(oT[:, half, :], o_bank[half][:, :]).then_inc(o_evac, 1)

            def body(n, p):
                for row in range(TB):
                    lag, e_row = (2, TB - 1) if row == 0 else (1, row - 1)
                    if has(n, lag):
                        for u in range(EU):
                            if EXPS[u][0] == e_row:
                                exp_unit(n - lag, u)
                    if row == 1 and has(n, 2):
                        evacuate(n - 2, 1)
                    if row == QUAD + 2 and has(n, 1):
                        evacuate(n - 1, 0)

            turns(s, body)

        @block.gpsimd
        def _(g_):
            nc.gpsimd.memset(vg[:], 0.0).then_inc(vg0, 1)
            g_.wait_ge(vg0, 1)
            nc.gpsimd.memset(vg[:, :, :, :, HD:HD + 1], 1.0).then_inc(vg0, 1)
            g_.wait_ge(vg0, 2)

            def body(n, p):
                if has(n, 0):
                    b, hg = n // QUAD, n % QUAD
                    need(g_, pv_ps, TB * (n - 2) + 1)
                    src = v_sb[:, bass.ds(b * TB, TB), bass.ds(hg * QUAD * HD, QUAD * HD)]
                    nc.gpsimd.tensor_copy(vg[:, p, :, :, 0:HD], src.rearrange("p k (j d) -> p k j d", d=HD)).then_inc(vg_ok, 1)

            turns(g_, body)


def layer1_out(nc, a, x_sb, ident, y_sb, o_sb, out):
    with ExitStack() as c:
        def sb(name, shape, dt=F32):
            return c.enter_context(nc.sbuf_tensor("out_" + name, shape, dt))

        def sem(name):
            return c.enter_context(nc.semaphore("out_" + name))

        b_T, b_S = (c.enter_context(nc.psum_tensor(f"out_bank{i}", [P, BANK], F32)) for i in range(2))
        w_p = sb("w_p", [P, D])
        o_s = sb("o_s", [P, 2, D])
        o_T = sb("o_T", [P, 2, P])
        th = sb("th", [P, NT, D])
        sg = sb("sg", [P, 2, D])
        w_in, os_ok, o_Tp, oT_ok, th_ok, g_ok, s_ps, sg_ok, x_ok, stored = (sem(n) for n in (
            "w_in", "os_ok", "o_Tp", "oT_ok", "th_ok", "g_ok", "s_ps", "sg_ok", "x_ok", "stored"))
        out_t = out.rearrange("b (k p) d -> p (b k) d", p=P)
        block = c.enter_context(nc.Block())

        @block.sync
        def _(sp):
            sp.dma_start(w_p[:], a["WpT"]).then_inc(w_in, 16)
            with sp.Fori(0, NT // 4) as i:
                sp.wait_ge(x_ok, 4 * i + 4)
                sp.dma_start(out_t[:, bass.ds(4 * i, 4), :], x_sb[:, bass.ds(4 * i, 4), :]).then_inc(stored, 16)
            sp.wait_ge(stored, 16 * (NT // 4))

        @block.scalar
        def _(s):
            def copy_o(t, p):
                need(s, o_Tp, t - 1)
                nc.scalar.copy(o_s[:, p:p + 1, :], o_sb[:, one(t), :]).then_inc(os_ok, 1)
                nc.scalar.activation(th[:, one(t), :], y_sb[:, one(t), :], ACT.Tanh, scale=0.5).then_inc(th_ok, 1)

            def copy_T(t, p):
                s.wait_ge(o_Tp, t + 1)
                need(s, s_ps, t - 1)
                nc.scalar.copy(o_T[:, p, :], b_T[:, 0:P]).then_inc(oT_ok, 1)

            tile_loop(s, NT, [(0, copy_o), (1, copy_T)])

        @block.tensor
        def _(pe):
            pe.wait_ge(w_in, 16)

            def transpose_o(t, p):
                pe.wait_ge(os_ok, t + 1)
                need(pe, oT_ok, t)
                nc.tensor.transpose(b_T[:, 0:P], o_s[:, p, :], ident[:]).then_inc(o_Tp, 1)

            def project(t, p):
                pe.wait_ge(oT_ok, t + 1)
                need(pe, sg_ok, t)
                nc.tensor.matmul(b_S[:, 0:D], o_T[:, p, :], w_p[:], start=True, stop=True).then_inc(s_ps, 1)

            tile_loop(pe, NT, [(0, transpose_o), (1, project)])

        @block.vector
        def _(v):
            def gate(t, p):
                v.wait_ge(th_ok, t + 1)
                nc.vector.scalar_tensor_tensor(y_sb[:, one(t), :], th[:, one(t), :], 1.0, y_sb[:, one(t), :],
                                               ALU.add, ALU.mult).then_inc(g_ok, 1)

            def finish(t, p):
                v.wait_ge(g_ok, t + 1)
                v.wait_ge(s_ps, t + 1)
                need(v, x_ok, t - 1)
                nc.vector.scalar_tensor_tensor(sg[:, p:p + 1, :], b_S[:, 0:D].unsqueeze(1), 0.5, y_sb[:, one(t), :],
                                               ALU.mult, ALU.mult).then_inc(sg_ok, 1)
                v.wait_ge(sg_ok, t + 1)
                nc.vector.tensor_tensor(x_sb[:, one(t), :], x_sb[:, one(t), :], sg[:, p:p + 1, :], ALU.add).then_inc(x_ok, 1)

            tile_loop(v, NT, [(0, gate), (1, finish)])


def constants():
    import numpy as np

    def bf16(v):
        u = np.ascontiguousarray(v, np.float32).view(np.uint32)
        return ((u + 0x7FFF + ((u >> 16) & 1)) >> 16).astype(np.uint16)

    def value(bits):
        return (bits.astype(np.uint32) << 16).view(np.float32).astype(np.float64)

    head = np.arange(P) // HD
    i, j = np.arange(P)[:, None], np.arange(P)[None, :]
    start = 2.0 ** (-(2.0 ** -1))
    slopes = np.asarray([start * start ** h for h in range(H)], np.float32).astype(np.float64)
    bias = -slopes[:, None] * np.arange(N, dtype=np.float64)[None, :]
    alibi = []
    for _ in range(PARTS):
        alibi.append(bf16(bias))
        bias = bias - value(alibi[-1])
    return {
        "ident": np.eye(P, dtype=np.float32),
        "head_mask": (head[:, None] == np.arange(H)[None, :]).astype(np.float32),
        "ident_bf": bf16(np.eye(P)),
        "below": bf16(np.where(j < i, -1e30, 0.0)),
        "later": bf16(np.where(j > i, -1e30, 0.0)),
        "alibi": np.stack(alibi),
        "ones_bf": bf16(np.ones((PARTS, QUAD, N))),
    }


def layouts(x):
    import numpy as np

    col = lambda v: np.asarray(v).reshape(-1, 1)
    t = lambda v: np.ascontiguousarray(np.asarray(v).T)
    out = {k: np.ascontiguousarray(np.asarray(x[k])) for k in (
        "L0_attn_x", "L0_attn_b_out", "L0_ffn_Wq", "L0_ffn_Wup", "L0_ffn_bq", "L0_ffn_bup", "L0_ffn_Wo",
        "L0_ffn_bo", "L0_ffn_Wg", "L0_ffn_bg", "L0_ffn_We", "L1_attn_Bq", "L1_attn_Bk", "L1_attn_Bv",
        "L1_ffn_b1", "L1_ffn_b2")}
    out.update(w_qkvT=t(x["L0_attn_w_qkv"]), w_outT=t(x["L0_attn_w_out"]), WdownT=t(x["L0_ffn_Wdown"]),
               gamma1=col(x["L0_ffn_gamma1"]), gamma2=col(x["L0_ffn_gamma2"]), bdown=col(x["L0_ffn_bdown"]),
               WqT=t(x["L1_attn_Wq"]), WkT=t(x["L1_attn_Wk"]), WvT=t(x["L1_attn_Wv"]), WpT=t(x["L1_attn_Wp"]),
               AqT=t(x["L1_attn_Aq"]), AkT=t(x["L1_attn_Ak"]), AvT=t(x["L1_attn_Av"]),
               ln1_g=col(x["L1_ffn_ln1_g"]), ln1_b=col(x["L1_ffn_ln1_b"]),
               ln2_g=col(x["L1_ffn_ln2_g"]), ln2_b=col(x["L1_ffn_ln2_b"]),
               w1T=t(x["L1_ffn_w1"]), w2T=t(x["L1_ffn_w2"]))
    return out


def kernel(**inputs):
    import numpy as _np
    import concourse.bacc as _bacc
    from concourse import mybir as _mybir
    from concourse.bass_utils import run_bass_kernel_spmd as _run

    nc = _bacc.Bacc("TRN2", target_bir_lowering=False, num_devices=1)
    arrays, args = {}, {}
    for name, arr in {**layouts(inputs), **constants()}.items():
        arrays[f"in_{name}_dram"] = arr
        args[name] = nc.dram_tensor(f"in_{name}_dram", arr.shape, _mybir.dt.from_np(arr.dtype), kind="ExternalInput").ap()
    out = nc.dram_tensor("out_0_dram", (B, N, D), F32, kind="ExternalOutput").ap()
    mixer_kernel(nc, args, out)
    r = _run(nc, [arrays], core_ids=[0])
    return r.results[0]["out_0_dram"]
```

```python
import concourse.bass as bass
from concourse import mybir
from contextlib import ExitStack

F32 = mybir.dt.float32
BF16 = mybir.dt.bfloat16
ALU = mybir.AluOpType
ACT = mybir.ActivationFunctionType
AX = mybir.AxisListType

B, N, D, H = 2, 1024, 128, 16
HD = D // H
P = 128
NT = B * N // P
TB = N // P
L = 64
E = 8
HID = 512
HC = HID // P
R = 8
QUAD = 4
NG = B * H // QUAD
PAIRS = TB // 2
BANK = 512

PARTS = 3
ROW_ALIBI = PARTS * PARTS * HD
ROW_MAX = 96
ROWS = ROW_MAX + PARTS

LN_EPS = 1e-5
RMS_EPS = 1e-6


def need(eng, sem, n):
    if isinstance(n, int) and n <= 0:
        return
    eng.wait_ge(sem, n)


def upto(n, most=NT):
    return min(n, most) if isinstance(n, int) else n


def one(i):
    return bass.ds(i, 1)


def tile_loop(eng, tiles, stages):
    deepest = max(lag for lag, _ in stages)

    def step(n, parity):
        for lag, stage in stages:
            if isinstance(n, int) and not 0 <= n - lag < tiles:
                continue
            stage(n - lag, (parity + lag) % 2)

    first = deepest + 4
    first += first % 2
    last = first + (tiles - first) // 2 * 2
    for n in range(first):
        step(n, n % 2)
    with eng.Fori(0, (last - first) // 2) as i:
        for u in range(2):
            step(2 * i + (first + u), u)
    for n in range(last, tiles + deepest):
        step(n, n % 2)


def mixer_kernel(nc, a, out):
    with ExitStack() as whole:
        def sb(name, shape, dt=F32, ctx=whole):
            return ctx.enter_context(nc.sbuf_tensor(name, shape, dt))

        x_sb = sb("x_sb", [P, NT, D])
        ident = sb("ident", [P, P])
        split_dram = nc.dram_tensor("split_scratch", [B, PARTS, 2, D, N], BF16, kind="Internal").ap()

        w1 = Layer1Weights(nc, a, whole)
        ops = ScoreOperands(nc, a, whole, split_dram)
        layer0(nc, a, w1, ops, x_sb, ident)
        with ExitStack() as c:
            v_sb = sb("v_sb", [P, NT, D], F32, c)
            y_sb = sb("y_sb", [P, NT, D], F32, c)
            layer1_dense(nc, a, w1, ops, x_sb, ident, v_sb, y_sb, split_dram)
            o_sb = sb("o_sb", [P, NT, D], F32, c)
            layer1_attention(nc, ops, ident, v_sb, y_sb, o_sb)
            layer1_out(nc, a, x_sb, ident, y_sb, o_sb, out)


def layer0(nc, a, w1, ops, x_sb, ident):
    with ExitStack() as c:
        def sb(name, shape, dt=F32):
            return c.enter_context(nc.sbuf_tensor("l0_" + name, shape, dt))

        def sem(name):
            return c.enter_context(nc.semaphore("l0_" + name))

        banks = [c.enter_context(nc.psum_tensor(f"l0_bank{i}", [P, BANK], F32)) for i in range(8)]

        w_all = sb("w_all", [P, 6 * D])
        w_out = sb("w_out", [P, D])
        w_o = sb("w_o", [P, D])
        w_e = sb("w_e", [P, E, D])
        w_g = sb("w_g", [P, E])
        w_q = sb("w_q", [P, D])
        w_dT = sb("w_dT", [L, D])
        w_up = sb("w_up", [L, 2 * D])
        gam1 = sb("gam1", [P, 1])
        gam2 = sb("gam2", [P, 1])
        b_down = sb("b_down", [L, 1])
        b_down_rep = sb("b_down_rep", [L, P])
        b_qkv = sb("b_qkv", [P, 3 * D])
        b_out = sb("b_out", [P, D])
        b_o = sb("b_o", [P, D])
        b_g = sb("b_g", [P, E])
        head_mask = sb("head_mask", [P, H])
        half = sb("half", [P, NT])

        st6 = sb("st6", [P, NT, 6])
        mv = sb("mv", [P, NT, 2])
        ve = sb("ve", [P, NT])
        rstd = sb("rstd", [P, NT])
        vr = sb("vr", [P, NT])
        rms1 = sb("rms1", [P, NT])

        qkv = sb("qkv", [P, NT, 3 * D])
        att = sb("att", [P, 2, H * H])
        rsum = sb("rsum", [P, 2, H])
        ql_T = sb("ql_T", [P, NT, P])
        kv_part = sb("kv_part", [P, NT, D + 1])
        gate = sb("gate", [P, NT, D])
        xnb = gate
        xs = sb("xs", [P, 2, D])
        xT = sb("xT", [P, 2, P])
        mn = sb("mn", [P, 2, 2 * D])
        ql = sb("ql", [P, 2, 2 * D])
        vl = sb("vl", [P, 2, D + 1])
        prod = sb("prod", [P, 2, 2, H * H * HD])
        mx = sb("mx", [P, 2, H])
        o_raw = sb("o_raw", [P, 2, D])
        o_n = sb("o_n", [P, 2, D])
        o_T = sb("o_T", [P, 2, P])
        em = sb("em", [P, 2, E + 1, D])
        x2_T = sb("x2_T", [P, 2, P])
        sq = sb("sq", [P, 2, D])
        ss = sb("ss", [P, NT])
        ms = sb("ms", [P, NT])
        rms2 = sb("rms2", [P, NT])
        lg = sb("lg", [P, 2, E])
        nmx = sb("nmx", [P, 2, 1])
        ge = sb("ge", [P, 2, E])
        gs = sb("gs", [P, 2, 1])
        gr = sb("gr", [P, 2, 1])
        gw = sb("gw", [P, 2, E])
        acc = sb("acc", [P, 2, D])
        th = sb("th", [P, 2, D])
        kv_sum = sb("kv_sum", [P, B, D + 1])
        bdks = sb("bdks", [P, B, D + H])
        q_s = sb("q_s", [P, 2, P])
        den = sb("den", [P, 2, H])
        rden = sb("rden", [P, 2, H])
        lin = sb("lin", [P, 2, D])
        lin_T = sb("lin_T", [P, 2, P])
        s_b = sb("s_b", [P, 2, D])
        s_g = sb("s_g", [P, 2, D])

        x_in, w_in, w1_in = sem("x_in"), sem("w_in"), sem("w1_in")
        w1_v, w1_ps, w1_g, st1_ok, ops_in = (sem(n) for n in ("w1_v", "w1_ps", "w1_g", "st1_ok", "ops_in"))
        prep_ps, prep, late_in, gains_ok = sem("prep_ps"), sem("prep"), sem("late_in"), sem("gains_ok")
        stat, pool_pow = sem("stat"), sem("pool_pow")
        xs_ok, xs_T, xT_ok = sem("xs_ok"), sem("xs_T"), sem("xT_ok")
        projA, projB = sem("projA"), sem("projB")
        mn_ok, ex_ok, ql_ok, vl_ok, qkv_ok = sem("mn_ok"), sem("ex_ok"), sem("ql_ok"), sem("vl_ok"), sem("qkv_ok")
        qlT_kv, qlT_ok = sem("qlT_kv"), sem("qlT_ok")
        xnb_ok = sem("xnb_ok")
        p1_ok, s1_ok, mx_ok, sub_ok, exp_ok, sum_ok, rs_ok = (sem(n) for n in (
            "p1_ok", "s1_ok", "mx_ok", "sub_ok", "exp_ok", "sum_ok", "rs_ok"))
        p2_ok, or_ok, on_ok, on_T, oT_ok, wo_ok, x2_ok = (sem(n) for n in (
            "p2_ok", "or_ok", "on_ok", "on_T", "oT_ok", "wo_ok", "x2_ok"))
        sq_ok, ms_ok, r2_ok, x2_T_ps, x2T_ok, gl_ok, moe_ok = (sem(n) for n in (
            "sq_ok", "ms_ok", "r2_ok", "x2_T_ps", "x2T_ok", "gl_ok", "moe_ok"))
        gv, ge_ok, em_ok, acc_ok, th_ok, gate_ok = (sem(n) for n in ("gv", "ge_ok", "em_ok", "acc_ok", "th_ok", "gate_ok"))
        kvs = sem("kvs")
        qs_ok, nd_ok, den_ok, rden_ok, lin_ok, lin_T_ps, linT_ok, so_ok, sb_ok, sg_ok, x1_ok = (sem(n) for n in (
            "qs_ok", "nd_ok", "den_ok", "rden_ok", "lin_ok", "lin_T_ps", "linT_ok", "so_ok", "sb_ok", "sg_ok", "x1_ok"))

        scale = float(HD) ** -0.5
        v_T, v_A, v_B, v_Q, v_O, v_G, v_M0, v_M1 = banks
        nd_bank, linT_bank, so_bank = (v_A, v_B), (v_T, v_Q), (v_O, v_G)

        FIRST_OF = (0, 4)

        early = (
            (ident[:], a["ident"]), (w_all[:, 0:3 * D], a["w_qkvT"]), (w_q[:], a["L0_ffn_Wq"]),
            (w_dT[:], a["WdownT"]), (w_up[:], a["Wup"]), (gam1[:], a["gamma1"]), (b_down[:], a["bdown"]),
            (b_qkv[:, 0:D], a["L0_ffn_bq"].partition_broadcast(P)),
            (b_qkv[:, D:3 * D], a["bup"].partition_broadcast(P)),
            (b_o[:], a["L0_ffn_bo"].partition_broadcast(P)))
        late = (
            (gam2[:], a["gamma2"]),
            (w_o[:], a["L0_ffn_Wo"]), (w_g[:], a["L0_ffn_Wg"]),
            (w_e[:], a["L0_ffn_We"].rearrange("e d f -> d e f")),
            (b_g[:], a["L0_ffn_bg"].partition_broadcast(P)), (head_mask[:], a["head_mask"]),
            (w_out[:], a["w_outT"]), (b_out[:], a["L0_attn_b_out"].partition_broadcast(P)))

        block = c.enter_context(nc.Block())

        @block.sync
        def _(sp):
            x_d = a["L0_attn_x"].rearrange("b (k p) d -> p (b k) d", p=P)
            for k in range(4):
                sp.dma_start(x_sb[:, 4 * k:4 * k + 4, :], x_d[:, 4 * k:4 * k + 4, :]).then_inc(x_in, 16)
            for dst, src in early:
                sp.dma_start(dst, src).then_inc(w_in, 16)
            for dst, src in late:
                sp.dma_start(dst, src).then_inc(late_in, 16)
            for dst, src in w1.loads:
                sp.dma_start(dst, src, allow_slow_non_contiguous=True).then_inc(w1_in, 16)
            for dst, src in ops.constants():
                sp.dma_start(dst, src).then_inc(ops_in, 16)
            sp.wait_ge(w1_in, 16 * len(w1.loads))
            sp.wait_ge(ops_in, 16 * len(ops.constants()))

        @block.vector
        def _(v):
            nc.vector.memset(half[:], -0.5).then_inc(prep, 1)
            nc.vector.memset(vl[:, :, D:D + 1], 1.0).then_inc(prep, 1)

            def statistics_of(lo, hi):
                for t in range(lo, hi):
                    nc.vector.bn_stats(st6[:, t, :], x_sb[:, t, :]).then_inc(stat, 1)
                v.wait_ge(stat, 2 * lo + hi - lo + (4 if lo else 0))
                for t in range(lo, hi):
                    nc.vector.bn_aggr(mv[:, t, :], st6[:, t, :]).then_inc(stat, 1)
                n = 2 * hi + (4 if lo else 0)
                v.wait_ge(stat, n)
                nc.vector.tensor_scalar(ve[:, lo:hi], mv[:, lo:hi, 1], LN_EPS, None, ALU.add).then_inc(stat, 1)
                v.wait_ge(stat, n + 1)
                nc.vector.reciprocal(vr[:, lo:hi], ve[:, lo:hi]).then_inc(stat, 1)
                v.wait_ge(stat, n + 2)
                nc.vector.tensor_tensor(vr[:, lo:hi], vr[:, lo:hi], mv[:, lo:hi, 1], ALU.mult).then_inc(stat, 1)
                v.wait_ge(stat, n + 3)
                nc.vector.tensor_scalar(vr[:, lo:hi], vr[:, lo:hi], RMS_EPS, None, ALU.add).then_inc(stat, 1)

            v.wait_ge(x_in, 16 * 4)
            statistics_of(0, FIRST_OF[1])

            v.wait_ge(w_in, 16 * len(early))
            nc.vector.tensor_copy(b_down_rep[:], b_down[:].broadcast_to([L, P])).then_inc(prep, 1)
            nc.vector.tensor_scalar(w_all[:, 3 * D:4 * D], w_q[:], gam1[:], scale, ALU.mult, ALU.mult).then_inc(prep, 1)
            nc.vector.tensor_scalar(b_qkv[:, 0:D], b_qkv[:, 0:D], scale, None, ALU.mult).then_inc(prep, 1)
            v.wait_ge(prep_ps, 1)
            nc.vector.tensor_scalar(w_all[:, 4 * D:6 * D], v_A[:, 0:2 * D], gam1[:], None, ALU.mult).then_inc(prep, 1)
            v.wait_ge(prep_ps, 2)
            nc.vector.tensor_tensor(b_qkv[:, D:3 * D], v_B[:, 0:2 * D], b_qkv[:, D:3 * D], ALU.add).then_inc(prep, 1)

            def other_statistics(t, p):
                if isinstance(t, int) and t == 0:
                    statistics_of(FIRST_OF[1], NT)

            def normalise(t, p):
                if isinstance(t, int) and t in FIRST_OF:
                    v.wait_ge(pool_pow, 2 * FIRST_OF.index(t) + 1)
                need(v, xnb_ok, t - 1)
                need(v, xs_T, t - 1)
                nc.vector.tensor_scalar(xs[:, p, :], x_sb[:, one(t), :], mv[:, one(t), 0], rstd[:, one(t)],
                                        ALU.subtract, ALU.mult).then_inc(xs_ok, 1)

            def elu_sum(t, p):
                v.wait_ge(ex_ok, t + 1)
                need(v, qlT_kv, t - 1)
                nc.vector.scalar_tensor_tensor(ql[:, p, :], v_A[:, 0:2 * D], 0.0, mn[:, p, :],
                                               ALU.max, ALU.add).then_inc(ql_ok, 1)

            def token_qkv(t, p):
                if isinstance(t, int) and t in FIRST_OF:
                    v.wait_ge(pool_pow, 2 * FIRST_OF.index(t) + 2)
                v.wait_ge(projB, t + 1)
                nc.vector.scalar_tensor_tensor(qkv[:, one(t), :], v_B[:, 0:3 * D], rms1[:, one(t)], b_qkv[:],
                                               ALU.mult, ALU.add).then_inc(qkv_ok, 1)

            def score_sums(t, p):
                v.wait_ge(p1_ok, t + 1)
                need(v, p2_ok, t - 1)
                nc.vector.tensor_reduce(att[:, p, :].rearrange("p (h g) -> p h g", g=H),
                                        prod[:, p, 0, :].rearrange("p (h d g) -> p h g d", g=H, d=HD),
                                        AX.X, ALU.add).then_inc(s1_ok, 1)

            def score_max(t, p):
                v.wait_ge(s1_ok, t + 1)
                need(v, sub_ok, t - 1)
                at = att[:, p, :].rearrange("p (h g) -> p h g", g=H)
                nc.vector.tensor_reduce(mx[:, p, :], at, AX.X, ALU.max).then_inc(mx_ok, 1)

            def subtract_max(t, p):
                v.wait_ge(mx_ok, t + 1)
                at = att[:, p, :].rearrange("p (h g) -> p h g", g=H)
                nc.vector.tensor_tensor(at, at, mx[:, p, :].unsqueeze(2).broadcast_to([P, H, H]),
                                        ALU.subtract).then_inc(sub_ok, 1)

            def sums(t, p):
                v.wait_ge(exp_ok, t + 1)
                nc.vector.tensor_reduce(rsum[:, p, :], att[:, p, :].rearrange("p (h g) -> p h g", g=H),
                                        AX.X, ALU.add).then_inc(sum_ok, 1)

            def sums_inverse(t, p):
                v.wait_ge(sum_ok, t + 1)
                nc.vector.reciprocal(rsum[:, p, :], rsum[:, p, :]).then_inc(rs_ok, 1)

            def weighted(t, p):
                v.wait_ge(p2_ok, t + 1)
                nc.vector.tensor_reduce(o_raw[:, p, :].rearrange("p (h d) -> p h d", d=HD),
                                        prod[:, p, 1, :].rearrange("p (h g d) -> p h d g", g=H, d=HD),
                                        AX.X, ALU.add).then_inc(or_ok, 1)

            def divided(t, p):
                v.wait_ge(or_ok, t + 1)
                v.wait_ge(rs_ok, t + 1)
                need(v, on_T, t - 1)
                nc.vector.tensor_tensor(o_n[:, p, :].rearrange("p (h d) -> p h d", d=HD),
                                        o_raw[:, p, :].rearrange("p (h d) -> p h d", d=HD),
                                        rsum[:, p, :].unsqueeze(2).broadcast_to([P, H, HD]),
                                        ALU.mult).then_inc(on_ok, 1)

            def residual(t, p):
                v.wait_ge(wo_ok, t + 1)
                v.wait_ge(xnb_ok, t + 1)
                need(v, x2_T_ps, t - 1)
                need(v, acc_ok, t - 1)
                need(v, sq_ok, t - 1)
                nc.vector.tensor_tensor(em[:, p, E, :], v_O[:, P:2 * P], xnb[:, one(t), :].rearrange("p o d -> p (o d)"),
                                        ALU.add).then_inc(x2_ok, 1)

            def mean_square(t, p):
                v.wait_ge(sq_ok, t + 1)
                nc.vector.tensor_scalar(ms[:, one(t)], ss[:, one(t)], 1.0 / D, RMS_EPS, ALU.mult, ALU.add).then_inc(ms_ok, 1)

            def gate_logits(t, p):
                if isinstance(t, int) and t == 0:
                    v.wait_ge(late_in, 16 * len(late))
                v.wait_ge(gl_ok, t + 1)
                v.wait_ge(r2_ok, t + 1)
                nc.vector.scalar_tensor_tensor(lg[:, p, :], v_G[:, 0:E], rms2[:, one(t)], b_g[:],
                                               ALU.mult, ALU.add).then_inc(gv, 1)

            def gate_max(t, p):
                v.wait_ge(gv, 4 * t + 1)
                nc.vector.tensor_reduce(nmx[:, p, :], lg[:, p, :], AX.X, ALU.max, negate=True).then_inc(gv, 1)

            def gate_inverse(t, p):
                v.wait_ge(ge_ok, t + 1)
                nc.vector.reciprocal(gr[:, p, :], gs[:, p, :]).then_inc(gv, 1)

            def gate_weights(t, p):
                v.wait_ge(gv, 4 * t + 3)
                need(v, em_ok, t - 1)
                nc.vector.tensor_scalar(gw[:, p, :], ge[:, p, :], gr[:, p, :], rms2[:, one(t)],
                                        ALU.mult, ALU.mult).then_inc(gv, 1)

            def combine(t, p):
                v.wait_ge(em_ok, t + 1)
                need(v, th_ok, t - 1)
                nc.vector.tensor_reduce(acc[:, p, :], em[:, p, :, :].rearrange("p e f -> p f e"), AX.X, ALU.add).then_inc(acc_ok, 1)

            def silu(t, p):
                v.wait_ge(th_ok, t + 1)
                nc.vector.scalar_tensor_tensor(gate[:, one(t), :], th[:, p:p + 1, :], 1.0, acc[:, p:p + 1, :],
                                               ALU.add, ALU.mult).then_inc(gate_ok, 1)

            tile_loop(v, NT, [(0, normalise), (3, score_sums), (8, combine), (3, score_max), (7, gate_logits),
                              (6, residual), (3, subtract_max), (1, elu_sum), (1, token_qkv), (5, weighted),
                              (1, other_statistics), (7, gate_max), (6, mean_square), (5, divided), (4, sums),
                              (7, gate_inverse), (4, sums_inverse), (7, gate_weights), (8, silu)])

            v.wait_ge(w1_in, 16 * len(w1.loads))
            nc.vector.memset(w1.ones[:], 1.0).then_inc(w1_v, 1)
            nc.vector.tensor_reduce(w1.asum[:, 0:1], w1.w1[:], AX.X, ALU.add, apply_absolute_value=True).then_inc(w1_v, 1)
            nc.vector.tensor_reduce(w1.asum[:, 1:2], w1.w2[:].rearrange("p c n -> p (c n)"), AX.X, ALU.add,
                                    apply_absolute_value=True).then_inc(w1_v, 1)

            v.wait_ge(qlT_ok, 2 * NT)
            for b in range(B):
                nc.vector.tensor_reduce(kv_sum[:, b, :], kv_part[:, b * TB:(b + 1) * TB, :].rearrange("p k n -> p n k"),
                                        AX.X, ALU.add).then_inc(kvs, 1)
            v.wait_ge(kvs, B)
            for b in range(B):
                nc.vector.tensor_tensor(bdks[:, b, 0:D].rearrange("p (h m) -> p h m", m=HD),
                                        kv_sum[:, b, 0:D].rearrange("p (h m) -> p h m", m=HD),
                                        head_mask[:].unsqueeze(2).broadcast_to([P, H, HD]), ALU.mult).then_inc(kvs, 1)
                nc.vector.tensor_scalar(bdks[:, b, D:D + H], head_mask[:], kv_sum[:, b, D:D + 1], None,
                                        ALU.mult).then_inc(kvs, 1)

            v.wait_ge(w1_ps, 1)
            nc.vector.tensor_scalar(w1.mean[:], v_M0[:, 0:2], 1.0 / (D * HID), 1e-5, ALU.mult, ALU.max).then_inc(w1_v, 1)
            v.wait_ge(w1_v, 4)
            nc.vector.reciprocal(w1.inv[:], w1.mean[:]).then_inc(w1_v, 1)
            v.wait_ge(w1_ps, 2)
            w_qkv1 = w1.w_qkv[:].rearrange("p n d -> p (n d)")
            nc.vector.scalar_tensor_tensor(w_qkv1, v_M1[:, 0:3 * D], 2.0, w_qkv1, ALU.mult, ALU.add).then_inc(w1_v, 1)
            v.wait_ge(w1_v, 6)
            nc.vector.tensor_scalar(w1.w_qkv[:, 0, :], w1.w_qkv[:, 0, :], scale, None, ALU.mult).then_inc(w1_v, 1)

            def denominators(t, p):
                v.wait_ge(nd_ok, t + 1)
                nc.vector.tensor_scalar(den[:, p, :], nd_bank[p][:, D:D + H], 1e-6, None, ALU.add).then_inc(den_ok, 1)

            def inverse(t, p):
                v.wait_ge(den_ok, t + 1)
                nc.vector.reciprocal(rden[:, p, :], den[:, p, :]).then_inc(rden_ok, 1)

            def quotients(t, p):
                v.wait_ge(rden_ok, t + 1)
                need(v, lin_T_ps, t - 1)
                nc.vector.tensor_tensor(lin[:, p, :].rearrange("p (h m) -> p h m", m=HD),
                                        nd_bank[p][:, 0:D].rearrange("p (h m) -> p h m", m=HD),
                                        rden[:, p, :].unsqueeze(2).broadcast_to([P, H, HD]), ALU.mult).then_inc(lin_ok, 1)

            def attended(t, p):
                v.wait_ge(so_ok, t + 1)
                v.wait_ge(gate_ok, NT)
                nc.vector.tensor_tensor(s_b[:, p, :], so_bank[p][:, 0:D], b_out[:], ALU.add).then_inc(sb_ok, 1)

            def gated(t, p):
                v.wait_ge(sb_ok, t + 1)
                nc.vector.scalar_tensor_tensor(s_g[:, p:p + 1, :], s_b[:, p:p + 1, :], 0.5, gate[:, one(t), :],
                                               ALU.mult, ALU.mult).then_inc(sg_ok, 1)

            def add_to_x(t, p):
                v.wait_ge(sg_ok, t + 1)
                nc.vector.tensor_tensor(x_sb[:, one(t), :], x_sb[:, one(t), :], s_g[:, p:p + 1, :], ALU.add).then_inc(x1_ok, 1)

            def statistics(t, p):
                v.wait_ge(x1_ok, t + 1)
                nc.vector.bn_stats(w1.st6[:, one(t), :], x_sb[:, one(t), :]).then_inc(st1_ok, 1)

            tile_loop(v, NT, [(0, denominators), (3, attended), (0, inverse), (0, quotients), (3, gated),
                              (4, add_to_x), (5, statistics)])

            v.wait_ge(w1_ps, 4)
            nc.vector.tensor_tensor(w1.b1[:], v_M0[:, :], w1.b1[:], ALU.add).then_inc(w1_v, 1)
            nc.vector.tensor_tensor(w1.b2[:], v_M1[:, 0:D], w1.b2[:], ALU.add).then_inc(w1_v, 1)
            v.wait_ge(w1_v, 9)
            v.wait_ge(st1_ok, NT)

        @block.tensor
        def _(pe):
            pe.wait_ge(w_in, 16 * len(early))
            nc.tensor.matmul(v_A[:, 0:2 * D], w_dT[:], w_up[:], start=True, stop=True).then_inc(prep_ps, 1)
            pe.wait_ge(prep, 3)
            nc.tensor.matmul(v_B[:, 0:2 * D], b_down_rep[:], w_up[:], start=True, stop=True).then_inc(prep_ps, 1)
            pe.wait_ge(prep, 7)

            def transpose_x(t, p):
                pe.wait_ge(xs_ok, t + 1)
                need(pe, xT_ok, t)
                need(pe, oT_ok, t - 5)
                nc.tensor.transpose(v_T[:, 0:P], xs[:, p, :], ident[:]).then_inc(xs_T, 1)

            def project(t, p):
                pe.wait_ge(xT_ok, t + 1)
                need(pe, ql_ok, t)
                need(pe, vl_ok, t)
                nc.tensor.matmul(v_A[:, 0:3 * D], xT[:, p, :], w_all[:, 0:3 * D], start=True, stop=True).then_inc(projA, 1)
                need(pe, qkv_ok, t)
                nc.tensor.matmul(v_B[:, 0:3 * D], xT[:, p, :], w_all[:, 3 * D:6 * D], start=True, stop=True).then_inc(projB, 1)

            def linear_kv(t, p):
                pe.wait_ge(ql_ok, t + 1)
                pe.wait_ge(vl_ok, t + 1)
                need(pe, qlT_ok, 2 * t)
                need(pe, x2T_ok, t - 4)
                nc.tensor.transpose(v_Q[:, 0:P], ql[:, p, 0:D], ident[:])
                nc.tensor.matmul(v_Q[:, P:P + D + 1], ql[:, p, D:2 * D], vl[:, p, :], start=True, stop=True).then_inc(qlT_kv, 1)

            def transpose_o(t, p):
                pe.wait_ge(on_ok, t + 1)
                need(pe, xT_ok, upto(t + 6))
                need(pe, oT_ok, t)
                nc.tensor.transpose(v_T[:, P:2 * P], o_n[:, p, :], ident[:]).then_inc(on_T, 1)

            def project_o(t, p):
                if isinstance(t, int) and t == 0:
                    pe.wait_ge(late_in, 16 * len(late))
                pe.wait_ge(oT_ok, t + 1)
                need(pe, x2_ok, t)
                nc.tensor.matmul(v_O[:, P:2 * P], o_T[:, p, :], w_o[:], start=True, stop=True).then_inc(wo_ok, 1)

            def transpose_x2(t, p):
                pe.wait_ge(x2_ok, t + 1)
                need(pe, x2T_ok, t)
                need(pe, qlT_ok, 2 * upto(t + 5))
                nc.tensor.transpose(v_Q[:, 3 * P:4 * P], em[:, p, E, :], ident[:]).then_inc(x2_T_ps, 1)

            def expert_products(t, p):
                if isinstance(t, int) and t == 0:
                    pe.wait_ge(gains_ok, 2)
                pe.wait_ge(x2T_ok, t + 1)
                need(pe, gv, 4 * t)
                need(pe, em_ok, t)
                nc.tensor.matmul(v_G[:, 0:E], x2_T[:, p, :], w_g[:], start=True, stop=True).then_inc(gl_ok, 1)
                for m, bank in enumerate((v_M0, v_M1)):
                    last = nc.tensor.matmul(bank[:, :], x2_T[:, p, :],
                                            w_e[:, 4 * m:4 * m + 4, :].rearrange("p e f -> p (e f)"), start=True, stop=True)
                last.then_inc(moe_ok, 1)

            tile_loop(pe, NT, [(0, transpose_x), (1, project), (7, expert_products), (6, transpose_x2),
                               (1, linear_kv), (5, transpose_o), (5, project_o)])

            pe.wait_ge(em_ok, NT)
            pe.wait_ge(w1_v, 3)
            nc.tensor.matmul(v_M0[:, 0:2], w1.ones[:], w1.asum[:], start=True, stop=True).then_inc(w1_ps, 1)
            for n in range(3):
                last = nc.tensor.matmul(v_M1[:, n * D:(n + 1) * D], w1.lora_b[:, n, :], w1.lora_aT[:, n, :],
                                        start=True, stop=True)
            last.then_inc(w1_ps, 1)

            pe.wait_ge(kvs, 3 * B)
            pe.wait_ge(x2T_ok, NT)

            def transpose_lin(t, p):
                pe.wait_ge(lin_ok, t + 1)
                need(pe, linT_ok, t - 1)
                nc.tensor.transpose(linT_bank[p][:, 0:P], lin[:, p, :], ident[:]).then_inc(lin_T_ps, 1)

            def project_lin(t, p):
                pe.wait_ge(linT_ok, t + 1)
                need(pe, sb_ok, t - 1)
                nc.tensor.matmul(so_bank[p][:, 0:D], lin_T[:, p, :], w_out[:], start=True, stop=True).then_inc(so_ok, 1)

            def nd(t, p):
                pe.wait_ge(qs_ok, t + 1)
                need(pe, lin_ok, t - 1)
                nc.tensor.matmul(nd_bank[p][:, 0:D + H], q_s[:, p, :], bdks[:, one(t // TB), :], start=True, stop=True).then_inc(nd_ok, 1)

            tile_loop(pe, NT, [(0, nd), (1, transpose_lin), (2, project_lin)])

            pe.wait_ge(w1_v, 6)
            pe.wait_ge(w1_g, 12)
            nc.tensor.matmul(v_M0[:, :], w1.be1_rep[:], w1.w1[:], start=True, stop=True).then_inc(w1_ps, 1)
            for n in range(HC):
                last = nc.tensor.matmul(v_M1[:, 0:D], w1.be2_rep[:, n, :], w1.w2[:, n, :], start=(n == 0), stop=(n == HC - 1))
            last.then_inc(w1_ps, 1)

        @block.scalar
        def _(s):
            def copies_x(t, p):
                s.wait_ge(xs_T, t + 1)
                need(s, projB, t - 1)
                nc.scalar.copy(xT[:, p, :], v_T[:, 0:P]).then_inc(xT_ok, 1)

            def minus_min(t, p):
                s.wait_ge(projA, t + 1)
                need(s, ql_ok, t - 1)
                nc.scalar.activation(mn[:, p, :], v_A[:, 0:2 * D], ACT.Relu, scale=-1.0).then_inc(mn_ok, 1)

            def exps(t, p):
                s.wait_ge(mn_ok, t + 1)
                nc.scalar.activation(mn[:, p, :], mn[:, p, :], ACT.Exp, scale=-1.0).then_inc(ex_ok, 1)
                need(s, qlT_kv, t - 1)
                s.wait_ge(ql_ok, t + 1)
                nc.scalar.copy(vl[:, p, 0:D], v_A[:, 2 * D:3 * D]).then_inc(vl_ok, 1)

            def keep_linear(t, p):
                s.wait_ge(qlT_kv, t + 1)
                nc.scalar.copy(ql_T[:, one(t), :], v_Q[:, 0:P]).then_inc(qlT_ok, 1)
                nc.scalar.copy(kv_part[:, one(t), :], v_Q[:, P:P + D + 1]).then_inc(qlT_ok, 1)

            def softmax_exp(t, p):
                s.wait_ge(sub_ok, t + 1)
                nc.scalar.activation(att[:, p, :], att[:, p, :], ACT.Exp).then_inc(exp_ok, 1)

            def late_weights(t, p):
                if isinstance(t, int) and t == 0:
                    s.wait_ge(late_in, 16 * len(late))
                    nc.scalar.activation(w_g[:], w_g[:], ACT.Copy, scale=gam2[:]).then_inc(gains_ok, 1)
                    nc.scalar.activation(w_e[:], w_e[:], ACT.Copy, scale=gam2[:]).then_inc(gains_ok, 1)

            def copy_oT(t, p):
                s.wait_ge(on_T, t + 1)
                need(s, wo_ok, t - 1)
                nc.scalar.copy(o_T[:, p, :], v_T[:, P:2 * P]).then_inc(oT_ok, 1)

            def square_x2(t, p):
                s.wait_ge(x2_ok, t + 1)
                need(s, sq_ok, t - 1)
                nc.scalar.activation(sq[:, p, :], em[:, p, E, :], ACT.Square, accum_out=ss[:, one(t)]).then_inc(sq_ok, 1)
                s.wait_ge(x2_T_ps, t + 1)
                need(s, moe_ok, t - 1)
                nc.scalar.copy(x2_T[:, p, :], v_Q[:, 3 * P:4 * P]).then_inc(x2T_ok, 1)

            def gate_exp(t, p):
                s.wait_ge(gv, 4 * t + 2)
                nc.scalar.activation(ge[:, p, :], lg[:, p, :], ACT.Exp, bias=nmx[:, p, :],
                                     accum_out=gs[:, p, :]).then_inc(ge_ok, 1)

            def weigh_experts(t, p):
                s.wait_ge(gv, 4 * t + 4)
                s.wait_ge(moe_ok, t + 1)
                need(s, acc_ok, t - 1)
                for e in range(E):
                    bank = (v_M0, v_M1)[e // 4]
                    last = nc.scalar.activation(em[:, p, e, :], bank[:, e % 4 * D:(e % 4 + 1) * D], ACT.Copy,
                                                scale=gw[:, p, e:e + 1])
                last.then_inc(em_ok, 1)

            def gate_tanh(t, p):
                s.wait_ge(acc_ok, t + 1)
                need(s, gate_ok, t - 1)
                nc.scalar.activation(th[:, p, :], acc[:, p, :], ACT.Tanh, scale=0.5).then_inc(th_ok, 1)

            tile_loop(s, NT, [(1, minus_min), (0, copies_x), (8, gate_tanh), (1, exps), (3, softmax_exp),
                              (3, late_weights), (6, square_x2), (7, gate_exp), (1, keep_linear), (5, copy_oT),
                              (7, weigh_experts)])

            def copy_q(t, p):
                need(s, nd_ok, t - 1)
                nc.scalar.copy(q_s[:, p:p + 1, :], ql_T[:, one(t), :]).then_inc(qs_ok, 1)

            def copy_linT(t, p):
                s.wait_ge(lin_T_ps, t + 1)
                need(s, so_ok, t - 1)
                nc.scalar.copy(lin_T[:, p, :], linT_bank[p][:, 0:P]).then_inc(linT_ok, 1)

            s.wait_ge(qlT_ok, 2 * NT)
            tile_loop(s, NT, [(0, copy_q), (1, copy_linT)])

        @block.gpsimd
        def _(g):
            g.wait_ge(prep, 1)
            def inverse_roots(n):
                lo, hi = FIRST_OF[n], (FIRST_OF + (NT,))[n + 1]
                g.wait_ge(stat, 2 * hi + 4 * n + 1)
                nc.gpsimd.tensor_tensor(rstd[:, lo:hi], ve[:, lo:hi], half[:, lo:hi], ALU.pow).then_inc(pool_pow, 1)
                g.wait_ge(stat, 2 * hi + 4 * n + 4)
                nc.gpsimd.tensor_tensor(rms1[:, lo:hi], vr[:, lo:hi], half[:, lo:hi], ALU.pow).then_inc(pool_pow, 1)

            inverse_roots(0)

            def other_roots(t, p):
                if isinstance(t, int) and t == 0:
                    inverse_roots(1)

            def products_qk(t, p):
                g.wait_ge(qkv_ok, t + 1)
                need(g, s1_ok, t - 1)
                q = qkv[:, one(t), 0:D].rearrange("p o (h d) -> p (o h) d", d=HD)
                k = qkv[:, one(t), D:2 * D].rearrange("p o (d g) -> p (o d) g", d=HD)
                nc.gpsimd.tensor_tensor(prod[:, p, 0, :].rearrange("p (h d g) -> p h d g", g=H, d=HD),
                                        q.unsqueeze(3).broadcast_to([P, H, HD, H]),
                                        k.unsqueeze(1).broadcast_to([P, H, HD, H]), ALU.mult).then_inc(p1_ok, 1)

            def products_av(t, p):
                g.wait_ge(exp_ok, t + 1)
                need(g, or_ok, t - 1)
                w = att[:, p, :].rearrange("p (h g) -> p h g", g=H)
                val = qkv[:, one(t), 2 * D:3 * D].rearrange("p o (g d) -> p (o g) d", d=HD)
                nc.gpsimd.tensor_tensor(prod[:, p, 1, :].rearrange("p (h g d) -> p h g d", g=H, d=HD),
                                        w.unsqueeze(3).broadcast_to([P, H, H, HD]),
                                        val.unsqueeze(1).broadcast_to([P, H, H, HD]),
                                        ALU.mult).then_inc(p2_ok, 1)

            def add_bias(t, p):
                if isinstance(t, int) and t == 0:
                    g.wait_ge(w_in, 16 * len(early))
                g.wait_ge(xs_ok, t + 1)
                nc.gpsimd.tensor_tensor(xnb[:, one(t), :], xs[:, p:p + 1, :], b_o[:].unsqueeze(1), ALU.add).then_inc(xnb_ok, 1)

            def rms_x2(t, p):
                g.wait_ge(ms_ok, t + 1)
                nc.gpsimd.tensor_tensor(rms2[:, one(t)], ms[:, one(t)], half[:, 0:1], ALU.pow).then_inc(r2_ok, 1)

            tile_loop(g, NT, [(2, products_qk), (7, rms_x2), (0, add_bias), (2, other_roots), (4, products_av)])

            g.wait_ge(w1_v, 5)
            g.wait_ge(or_ok, NT)
            tern = prod[:, 0, 0, 0:2 * HID].rearrange("p (s n) -> p s n", s=2)
            n_g = 0
            for n, w in enumerate((w1.w1[:], w1.w2[:].rearrange("p c n -> p (c n)"))):
                nc.gpsimd.tensor_scalar(tern[:, 0, :], w, w1.inv[:, n:n + 1], 0.5, ALU.mult, ALU.is_gt).then_inc(w1_g, 1)
                nc.gpsimd.tensor_scalar(tern[:, 1, :], w, w1.inv[:, n:n + 1], -0.5, ALU.mult, ALU.is_lt).then_inc(w1_g, 1)
                g.wait_ge(w1_g, n_g + 2)
                nc.gpsimd.tensor_tensor(tern[:, 0, :], tern[:, 0, :], tern[:, 1, :], ALU.subtract).then_inc(w1_g, 1)
                g.wait_ge(w1_g, n_g + 3)
                nc.gpsimd.tensor_scalar(w, tern[:, 0, :], w1.mean[:, n:n + 1], None, ALU.mult).then_inc(w1_g, 1)
                g.wait_ge(w1_g, n_g + 4)
                n_g += 4
            nc.gpsimd.tensor_copy(w1.be1_rep[:], w1.be1[:].broadcast_to([P, P])).then_inc(w1_g, 1)
            nc.gpsimd.tensor_copy(w1.be2_rep[:], w1.be2[:].unsqueeze(2).broadcast_to([P, HC, P])).then_inc(w1_g, 1)
            nc.gpsimd.tensor_scalar(w1.w1g[:], w1.w1[:], w1.g1[:], None, ALU.mult).then_inc(w1_g, 1)
            nc.gpsimd.tensor_tensor(w1.w2g[:], w1.w2[:], w1.g2[:].unsqueeze(2).broadcast_to([P, HC, D]), ALU.mult).then_inc(w1_g, 1)




class Layer1Weights:

    def __init__(self, nc, a, c):
        def sb(name, shape):
            return c.enter_context(nc.sbuf_tensor("l1_" + name, shape, F32))

        self.w_qkv = sb("w_qkv", [P, 3, D])
        self.lora_b = sb("lora_b", [R, 3, D])
        self.lora_aT = sb("lora_aT", [R, 3, D])
        self.w1 = sb("w1", [P, HID])
        self.w2 = sb("w2", [P, HC, D])
        self.g1 = sb("g1", [P, 1])
        self.be1 = sb("be1", [P, 1])
        self.g2 = sb("g2", [P, HC])
        self.be2 = sb("be2", [P, HC])
        self.b1 = sb("b1", [P, HID])
        self.b2 = sb("b2", [P, D])
        self.w1g = sb("w1g", [P, HID])
        self.w2g = sb("w2g", [P, HC, D])
        self.be1_rep = sb("be1_rep", [P, P])
        self.be2_rep = sb("be2_rep", [P, HC, P])
        self.asum = sb("asum", [P, 2])
        self.mean = sb("mean", [P, 2])
        self.inv = sb("inv", [P, 2])
        self.ones = sb("ones", [P, P])
        self.st6 = sb("st6", [P, NT, 6])
        self.loads = []
        for n, k in enumerate("qkv"):
            self.loads += [(self.w_qkv[:, n, :], a[f"W{k}T"]), (self.lora_b[:, n, :], a[f"L1_attn_B{k}"]),
                           (self.lora_aT[:, n, :], a[f"A{k}T"])]
        self.loads += [(self.w1[:], a["w1T"]), (self.w2[:], a["w2T"].rearrange("(c p) n -> p c n", p=P)),
                       (self.g1[:], a["ln1_g"]), (self.be1[:], a["ln1_b"]),
                       (self.g2[:], a["ln2_g"].rearrange("(c p) o -> p (c o)", p=P)),
                       (self.be2[:], a["ln2_b"].rearrange("(c p) o -> p (c o)", p=P)),
                       (self.b1[:], a["L1_ffn_b1"].partition_broadcast(P)),
                       (self.b2[:], a["L1_ffn_b2"].partition_broadcast(P))]


class ScoreOperands:
    NB = 3
    LOADS = 2 * PARTS * PARTS + 1

    def __init__(self, nc, a, c, split_dram):
        def sb(name, shape):
            return c.enter_context(nc.sbuf_tensor("at_" + name, shape, BF16))

        self.a, self.split_dram = a, split_dram
        self.qa = sb("qa", [P, self.NB, QUAD, N])
        self.ka = sb("ka", [P, self.NB, QUAD, N])
        self.ident_bf = sb("ident_bf", [P, P])
        self.below = sb("below", [P, P])
        self.later = sb("later", [P, P])
        self.pick = c.enter_context(nc.sbuf_tensor("at_pick", [P, QUAD * (HD + 1)], F32))
        self.rows_in = [c.enter_context(nc.semaphore(f"at_rows_in{i}")) for i in range(self.NB)]

    def constants(self):
        loads = [(dst[:], self.a[name].bitcast(BF16)) for dst, name in (
            (self.ident_bf, "ident_bf"), (self.below, "below"), (self.later, "later"))]
        loads.append((self.pick[:], self.a["pick"]))
        for p in range(self.NB):
            loads.append((self.qa[ROW_ALIBI:ROW_MAX, p, :, :], self.a["ones_zeros"].bitcast(BF16)))
            loads.append((self.ka[ROW_ALIBI + PARTS:ROWS, p, :, :], self.a["zeros_ones"].bitcast(BF16)))
        return loads

    def load(self, q, g, p):
        b, hg = g // QUAD, g % QUAD
        for i in range(PARTS):
            for k in range(PARTS):
                rows = slice((i * PARTS + k) * HD, (i * PARTS + k + 1) * HD)
                for w, dst, part in ((0, self.qa, i), (1, self.ka, k)):
                    src = self.split_dram[one(b), part, w, bass.ds(hg * QUAD * HD, QUAD * HD), :]
                    q.dma_start(dst[rows, p, :, :],
                                src.rearrange("o (j d) t -> (o d) j t", d=HD)).then_inc(self.rows_in[p], 16)
        src = self.a["alibi"].bitcast(BF16)[:, bass.ds(hg * QUAD, QUAD), :]
        q.dma_start(self.ka[ROW_ALIBI:ROW_ALIBI + PARTS, p, :, :], src).then_inc(self.rows_in[p], 16)


def layer1_dense(nc, a, w, ops, x_sb, ident, v_sb, y_sb, split_dram):
    with ExitStack() as c:
        def sb(name, shape, dt=F32):
            return c.enter_context(nc.sbuf_tensor("l1_" + name, shape, dt))

        def sem(name):
            return c.enter_context(nc.semaphore("l1_" + name))

        banks = [c.enter_context(nc.psum_tensor(f"l1_bank{i}", [P, BANK], F32)) for i in range(8)]
        k_T, k_Y = banks[0:2]
        k_QKV, k_H, k_T4 = banks[2:4], banks[4:6], banks[6:8]

        w_qkv, w1g, w2g, b1, b2, st6 = w.w_qkv, w.w1g, w.w2g, w.b1, w.b2, w.st6
        half = sb("half", [P, NT])
        mv = sb("mv", [P, NT, 2])
        ve = sb("ve", [P, NT])
        rstd = sb("rstd", [P, NT])
        vr = sb("vr", [P, NT])
        rln1 = sb("rln1", [P, NT])
        h = sb("h", [P, NT, HID])
        hst6 = sb("hst6", [P, 2, 6])
        hmv = sb("hmv", [P, 2, 2])
        hve = sb("hve", [P, 2])
        hrstd = sb("hrstd", [P, 2])
        parts = sb("parts", [P, PARTS, 2, NT, P], BF16)
        xs = sb("xs", [P, 2, D])
        xT = sb("xT", [P, 2, P])
        rest = sb("rest", [P, 2, 2 * P])
        hn = sb("hn", [P, 2, HID])
        hT = sb("hT", [P, 2, HID])

        FIRST_OF = (0, 4)
        half_ok, stat, pool_pow = (sem(n) for n in ("half_ok", "stat", "pool_pow"))
        xs_ok, xs_T, xT_ok, qkv_ps, ph_ok, r_h = (sem(n) for n in ("xs_ok", "xs_T", "xT_ok", "qkv_ps", "ph_ok", "r_h"))
        part1, rest1, part2, part3, v_ok = (sem(n) for n in ("part1", "rest1", "part2", "part3", "v_ok"))
        h_ok, gelu_ok, hst, hn_ok, hn_T, hT_ok, y_ps, y_ok = (sem(n) for n in (
            "h_ok", "gelu_ok", "hst", "hn_ok", "hn_T", "hT_ok", "y_ps", "y_ok"))
        stored = sem("stored")

        block = c.enter_context(nc.Block())

        @block.sync
        def _(sp):
            for b in range(B):
                for part in range(PARTS):
                    sp.wait_ge((part1, part2, part3)[part], (b + 1) * TB)
                    for w in range(2):
                        sp.dma_start(split_dram[b, part, w, :, :],
                                     parts[:, part, w, b * TB:(b + 1) * TB, :].rearrange("p k t -> p (k t)")).then_inc(stored, 16)
                if b == 0:
                    sp.wait_ge(stored, 16 * PARTS * 2)
                    for g in range(2):
                        ops.load(sp, g, g)
            sp.wait_ge(stored, 16 * B * PARTS * 2)

        @block.vector
        def _(v):
            nc.vector.memset(half[:], -0.5).then_inc(half_ok, 1)
            for t in range(NT):
                nc.vector.bn_aggr(mv[:, t, :], st6[:, t, :]).then_inc(stat, 1)
            v.wait_ge(stat, NT)
            nc.vector.tensor_scalar(ve[:], mv[:, :, 1], LN_EPS, None, ALU.add).then_inc(stat, 1)
            v.wait_ge(stat, NT + 1)
            nc.vector.reciprocal(vr[:], ve[:]).then_inc(stat, 1)
            v.wait_ge(stat, NT + 2)
            nc.vector.tensor_tensor(vr[:], vr[:], mv[:, :, 1], ALU.mult).then_inc(stat, 1)
            v.wait_ge(stat, NT + 3)
            nc.vector.tensor_scalar(vr[:], vr[:], LN_EPS, None, ALU.add).then_inc(stat, 1)

            def normalise(t, p):
                if isinstance(t, int) and t in FIRST_OF:
                    v.wait_ge(pool_pow, 2 * FIRST_OF.index(t) + 1)
                need(v, xs_T, t - 1)
                nc.vector.tensor_scalar(xs[:, p:p + 1, :], x_sb[:, one(t), :], mv[:, one(t), 0], rstd[:, one(t)],
                                        ALU.subtract, ALU.mult).then_inc(xs_ok, 1)

            def hidden(t, p):
                if isinstance(t, int) and t in FIRST_OF:
                    v.wait_ge(pool_pow, 2 * FIRST_OF.index(t) + 2)
                v.wait_ge(ph_ok, t + 1)
                nc.vector.scalar_tensor_tensor(h[:, one(t), :], k_H[p][:, :], rln1[:, one(t)], b1[:],
                                               ALU.mult, ALU.add).then_inc(h_ok, 1)

            def first_rest(t, p):
                v.wait_ge(part1, t + 1)
                need(v, part3, t - 1)
                nc.vector.tensor_tensor(rest[:, p, :], k_QKV[p][:, 0:2 * P],
                                        parts[:, 0, :, one(t), :].rearrange("p w o t -> p w (o t)"), ALU.subtract).then_inc(rest1, 1)

            def hidden_stats(t, p):
                v.wait_ge(gelu_ok, t + 1)
                nc.vector.bn_stats(hst6[:, p, :], h[:, one(t), :]).then_inc(hst, 1)

            def stats_in(t, p):
                v.wait_ge(hst, 3 * t + 1)

            def hidden_moments(t, p):
                nc.vector.bn_aggr(hmv[:, p, :], hst6[:, p, :]).then_inc(hst, 1)

            def hidden_variance(t, p):
                v.wait_ge(hst, 3 * t + 2)
                nc.vector.tensor_scalar(hve[:, p:p + 1], hmv[:, p, 1:2], LN_EPS, None, ALU.add).then_inc(hst, 1)

            def normalise_hidden(t, p):
                v.wait_ge(r_h, t + 1)
                need(v, hn_T, t - 1)
                nc.vector.tensor_scalar(hn[:, p:p + 1, :], h[:, one(t), :], hmv[:, p, 0:1], hrstd[:, p:p + 1],
                                        ALU.subtract, ALU.mult).then_inc(hn_ok, 1)

            def keep_y(t, p):
                v.wait_ge(y_ps, t + 1)
                nc.vector.tensor_tensor(y_sb[:, one(t), :], k_Y[:, 0:D].unsqueeze(1), b2[:].unsqueeze(1), ALU.add).then_inc(y_ok, 1)

            tile_loop(v, NT, [(4, normalise_hidden), (0, normalise), (3, hidden_stats), (3, stats_in), (6, keep_y),
                              (3, hidden_moments), (3, hidden_variance), (1, hidden), (1, first_rest)])

        @block.tensor
        def _(pe):
            def transpose_x(t, p):
                pe.wait_ge(xs_ok, t + 1)
                need(pe, xT_ok, t)
                nc.tensor.transpose(k_T[:, 0:P], xs[:, p, :], ident[:]).then_inc(xs_T, 1)

            def project(t, p):
                pe.wait_ge(xT_ok, t + 1)
                need(pe, rest1, t - 1)
                need(pe, v_ok, t - 1)
                nc.tensor.matmul(k_QKV[p][:, 2 * P:2 * P + D], xT[:, p, :], w_qkv[:, 2, :], start=True, stop=True)
                for n in range(2):
                    last = nc.tensor.matmul(k_QKV[p][:, n * P:(n + 1) * P], w_qkv[:, n, :], xT[:, p, :], start=True, stop=True)
                last.then_inc(qkv_ps, 1)
                need(pe, h_ok, t - 1)
                nc.tensor.matmul(k_H[p][:, :], xT[:, p, :], w1g[:], start=True, stop=True).then_inc(ph_ok, 1)

            def transpose_hidden(t, p):
                pe.wait_ge(hn_ok, t + 1)
                need(pe, hT_ok, t - 1)
                for n in range(HC):
                    last = nc.tensor.transpose(k_T4[p][:, n * P:(n + 1) * P], hn[:, p, n * P:(n + 1) * P], ident[:])
                last.then_inc(hn_T, 1)

            def second(t, p):
                pe.wait_ge(hT_ok, t + 1)
                need(pe, y_ok, t)
                for n in range(HC):
                    last = nc.tensor.matmul(k_Y[:, 0:D], hT[:, p, n * P:(n + 1) * P], w2g[:, n, :],
                                            start=(n == 0), stop=(n == HC - 1))
                last.then_inc(y_ps, 1)

            tile_loop(pe, NT, [(1, project), (0, transpose_x), (4, transpose_hidden), (5, second)])

        @block.scalar
        def _(s):
            def copy_xT(t, p):
                s.wait_ge(xs_T, t + 1)
                need(s, ph_ok, t - 1)
                nc.scalar.copy(xT[:, p, :], k_T[:, 0:P]).then_inc(xT_ok, 1)

            def first_part(t, p):
                s.wait_ge(qkv_ps, t + 1)
                nc.scalar.copy(v_sb[:, one(t), :], k_QKV[p][:, 2 * P:2 * P + D]).then_inc(v_ok, 1)
                nc.scalar.copy(parts[:, 0, :, one(t), :].rearrange("p w o t -> p w (o t)"),
                               k_QKV[p][:, 0:2 * P].rearrange("p (w t) -> p w t", w=2)).then_inc(part1, 1)

            def second_part(t, p):
                s.wait_ge(rest1, t + 1)
                nc.scalar.copy(parts[:, 1, :, one(t), :].rearrange("p w o t -> p w (o t)"),
                               rest[:, p, :].rearrange("p (w t) -> p w t", w=2)).then_inc(part2, 1)

            def gelu(t, p):
                s.wait_ge(h_ok, t + 1)
                nc.scalar.activation(h[:, one(t), :], h[:, one(t), :], ACT.Gelu).then_inc(gelu_ok, 1)

            def copy_hT(t, p):
                s.wait_ge(hn_T, t + 1)
                need(s, y_ps, t - 1)
                nc.scalar.copy(hT[:, p, :], k_T4[p][:, :]).then_inc(hT_ok, 1)

            tile_loop(s, NT, [(2, gelu), (0, copy_xT), (2, second_part), (1, first_part), (4, copy_hT)])

        @block.gpsimd
        def _(g):
            g.wait_ge(half_ok, 1)
            g.wait_ge(stat, NT + 1)
            for lo, hi in zip(FIRST_OF, FIRST_OF[1:] + (NT,)):
                nc.gpsimd.tensor_tensor(rstd[:, lo:hi], ve[:, lo:hi], half[:, lo:hi], ALU.pow).then_inc(pool_pow, 1)
                if lo == 0:
                    g.wait_ge(stat, NT + 4)
                nc.gpsimd.tensor_tensor(rln1[:, lo:hi], vr[:, lo:hi], half[:, lo:hi], ALU.pow).then_inc(pool_pow, 1)

            def last_part(t, p):
                g.wait_ge(part2, t + 1)
                nc.gpsimd.tensor_tensor(parts[:, 2, :, one(t), :].rearrange("p w o t -> p w (o t)"),
                                        rest[:, p, :].rearrange("p (w t) -> p w t", w=2),
                                        parts[:, 1, :, one(t), :].rearrange("p w o t -> p w (o t)"), ALU.subtract).then_inc(part3, 1)

            def hidden_rstd(t, p):
                g.wait_ge(hst, 3 * t + 3)
                nc.gpsimd.tensor_tensor(hrstd[:, p:p + 1], hve[:, p:p + 1], half[:, 0:1], ALU.pow).then_inc(r_h, 1)

            tile_loop(g, NT, [(3, hidden_rstd), (2, last_part)])


def layer1_attention(nc, ops, ident, v_sb, y_sb, o_sb):
    with ExitStack() as c:
        def sb(name, shape, dt=F32):
            return c.enter_context(nc.sbuf_tensor("at_" + name, shape, dt))

        def sem(name):
            return c.enter_context(nc.semaphore("at_" + name))

        s_bank = [c.enter_context(nc.psum_tensor(f"at_s{i}", [P, BANK], F32)) for i in range(3)]
        e_bank = [c.enter_context(nc.psum_tensor(f"at_e{i}", [P, BANK], F32)) for i in range(3)]
        o_bank = [c.enter_context(nc.psum_tensor(f"at_o{i}", [P, BANK], F32)) for i in range(2)]

        NB = ops.NB
        qa, ka, ident_bf, below, later, rows_in = ops.qa, ops.ka, ops.ident_bf, ops.below, ops.later, ops.rows_in
        m = sb("m", [P, NB, QUAD, TB])
        m2 = sb("m2", [P, QUAD, PAIRS, 2])
        mpart = sb("mpart", [QUAD * TB, NB, PARTS, P], BF16)
        mrest = sb("mrest", [QUAD * TB, NB, P])
        vg = sb("vg", [P, NB, TB, QUAD, 32])
        pr = sb("pr", [P, 2, QUAD, N + P])
        oT = sb("oT", [P, 2, BANK])
        rd = sb("rd", [P, TB, QUAD])
        th = sb("th", [P, NT, D])

        vg0, th_ok = sem("vg0"), sem("th_ok")
        s_ps, s_max = sem("s_ps"), sem("s_max")
        m_ok, mp_ok = sem("m_ok"), sem("mp_ok")
        m_in = [sem(f"m_in{i}") for i in range(NB)]
        e_ps, e_ok, pv_ps = sem("e_ps"), sem("e_ok"), sem("pv_ps")
        o_evac, oT_ps, rd_ok, o_norm, vg_ok = sem("o_evac"), sem("oT_ps"), sem("rd_ok"), sem("o_norm"), sem("vg_ok")

        UNITS = []
        EXPS = []
        for d in range(PAIRS):
            long = (TB - d) * P
            for j in range(QUAD):
                UNITS += [(TB - 1 - d, j, 0, BANK), (TB - 1 - d, j, BANK, long - BANK), (d, j, 0, (d + 1) * P)]
                EXPS += [(d, j, 0, BANK, 0), (d, j, BANK, long - BANK, BANK), (TB - 1 - d, j, 0, (d + 1) * P, long)]
        STEP = 3 * QUAD
        M_UNIT = len(UNITS)
        MU = M_UNIT + 1
        EU = len(EXPS)
        T_SLOT = 3 * STEP
        OUT = HD + 1

        def slot(u):
            return u + (u >= T_SLOT)

        block = c.enter_context(nc.Block())

        @block.sync
        def _(sp):
            def maxima_rows(g, p):
                sp.wait_ge(mp_ok, 4 * (g + 1))
                for part in range(PARTS):
                    sp.dma_start(qa[ROW_MAX + part:ROW_MAX + part + 1, p, :, :].rearrange("o j t -> o (j t)"),
                                 mpart[:, p, part, :]).then_inc(m_in[p], 16)

            with sp.Fori(0, (NG - 2) // NB) as i:
                for u in range(NB):
                    maxima_rows(NB * i + u, u)
                    g = NB * i + (u + 2)
                    sp.wait_ge(e_ok, EU * (g - 2) + 1)
                    ops.load(sp, g, (u + 2) % NB)
            for g in range(NG - 2, NG):
                maxima_rows(g, g % NB)
            for p in range(NB):
                sp.wait_ge(m_in[p], 16 * PARTS * len(range(p, NG, NB)))

        def turns(eng, body):
            for n in range(2):
                body(n, n % NB)
            with eng.Fori(0, (NG - 2) // NB) as i:
                for u in range(NB):
                    body(NB * i + (2 + u), (2 + u) % NB)
            for n in range(NG, NG + 2):
                body(n, n % NB)

        def has(n, lag):
            return not isinstance(n, int) or 0 <= n - lag < NG

        @block.tensor
        def _(pe):
            def bank_free(n, u):
                last = slot(u) - 3
                if u < 2:
                    need(pe, s_max, MU * n - 1 + u)
                elif last < 0:
                    need(pe, s_max, MU * n - 2)
                elif last == T_SLOT:
                    if has(n, 2):
                        pe.wait_ge(o_norm, n - 1)
                else:
                    pe.wait_ge(s_max, MU * n + last - (last > T_SLOT) + 1)

            def score_unit(n, p, u):
                qb, j, lo, w = UNITS[u]
                bank_free(n, u)
                bank = s_bank[slot(u) % 3]
                diagonal = lo + w == (qb + 1) * P
                last = nc.tensor.matmul(bank[:, 0:w], qa[0:ROW_MAX, p, j, qb * P:(qb + 1) * P],
                                        ka[0:ROW_MAX, p, j, lo:lo + w], start=True, stop=not diagonal)
                if diagonal:
                    last = nc.tensor.matmul(bank[:, w - P:w], ident_bf[:], later[:], start=False, stop=True)
                last.then_inc(s_ps, 1)

            def exp_unit(g, p, u):
                kb, j, lo, w, _ = EXPS[u]
                need(pe, e_ok, EU * g + u - 2)
                bank = e_bank[u % 3]
                last = nc.tensor.matmul(bank[:, 0:w], ka[0:ROWS, p, j, kb * P:(kb + 1) * P],
                                        qa[0:ROWS, p, j, kb * P + lo:kb * P + lo + w], start=True, stop=lo > 0)
                if lo == 0:
                    last = nc.tensor.matmul(bank[:, 0:P], ident_bf[:], below[:], start=False, stop=True)
                last.then_inc(e_ps, 1)

            def values(g, p, d, kb, half):
                lo = max(kb * P, half * BANK)
                off = lo - kb * P if kb == d else lo - kb * P + (TB - d) * P
                if kb == 0:
                    need(pe, o_evac, 2 * g - 1 + half)
                for j in range(QUAD):
                    last = nc.tensor.matmul(
                        o_bank[half][32 * j:32 * (j + 1), lo - half * BANK:BANK],
                        vg[:, p, kb, j, :], pr[:, d % 2, j, off:off + (half + 1) * BANK - lo],
                        start=(kb == 0), stop=(kb == QUAD - 1 + half))
                if kb != d:
                    last.then_inc(pv_ps, 1)

            def transpose_out(n):
                if has(n, 0):
                    pe.wait_ge(s_max, MU * n + T_SLOT - 2)
                else:
                    pe.wait_ge(o_norm, n - 2)
                for half in range(2):
                    pe.wait_ge(o_evac, 2 * (n - 2) + half + 1)
                    for k in range(QUAD):
                        at = (half * QUAD + k) * QUAD * OUT
                        last = nc.tensor.matmul(s_bank[T_SLOT % 3][:, at:at + QUAD * OUT],
                                                oT[:, half, k * P:(k + 1) * P], ops.pick[:], start=True, stop=True)
                last.then_inc(oT_ps, 1)

            def body(n, p):
                for d in range(PAIRS):
                    e_lag, e_d = (2, PAIRS - 1) if d == 0 else (1, d - 1)
                    v_lag, v_d = (2, d + 2) if d < 2 else (1, d - 2)
                    if d == 0 and has(n, 0):
                        pe.wait_ge(rows_in[p], 16 * ops.LOADS * (n // NB + 1))
                    if d == 1 and has(n, 1):
                        pe.wait_ge(m_in[(p - 1) % NB], 16 * PARTS * ((n - 1) // NB + 1))
                        pe.wait_ge(vg_ok, n)
                    if d == 3 and has(n, 2):
                        transpose_out(n)
                    for j in range(QUAD):
                        for piece in range(3):
                            if has(n, 0):
                                score_unit(n, p, STEP * d + 3 * j + piece)
                            if has(n, e_lag):
                                exp_unit(n - e_lag, (p - e_lag) % NB, STEP * e_d + 3 * j + piece)
                        if has(n, v_lag) and j > 0:
                            if j == 1:
                                pe.wait_ge(e_ok, EU * (n - v_lag) + STEP * (v_d + 1))
                            kb, half = ((v_d, 0), (v_d, 1), (TB - 1 - v_d, 1))[j - 1]
                            values(n - v_lag, (p - v_lag) % NB, v_d, kb, half)
                if has(n, 0):
                    pe.wait_ge(m_ok, n + 1)
                    bank_free(n, M_UNIT)
                    nc.tensor.transpose(s_bank[slot(M_UNIT) % 3][0:QUAD * TB, 0:P],
                                        m[:, p, :, :].rearrange("p j k -> p (j k)"), ident[:]).then_inc(s_ps, 1)

            turns(pe, body)

        @block.vector
        def _(v):
            def maxima(n, p, d):
                for u in range(STEP * d, STEP * (d + 1)):
                    qb, j, lo, w = UNITS[u]
                    v.wait_ge(s_ps, MU * n + u + 1)
                    dst = m[:, p, j, qb:qb + 1] if qb < QUAD else m2[:, j, qb - QUAD, lo // BANK:lo // BANK + 1]
                    nc.vector.tensor_reduce(dst, s_bank[slot(u) % 3][:, 0:w], AX.X, ALU.max).then_inc(s_max, 1)

            def minus_maxima(n, p):
                v.wait_ge(s_ps, MU * n + MU)
                mt = s_bank[slot(M_UNIT) % 3][0:QUAD * TB, 0:P]
                nc.vector.tensor_scalar(mpart[:, p, 0, :], mt, -1.0, None, ALU.mult).then_inc(mp_ok, 1)
                v.wait_ge(mp_ok, 4 * n + 1)
                nc.vector.scalar_tensor_tensor(mrest[:, p, :], mt, -1.0, mpart[:, p, 0, :],
                                               ALU.mult, ALU.subtract).then_inc(s_max, 1)
                v.wait_ge(s_max, MU * (n + 1))
                nc.vector.tensor_copy(mpart[:, p, 1, :], mrest[:, p, :]).then_inc(mp_ok, 1)
                v.wait_ge(mp_ok, 4 * n + 2)
                nc.vector.tensor_tensor(mpart[:, p, 2, :], mrest[:, p, :], mpart[:, p, 1, :],
                                        ALU.subtract).then_inc(mp_ok, 2)

            def outputs(g):
                b, hg = g // QUAD, g % QUAD
                v.wait_ge(oT_ps, g + 1)
                need(v, o_norm, g)
                ot = s_bank[T_SLOT % 3][:, 0:TB * QUAD * OUT].rearrange("p (n j r) -> p n j r", n=TB, j=QUAD)
                nc.vector.reciprocal(rd[:], ot[:, :, :, HD]).then_inc(rd_ok, 1)
                v.wait_ge(rd_ok, g + 1)
                dst = o_sb[:, bass.ds(b * TB, TB), bass.ds(hg * QUAD * HD, QUAD * HD)]
                nc.vector.tensor_tensor(dst.rearrange("p n (j d) -> p n j d", d=HD), ot[:, :, :, 0:HD],
                                        rd[:].unsqueeze(3).broadcast_to([P, TB, QUAD, HD]), ALU.mult).then_inc(o_norm, 1)

            def body(n, p):
                for d in range(PAIRS):
                    if d == 3 and has(n, 2):
                        outputs(n - 2)
                    if has(n, 0):
                        maxima(n, p, d)
                if has(n, 0):
                    v.wait_ge(s_max, MU * n + M_UNIT)
                    nc.vector.tensor_reduce(m[:, p, :, QUAD:TB], m2[:], AX.X, ALU.max).then_inc(m_ok, 1)
                    minus_maxima(n, p)

            turns(v, body)

        @block.scalar
        def _(s):
            def exps(g, d):
                need(s, pv_ps, PAIRS * g + d - 1)
                for u in range(STEP * d, STEP * (d + 1)):
                    _, j, lo, w, at = EXPS[u]
                    s.wait_ge(e_ps, EU * g + u + 1)
                    nc.scalar.activation(pr[:, d % 2, j, at:at + w], e_bank[u % 3][:, 0:w], ACT.Exp).then_inc(e_ok, 1)

            def evacuate(g):
                s.wait_ge(pv_ps, PAIRS * (g + 1))
                need(s, oT_ps, g)
                for half in range(2):
                    nc.scalar.copy(oT[:, half, :], o_bank[half][:, :]).then_inc(o_evac, 1)

            def body(n, p):
                for d in range(PAIRS):
                    lag, e_d = (2, PAIRS - 1) if d == 0 else (1, d - 1)
                    if has(n, lag):
                        exps(n - lag, e_d)
                    if d == 1 and has(n, 2):
                        evacuate(n - 2)

            nc.scalar.activation(th[:], y_sb[:], ACT.Tanh, scale=0.5).then_inc(th_ok, 1)
            turns(s, body)

        @block.gpsimd
        def _(g_):
            nc.gpsimd.memset(vg[:], 0.0).then_inc(vg0, 1)
            g_.wait_ge(vg0, 1)
            nc.gpsimd.memset(vg[:, :, :, :, HD:HD + 1], 1.0).then_inc(vg0, 1)
            g_.wait_ge(vg0, 2)

            def gate_y():
                g_.wait_ge(th_ok, 1)
                nc.gpsimd.tensor_tensor(th[:], th[:], y_sb[:], ALU.mult).then_inc(th_ok, 1)
                g_.wait_ge(th_ok, 2)
                nc.gpsimd.tensor_tensor(y_sb[:], th[:], y_sb[:], ALU.add).then_inc(th_ok, 1)

            def body(n, p):
                if isinstance(n, int) and n == 1:
                    gate_y()
                if has(n, 0):
                    b, hg = n // QUAD, n % QUAD
                    need(g_, pv_ps, PAIRS * (n - 2) + 1)
                    src = v_sb[:, bass.ds(b * TB, TB), bass.ds(hg * QUAD * HD, QUAD * HD)]
                    nc.gpsimd.tensor_copy(vg[:, p, :, :, 0:HD], src.rearrange("p k (j d) -> p k j d", d=HD)).then_inc(vg_ok, 1)

            turns(g_, body)


def layer1_out(nc, a, x_sb, ident, y_sb, o_sb, out):
    with ExitStack() as c:
        def sb(name, shape, dt=F32):
            return c.enter_context(nc.sbuf_tensor("out_" + name, shape, dt))

        def sem(name):
            return c.enter_context(nc.semaphore("out_" + name))

        banks = [c.enter_context(nc.psum_tensor(f"out_bank{i}", [P, BANK], F32)) for i in range(4)]
        b_T, b_S = banks[0:2], banks[2:4]
        w_p = sb("w_p", [P, D])
        o_s = sb("o_s", [P, 2, D])
        o_T = sb("o_T", [P, 2, P])
        sg = sb("sg", [P, 2, D])
        w_in, os_ok, o_Tp, oT_ok, s_ps, sg_ok, x_ok, stored = (sem(n) for n in (
            "w_in", "os_ok", "o_Tp", "oT_ok", "s_ps", "sg_ok", "x_ok", "stored"))
        out_t = out.rearrange("b (k p) d -> p (b k) d", p=P)
        block = c.enter_context(nc.Block())

        @block.sync
        def _(sp):
            sp.dma_start(w_p[:], a["WpT"]).then_inc(w_in, 16)
            with sp.Fori(0, NT // 4) as i:
                sp.wait_ge(x_ok, 4 * i + 4)
                sp.dma_start(out_t[:, bass.ds(4 * i, 4), :], x_sb[:, bass.ds(4 * i, 4), :]).then_inc(stored, 16)
            sp.wait_ge(stored, 16 * (NT // 4))

        @block.scalar
        def _(s):
            def copy_o(t, p):
                need(s, o_Tp, t - 1)
                nc.scalar.copy(o_s[:, p:p + 1, :], o_sb[:, one(t), :]).then_inc(os_ok, 1)

            def copy_T(t, p):
                s.wait_ge(o_Tp, t + 1)
                need(s, s_ps, t - 1)
                nc.scalar.copy(o_T[:, p, :], b_T[p][:, 0:P]).then_inc(oT_ok, 1)

            tile_loop(s, NT, [(0, copy_o), (1, copy_T)])

        @block.tensor
        def _(pe):
            pe.wait_ge(w_in, 16)

            def transpose_o(t, p):
                pe.wait_ge(os_ok, t + 1)
                need(pe, oT_ok, t - 1)
                nc.tensor.transpose(b_T[p][:, 0:P], o_s[:, p, :], ident[:]).then_inc(o_Tp, 1)

            def project(t, p):
                pe.wait_ge(oT_ok, t + 1)
                need(pe, sg_ok, t - 1)
                nc.tensor.matmul(b_S[p][:, 0:D], o_T[:, p, :], w_p[:], start=True, stop=True).then_inc(s_ps, 1)

            tile_loop(pe, NT, [(2, project), (0, transpose_o)])

        @block.vector
        def _(v):
            def gated(t, p):
                v.wait_ge(s_ps, t + 1)
                need(v, x_ok, t - 1)
                nc.vector.scalar_tensor_tensor(sg[:, p:p + 1, :], b_S[p][:, 0:D].unsqueeze(1), 0.5, y_sb[:, one(t), :],
                                               ALU.mult, ALU.mult).then_inc(sg_ok, 1)

            def add_to_x(t, p):
                v.wait_ge(sg_ok, t + 1)
                nc.vector.tensor_tensor(x_sb[:, one(t), :], x_sb[:, one(t), :], sg[:, p:p + 1, :], ALU.add).then_inc(x_ok, 1)

            tile_loop(v, NT, [(2, gated), (3, add_to_x)])




def constants():
    import numpy as np

    def bf16(v):
        u = np.ascontiguousarray(v, np.float32).view(np.uint32)
        return ((u + 0x7FFF + ((u >> 16) & 1)) >> 16).astype(np.uint16)

    def value(bits):
        return (bits.astype(np.uint32) << 16).view(np.float32).astype(np.float64)

    head = np.arange(P) // HD
    i, j = np.arange(P)[:, None], np.arange(P)[None, :]
    start = 2.0 ** (-(2.0 ** -1))
    slopes = np.asarray([start * start ** h for h in range(H)], np.float32).astype(np.float64)
    bias = -slopes[:, None] * np.arange(N, dtype=np.float64)[None, :]
    alibi = []
    for _ in range(PARTS):
        alibi.append(bf16(bias))
        bias = bias - value(alibi[-1])
    return {
        "ident": np.eye(P, dtype=np.float32),
        "head_mask": (head[:, None] == np.arange(H)[None, :]).astype(np.float32),
        "pick": np.eye(P, dtype=np.float32).reshape(P, QUAD, 32)[:, :, 0:HD + 1].reshape(P, QUAD * (HD + 1)).copy(),
        "ident_bf": bf16(np.eye(P)),
        "below": bf16(np.where(j < i, -1e30, 0.0)),
        "later": bf16(np.where(j > i, -1e30, 0.0)),
        "alibi": np.stack(alibi),
        "ones_zeros": bf16(np.concatenate([np.ones((PARTS, QUAD, N)), np.zeros((ROW_MAX - ROW_ALIBI - PARTS, QUAD, N))])),
        "zeros_ones": bf16(np.concatenate([np.zeros((ROW_MAX - ROW_ALIBI - PARTS, QUAD, N)), np.ones((PARTS, QUAD, N))])),
    }


def layouts(x):
    import numpy as np

    col = lambda v: np.asarray(v).reshape(-1, 1)
    t = lambda v: np.ascontiguousarray(np.asarray(v).T)
    out = {k: np.ascontiguousarray(np.asarray(x[k])) for k in (
        "L0_attn_x", "L0_attn_b_out", "L0_ffn_Wq", "L0_ffn_bq", "L0_ffn_Wo",
        "L0_ffn_bo", "L0_ffn_Wg", "L0_ffn_bg", "L0_ffn_We", "L1_attn_Bq", "L1_attn_Bk", "L1_attn_Bv",
        "L1_ffn_b1", "L1_ffn_b2")}
    column = np.arange(2 * D).reshape(H, 2, HD)
    column = np.concatenate([column[:, 0].T.reshape(-1), column[:, 1].reshape(-1)])
    out.update(Wup=np.ascontiguousarray(np.asarray(x["L0_ffn_Wup"])[:, column]),
               bup=np.ascontiguousarray(np.asarray(x["L0_ffn_bup"])[column]))
    out.update(w_qkvT=t(x["L0_attn_w_qkv"]), w_outT=t(x["L0_attn_w_out"]), WdownT=t(x["L0_ffn_Wdown"]),
               gamma1=col(x["L0_ffn_gamma1"]), gamma2=col(x["L0_ffn_gamma2"]), bdown=col(x["L0_ffn_bdown"]),
               WqT=t(x["L1_attn_Wq"]), WkT=t(x["L1_attn_Wk"]), WvT=t(x["L1_attn_Wv"]), WpT=t(x["L1_attn_Wp"]),
               AqT=t(x["L1_attn_Aq"]), AkT=t(x["L1_attn_Ak"]), AvT=t(x["L1_attn_Av"]),
               ln1_g=col(x["L1_ffn_ln1_g"]), ln1_b=col(x["L1_ffn_ln1_b"]),
               ln2_g=col(x["L1_ffn_ln2_g"]), ln2_b=col(x["L1_ffn_ln2_b"]),
               w1T=t(x["L1_ffn_w1"]), w2T=t(x["L1_ffn_w2"]))
    return out


def kernel(**inputs):
    import numpy as _np
    import concourse.bacc as _bacc
    from concourse import mybir as _mybir
    from concourse.bass_utils import run_bass_kernel_spmd as _run

    nc = _bacc.Bacc("TRN2", target_bir_lowering=False, num_devices=1)
    arrays, args = {}, {}
    for name, arr in {**layouts(inputs), **constants()}.items():
        arrays[f"in_{name}_dram"] = arr
        args[name] = nc.dram_tensor(f"in_{name}_dram", arr.shape, _mybir.dt.from_np(arr.dtype), kind="ExternalInput").ap()
    out = nc.dram_tensor("out_0_dram", (B, N, D), F32, kind="ExternalOutput").ap()
    mixer_kernel(nc, args, out)
    r = _run(nc, [arrays], core_ids=[0])
    return r.results[0]["out_0_dram"]
```
